# Optimizing a Trainium2 kernel written in Bass

```python
import numpy as np
import jax
import jax.numpy as jnp

def _softmax(x, axis=-1):
    return jax.nn.softmax(x, axis=axis)

def _gelu(x):
    return jax.nn.gelu(x, approximate=True)

def _silu(x):
    return jax.nn.silu(x)

def _sigmoid(x):
    return jax.nn.sigmoid(x)

def _layernorm(x, axis=-1, eps=1e-05):
    m = jnp.mean(x, axis=axis, keepdims=True)
    v = jnp.var(x, axis=axis, keepdims=True)
    return (x - m) / jnp.sqrt(v + eps)

def _scatter_add(tgt, idx, src, axis=0):
    return tgt.at[idx].add(src)

def _segment_sum(src, seg, n):
    return jax.ops.segment_sum(src, seg, n)
kernel_name = 'mk_xattn_ffn_d2_seqx_r4_d64205'

def setup_inputs(seed: int=0):
    np.random.seed(seed)
    _w = jnp.asarray

    def _rec_inputs():
        import jax
        import jax.numpy as jnp
        _rk = jax.random.key(seed)
        x = -0.000125 + 0.9999 * jax.random.normal(jax.random.fold_in(_rk, 1), (8, 256, 512), jnp.float32)
        _lenS = 256 - jax.random.randint(jax.random.fold_in(_rk, 7), (8,), 0, max(1, 256 // 4) + 1, jnp.int32)
        _lenS2 = 256 - jax.random.randint(jax.random.fold_in(_rk, 8), (8,), 0, max(1, 256 // 4) + 1, jnp.int32)
        _ctx_2048P = jax.random.normal(jax.random.fold_in(_rk, 11), (8, 16, 512), jnp.float32)
        _ctx_2048c = jax.random.dirichlet(jax.random.fold_in(_rk, 511), 0.3 * jnp.ones((16,), jnp.float32), (8, 256))
        _ctx_2048t = jnp.einsum('bsk,bkd->bsd', _ctx_2048c, _ctx_2048P)
        _ctx_2048t = _ctx_2048t * jax.lax.rsqrt(jnp.mean(jnp.square(_ctx_2048t)) + 1e-12) * 0.953939
        ctx_2048 = -0.000514642 + 1.00011 * (_ctx_2048t + 0.3 * jax.random.normal(jax.random.fold_in(_rk, 611), (8, 256, 512), jnp.float32))
        _validS = jnp.arange(256)[None, :] < _lenS[:, None]
        _validS2 = jnp.arange(256)[None, :] < _lenS2[:, None]
        _causal = jnp.tril(jnp.ones((256, 256), dtype=bool))
        mask_BxS2_bk0 = jnp.logical_not(jnp.broadcast_to(_validS2[:, :], (8, 256)))
        return (x, ctx_2048, mask_BxS2_bk0)
    x, ctx_2048, mask_BxS2_bk0 = _rec_inputs()

    def _L0_xattn_setup():
        import jax, jax.numpy as jnp
        import numpy as np
        key = jax.random.key(seed)
        k1, k2, k3 = jax.random.split(key, 3)
        B, S, D, M = (8, 512, 512, 128)
        hidden_states = jax.random.normal(k1, (B, S, D), dtype=jnp.float32)
        memory_tokens = jax.random.normal(k2, (B, M, D), dtype=jnp.float32)
        memory_mask = jax.random.randint(k3, (B, M), 0, 2).astype(jnp.bool_)
        return {'hidden_states': hidden_states, 'memory_tokens': memory_tokens, 'memory_mask': memory_mask}
    _L0_xattn_all = _L0_xattn_setup()
    _L0_xattn_in = {k: v for k, v in _L0_xattn_all.items() if k in ()}
    del _L0_xattn_all

    def _L0_ffn_setup():
        import jax, jax.numpy as jnp
        import numpy as np
        B, S, H, I = (1, 64, 512, 1536)

        def _quantized_matmul(x, w, scale):
            wq = w.astype(jnp.float8_e4m3fn).astype(x.dtype)
            y = jnp.einsum('bsi,io->bso', x, wq)
            return y * scale
        key = jax.random.key(seed)
        ks = jax.random.split(key, 7)
        return {'x': jax.random.normal(ks[0], (B, S, H), dtype=jnp.float32), 'gate_w': jax.random.normal(ks[1], (H, I), dtype=jnp.float32) * 0.02, 'up_w': jax.random.normal(ks[2], (H, I), dtype=jnp.float32) * 0.02, 'down_w': jax.random.normal(ks[3], (I, H), dtype=jnp.float32) * 0.02, 'gate_scale': jax.random.uniform(ks[4], (I,), dtype=jnp.float32, minval=0.5, maxval=1.5), 'up_scale': jax.random.uniform(ks[5], (I,), dtype=jnp.float32, minval=0.5, maxval=1.5), 'down_scale': jax.random.uniform(ks[6], (H,), dtype=jnp.float32, minval=0.5, maxval=1.5)}
    _L0_ffn_all = _L0_ffn_setup()
    _L0_ffn_in = {k: v for k, v in _L0_ffn_all.items() if k in ('gate_w', 'up_w', 'down_w', 'gate_scale', 'up_scale', 'down_scale')}
    del _L0_ffn_all

    def _L1_xattn_setup():
        import jax, jax.numpy as jnp
        import numpy as np
        B, S, DIM, HD = (4, 256, 512, 128)
        H = DIM // HD
        GN_EPS = 0.001

        def _decay_masks(n_heads, seq_len):
            gam = 1.0 - 2.0 ** (-5.0 - jnp.arange(n_heads, dtype=jnp.float32))
            idx = jnp.arange(seq_len, dtype=jnp.float32)
            expo = idx[None, :] - idx[:, None]
            D = jnp.where(expo[None, :, :] <= 0, gam[:, None, None] ** expo[None, :, :], 0.0)
            return D / jnp.sqrt(D.sum(axis=-1))[:, None, :]
        key = jax.random.key(seed)
        ks = jax.random.split(key, 8)
        x = jax.random.normal(ks[0], (B, S, DIM), dtype=jnp.float32)
        k = jax.random.normal(ks[1], (B, S, DIM), dtype=jnp.float32)
        v = jax.random.normal(ks[2], (B, S, DIM), dtype=jnp.float32)
        Wh = jax.random.normal(ks[3], (H, HD, HD), dtype=jnp.float32) / np.sqrt(HD)
        wg_w = jax.random.normal(ks[4], (DIM, DIM), dtype=jnp.float32) / np.sqrt(DIM)
        wo_w = jax.random.normal(ks[5], (DIM, DIM), dtype=jnp.float32) / np.sqrt(DIM)
        gn_gamma = jnp.ones((DIM,), dtype=jnp.float32)
        gn_beta = jnp.zeros((DIM,), dtype=jnp.float32)
        return {'x': x, 'k': k, 'v': v, 'Wh': Wh, 'wg_w': wg_w, 'wo_w': wo_w, 'gn_gamma': gn_gamma, 'gn_beta': gn_beta}
    _L1_xattn_all = _L1_xattn_setup()
    _L1_xattn_in = {k: v for k, v in _L1_xattn_all.items() if k in ('Wh', 'wg_w', 'wo_w', 'gn_gamma', 'gn_beta')}
    del _L1_xattn_all

    def _L1_ffn_setup():
        import jax, jax.numpy as jnp
        import numpy as np
        from jax import lax
        TOP_K = 2
        N_EXPERTS = 8
        key = jax.random.key(seed)
        ks = jax.random.split(key, 7)
        B, S, H, I, E = (4, 512, 512, 352, N_EXPERTS)
        s_h = 1.0 / np.sqrt(H)
        s_i = 1.0 / np.sqrt(I)
        return {'hidden_states': jax.random.normal(ks[0], (B, S, H), jnp.float32), 'gate_w': jax.random.normal(ks[1], (E, H), jnp.float32) * s_h, 'w1': jax.random.normal(ks[2], (E, H, 2 * I), jnp.float32) * s_h, 'w2': jax.random.normal(ks[3], (E, I, H), jnp.float32) * s_i, 'sw1': jax.random.normal(ks[4], (I, H), jnp.float32) * s_h, 'sw2': jax.random.normal(ks[5], (I, H), jnp.float32) * s_h, 'sw3': jax.random.normal(ks[6], (H, I), jnp.float32) * s_i}
    _L1_ffn_all = _L1_ffn_setup()
    _L1_ffn_in = {k: v for k, v in _L1_ffn_all.items() if k in ('gate_w', 'w1', 'w2', 'sw1', 'sw2', 'sw3')}
    del _L1_ffn_all
    return {'x': x, 'ctx_2048': ctx_2048, 'mask_BxS2_bk0': mask_BxS2_bk0, 'L0_ffn_gate_w': _L0_ffn_in['gate_w'], 'L0_ffn_up_w': _L0_ffn_in['up_w'], 'L0_ffn_down_w': _L0_ffn_in['down_w'], 'L0_ffn_gate_scale': _L0_ffn_in['gate_scale'], 'L0_ffn_up_scale': _L0_ffn_in['up_scale'], 'L0_ffn_down_scale': _L0_ffn_in['down_scale'], 'L1_xattn_Wh': _L1_xattn_in['Wh'], 'L1_xattn_wg_w': _L1_xattn_in['wg_w'], 'L1_xattn_wo_w': _L1_xattn_in['wo_w'], 'L1_xattn_gn_gamma': _L1_xattn_in['gn_gamma'], 'L1_xattn_gn_beta': _L1_xattn_in['gn_beta'], 'L1_ffn_gate_w': _L1_ffn_in['gate_w'], 'L1_ffn_w1': _L1_ffn_in['w1'], 'L1_ffn_w2': _L1_ffn_in['w2'], 'L1_ffn_sw1': _L1_ffn_in['sw1'], 'L1_ffn_sw2': _L1_ffn_in['sw2'], 'L1_ffn_sw3': _L1_ffn_in['sw3']}

def reference(x, ctx_2048, mask_BxS2_bk0, L0_ffn_gate_w, L0_ffn_up_w, L0_ffn_down_w, L0_ffn_gate_scale, L0_ffn_up_scale, L0_ffn_down_scale, L1_xattn_Wh, L1_xattn_wg_w, L1_xattn_wo_w, L1_xattn_gn_gamma, L1_xattn_gn_beta, L1_ffn_gate_w, L1_ffn_w1, L1_ffn_w2, L1_ffn_sw1, L1_ffn_sw2, L1_ffn_sw3):
    import jax
    import jax.numpy as jnp

    def _L0_xattn_ref(hidden_states, memory_tokens, memory_mask):
        import jax, jax.numpy as jnp
        import numpy as np
        B, S, D = hidden_states.shape
        scale = 1.0 / jnp.sqrt(jnp.asarray(D, hidden_states.dtype))
        scores = jnp.einsum('bsd,bmd->bsm', hidden_states, memory_tokens) * scale
        neg_inf = jnp.asarray(-1e+30, scores.dtype)
        scores = jnp.where(memory_mask[:, None, :], scores, neg_inf)
        attn = jax.nn.softmax(scores, axis=-1)
        readout = jnp.einsum('bsm,bmd->bsd', attn, memory_tokens)
        valid_b = jnp.any(memory_mask, axis=-1)
        out = jnp.where(valid_b[:, None, None], readout, jnp.zeros_like(readout))
        return out

    def _L0_ffn_ref(x, gate_w, up_w, down_w, gate_scale, up_scale, down_scale):
        import jax, jax.numpy as jnp
        import numpy as np
        B, S, H, I = (1, 64, 512, 1536)

        def _quantized_matmul(x, w, scale):
            wq = w.astype(jnp.float8_e4m3fn).astype(x.dtype)
            y = jnp.einsum('bsi,io->bso', x, wq)
            return y * scale
        gate = jax.nn.silu(_quantized_matmul(x, gate_w, gate_scale))
        up = _quantized_matmul(x, up_w, up_scale)
        fuse = gate * up
        return _quantized_matmul(fuse, down_w, down_scale)

    def _L1_xattn_ref(x, k, v, Wh, wg_w, wo_w, gn_gamma, gn_beta):
        import jax, jax.numpy as jnp
        import numpy as np
        B, S, DIM, HD = (4, 256, 512, 128)
        H = DIM // HD
        GN_EPS = 0.001

        def _decay_masks(n_heads, seq_len):
            gam = 1.0 - 2.0 ** (-5.0 - jnp.arange(n_heads, dtype=jnp.float32))
            idx = jnp.arange(seq_len, dtype=jnp.float32)
            expo = idx[None, :] - idx[:, None]
            D = jnp.where(expo[None, :, :] <= 0, gam[:, None, None] ** expo[None, :, :], 0.0)
            return D / jnp.sqrt(D.sum(axis=-1))[:, None, :]
        b, s, dim = x.shape
        h, hd, _ = Wh.shape
        xh = x.reshape(b, s, h, hd)
        kh = k.reshape(b, s, h, hd)
        vh = v.reshape(b, s, h, hd)
        Q = jnp.einsum('bshd,hde->bshe', xh, Wh)
        K = jnp.einsum('bshd,hde->bshe', kh, Wh)
        V = jnp.einsum('bshd,hde->bshe', vh, Wh)
        scores = jnp.einsum('bshe,bthe->bhst', Q, K) / jnp.sqrt(jnp.float32(hd))
        Dn = _decay_masks(h, s)
        masked = scores * Dn[None, :, :, :]
        A = jnp.maximum(jnp.abs(masked.sum(axis=0)), 1.0)
        O = jnp.einsum('hst,bthe->bshe', A, V).reshape(b, s, dim)
        mu = O.mean(axis=-1, keepdims=True)
        var = O.var(axis=-1, keepdims=True)
        Y = (O - mu) / jnp.sqrt(var + GN_EPS) * gn_gamma + gn_beta
        W = jax.nn.relu(x @ wg_w)
        return W * Y @ wo_w

    def _L1_ffn_ref(hidden_states, gate_w, w1, w2, sw1, sw2, sw3):
        import jax, jax.numpy as jnp
        import numpy as np
        from jax import lax
        TOP_K = 2
        N_EXPERTS = 8
        B, S, H = hidden_states.shape
        x = hidden_states.reshape(-1, H)
        T = x.shape[0]
        logits = jnp.einsum('th,eh->te', x.astype(jnp.float32), gate_w.astype(jnp.float32))
        scores = jax.nn.softmax(logits, axis=-1)
        topk_w, topk_idx = lax.top_k(scores, TOP_K)
        topk_w = topk_w / (topk_w.sum(-1, keepdims=True) + 1e-20)
        topk_w = topk_w.astype(hidden_states.dtype)
        cw = jnp.zeros((T, N_EXPERTS), hidden_states.dtype).at[jnp.arange(T)[:, None], topk_idx].add(topk_w)

        def body(acc, ew):
            w1e, w2e, cwe = ew
            h = x @ w1e
            g, u = jnp.split(h, 2, axis=-1)
            y = jax.nn.silu(g) * u @ w2e
            return (acc + cwe[:, None] * y, None)
        moe, _ = lax.scan(body, jnp.zeros_like(x), (w1, w2, cw.T))
        moe = moe.reshape(B, S, H)
        shared = jnp.einsum('bsi,hi->bsh', jax.nn.silu(jnp.einsum('bsh,ih->bsi', hidden_states, sw1)) * jnp.einsum('bsh,ih->bsi', hidden_states, sw2), sw3)
        return moe + shared
    x = x + _L0_xattn_ref(_layernorm(x, axis=-1), ctx_2048, mask_BxS2_bk0)
    x = x + _L0_ffn_ref(_layernorm(x, axis=-1), L0_ffn_gate_w, L0_ffn_up_w, L0_ffn_down_w, L0_ffn_gate_scale, L0_ffn_up_scale, L0_ffn_down_scale)
    x = x + _L1_xattn_ref(_layernorm(x, axis=-1), ctx_2048, ctx_2048, L1_xattn_Wh, L1_xattn_wg_w, L1_xattn_wo_w, L1_xattn_gn_gamma, L1_xattn_gn_beta)
    x = x + _L1_ffn_ref(_layernorm(x, axis=-1), L1_ffn_gate_w, L1_ffn_w1, L1_ffn_w2, L1_ffn_sw1, L1_ffn_sw2, L1_ffn_sw3)
    return x

_drawn_inputs = setup_inputs


def setup_inputs(seed=0):
    import zlib

    import numpy as np

    out = dict(_drawn_inputs(seed))
    spreads = {'L1_xattn_gn_gamma': (1.0, 0.2), 'L1_xattn_gn_beta': (0.0, 0.1)}
    factors = {}
    for name, (base, spread) in spreads.items():
        noise = np.random.default_rng([zlib.crc32(name.encode()), seed]).standard_normal(out[name].shape)
        drawn = base * np.exp(spread * noise) if base else spread * noise
        out[name] = jnp.asarray(drawn.astype(out[name].dtype))
    for name, factor in factors.items():
        out[name] = (out[name] * factor).astype(out[name].dtype)
    return out
```

```python
import concourse.bass as bass
from concourse import mybir
from contextlib import ExitStack


def build_decoder_pair(nc, x_in, ctx_in, mask_in, l0_gate, l0_up, l0_down, l0_gscale, l0_uscale, l0_dscale,
                       wh_in, wg_in, wo_in, gamma_in, beta_in, router_in, w1_in, w2_in, sw1_in, sw2_in, sw3_in,
                       decay_in, out):
    F32, F16, U8, U32 = mybir.dt.float32, mybir.dt.float16, mybir.dt.uint8, mybir.dt.uint32
    ALU, ACT, AX = mybir.AluOpType, mybir.ActivationFunctionType, mybir.AxisListType

    P = 128
    BATCH, SEQ, DIM = x_in.shape
    CTX = ctx_in.shape[1]
    ROWT = SEQ // P
    TILES = BATCH * ROWT
    TOK = BATCH * SEQ
    KC = DIM // P
    GT = 4
    GW = GT * P
    GROUPS = TILES // GT
    FFN = l0_gate.shape[1]
    FC = FFN // P
    QW = 3 * DIM
    SCALE = float(DIM) ** -0.5
    LN_EPS = 1e-5
    HEADS = wh_in.shape[0]
    GN_EPS = 1e-3
    EXPERTS = w1_in.shape[0]
    HID = w2_in.shape[1]
    HC = [P, P, HID - 2 * P]
    WS = 32.0
    MASKED = -1e32

    ctx_stack = ExitStack()
    with ctx_stack as top:
        def sb(scope, name, shape, dt):
            return scope.enter_context(nc.sbuf_tensor(name, shape, dt))

        free_at_start = {}

        def sem(name, free=0):
            s = top.enter_context(nc.semaphore(name))
            free_at_start[name] = (s, free)
            return s

        def done(s, n):
            return n + 1 + next(free for t, free in free_at_start.values() if t is s)

        def room(s, n):
            return n + 1

        ident = sb(top, "ident", [P, P], F32)
        x_res = sb(top, "x_res", [P, TILES, DIM], F32)
        ctxT = sb(top, "ctxT", [P, KC, TOK], F32)
        with ExitStack() as early:
            ctx_nat = sb(early, "ctx_nat", [P, TILES, DIM], F32)
        xT_hi = sb(top, "xT_hi", [P, KC, TOK], F16)
        xT_lo = sb(top, "xT_lo", [P, KC, TOK], F16)
        xn = sb(top, "xn", [P, GT, DIM], F32)
        stats = sb(top, "stats", [P, GT, 6], F32)
        meanvar = sb(top, "meanvar", [P, GT, 2], F32)
        vareps = sb(top, "vareps", [P, GT], F32)
        rstd = sb(top, "rstd", [P, GT], F32)
        minus_half = sb(top, "minus_half", [P, GT], F32)

        with ExitStack() as pairs:
            pair = [pairs.enter_context(nc.psum_tensor(f"pair{i}", [P, 2, 512], F32)) for i in range(4)]
        bank = [top.enter_context(nc.psum_tensor(f"bank{i}", [P, 512], F32)) for i in range(8)]

        ffn_w = ExitStack()
        RAW = 4
        raw = sb(ffn_w, "raw", [P, RAW, QW], F32)
        expo = sb(ffn_w, "expo", [P, QW], F32)
        wq = sb(ffn_w, "wq", [P, FC, QW], F16)
        gscale = sb(ffn_w, "gscale", [P, FC], F32)
        uscale = sb(ffn_w, "uscale", [P, FC], F32)
        dscale = sb(ffn_w, "dscale", [P, DIM], F32)

        att0 = ExitStack()
        ctx_stage = sb(att0, "ctx_stage", [P, ROWT, DIM], F32)
        xn0 = sb(att0, "xn0", [P, ROWT, DIM], F32)
        xnT0 = sb(att0, "xnT0", [P, KC, SEQ], F32)
        scores_sb = sb(att0, "scores_sb", [P, ROWT, CTX], F32)
        probs = sb(att0, "probs", [P, ROWT, CTX], F32)
        probsT = sb(att0, "probsT", [P, CTX // P, SEQ], F32)
        mask_u8 = sb(att0, "mask_u8", [P, BATCH, CTX], U8)
        maskbias = sb(att0, "maskbias", [P, BATCH, CTX], F32)
        valid = sb(att0, "valid", [P, BATCH], F32)
        rowmax = sb(att0, "rowmax", [P, ROWT], F32)
        negmax = sb(att0, "negmax", [P, ROWT], F32)
        rowsum = sb(att0, "rowsum", [P, ROWT], F32)
        rinv = sb(att0, "rinv", [P, ROWT], F32)
        rscale = sb(att0, "rscale", [P, ROWT], F32)
        att0.close()

        ffn = ExitStack()
        silu = sb(ffn, "silu", [P, 2, GW], F32)
        fused = sb(ffn, "fused", [P, 2, GW], F32)
        FR = 3
        fT_hi = sb(ffn, "fT_hi", [P, FR, GW], F16)
        fT_lo = sb(ffn, "fT_lo", [P, FR, GW], F16)
        down = sb(ffn, "down", [P, 2, DIM], F32)
        ffn.close()
        ffn_w.close()

        ret = ExitStack()
        wh_f32 = sb(ret, "wh_f32", [P, HEADS, P], F32)
        wh_head = sb(ret, "wh_head", [P, P], F32)
        wh_hi = sb(ret, "wh_hi", [P, HEADS, P], F16)
        wh_lo = sb(ret, "wh_lo", [P, HEADS, P], F16)
        wgo_f32 = sb(ret, "wgo_f32", [P, 2, KC, DIM], F32)
        wgo_hi = sb(ret, "wgo_hi", [P, 2, KC, DIM], F16)
        wgo_lo = sb(ret, "wgo_lo", [P, 2, KC, DIM], F16)
        decay = sb(ret, "decay", [P, ROWT, HEADS, SEQ], F32)
        gamma = sb(ret, "gamma", [P, DIM], F32)
        beta = sb(ret, "beta", [P, DIM], F32)
        qT = sb(ret, "qT", [P, TOK], F32)
        kT = sb(ret, "kT", [P, TOK], F32)
        v = sb(ret, "v", [P, TILES, P], F32)
        scaled = sb(ret, "scaled", [P, SEQ + P], F32)
        floored = sb(ret, "floored", [P, SEQ + P], F32)
        weightT = sb(ret, "weightT", [P, ROWT, SEQ], F32)
        gn_stats = sb(ret, "gn_stats", [P, 6], F32)
        gn_meanvar = sb(ret, "gn_meanvar", [P, 2], F32)
        gn_mean = sb(ret, "gn_mean", [P, TILES], F32)
        gn_vareps = sb(ret, "gn_vareps", [P, TILES], F32)
        gn_rstd = sb(ret, "gn_rstd", [P, TILES], F32)
        y_norm = sb(ret, "y_norm", [P, DIM], F32)
        y_gamma = sb(ret, "y_gamma", [P, DIM], F32)
        y = sb(ret, "y", [P, DIM], F32)
        w_relu = sb(ret, "w_relu", [P, DIM], F32)
        z = sb(ret, "z", [P, DIM], F32)
        zT_hi = sb(ret, "zT_hi", [P, KC, P], F16)
        zT_lo = sb(ret, "zT_lo", [P, KC, P], F16)
        ret.close()

        moe = ExitStack()
        w1_f32 = sb(moe, "w1_f32", [P, KC, 2 * HID], F32)
        w2_f32 = sb(moe, "w2_f32", [P, len(HC), DIM], F32)
        w1_hi = [sb(moe, f"w1_hi{i}", [P, KC, 2 * HID], F16) for i in range(2)]
        w1_lo = [sb(moe, f"w1_lo{i}", [P, KC, 2 * HID], F16) for i in range(2)]
        w2_hi = [sb(moe, f"w2_hi{i}", [P, len(HC), DIM], F16) for i in range(2)]
        w2_lo = [sb(moe, f"w2_lo{i}", [P, len(HC), DIM], F16) for i in range(2)]
        sw12_f32 = sb(moe, "sw12_f32", [P, 2, len(HC), DIM], F32)
        sw3_f32 = sb(moe, "sw3_f32", [P, KC, HID], F32)
        router_f32 = sb(moe, "router_f32", [EXPERTS, DIM], F32)
        router_hi = sb(moe, "router_hi", [P, KC, EXPERTS], F16)
        router_lo = sb(moe, "router_lo", [P, KC, EXPERTS], F16)
        NR = TILES * EXPERTS
        prob = sb(moe, "prob", [P, TILES, EXPERTS], F32)
        prob_max = sb(moe, "prob_max", [P, TILES], F32)
        prob_sum = sb(moe, "prob_sum", [P, TILES], F32)
        above = sb(moe, "above", [P, TILES, EXPERTS, EXPERTS], F32)
        tied = sb(moe, "tied", [P, TILES, EXPERTS, EXPERTS], F32)
        lower = sb(moe, "lower", [P, EXPERTS, EXPERTS], F32)
        rank = sb(moe, "rank", [P, TILES, EXPERTS], F32)
        expert_w = sb(moe, "expert_w", [P, TILES, EXPERTS], F32)
        hg = sb(moe, "hg", [P, 2, GW], F32)
        hp = sb(moe, "hp", [P, 2, GW], F32)
        hT_hi = sb(moe, "hT_hi", [P, 2, len(HC), GW], F16)
        hT_lo = sb(moe, "hT_lo", [P, 2, len(HC), GW], F16)
        moe.close()

        ident_zero, ident_ready = sem("ident_zero"), sem("ident_ready")
        half_ready = sem("half_ready")
        mask_loaded = sem("mask_loaded")
        x_loaded = [sem(f"x_loaded{b}") for b in range(BATCH)]
        c_loaded = [sem(f"c_loaded{b}") for b in range(BATCH)]
        batches_loaded = sem("batches_loaded")
        a_stats, a_meanvar, a_vareps, a_rstd, a_xn = (sem("a_" + n) for n in ("stats", "meanvar", "vareps", "rstd", "xn"))
        a_xnT_psum, a_ctxT_psum, a_xnT, a_ctxT = (sem("a_" + n, 1) for n in ("xnT_psum", "ctxT_psum", "xnT", "ctxT"))
        a_ctx_staged = sem("a_ctx_staged")
        a_bias, a_valid, a_rowmax, a_negmax, a_rscale = (
            sem("a_" + n) for n in ("bias", "valid", "rowmax", "negmax", "rscale"))
        a_scores, a_masked, a_probs, a_probsT_psum, a_probsT, a_readout, a_rinv, a_resid = (
            sem("a_" + n, 1) for n in ("scores", "masked", "probs", "probsT_psum", "probsT", "readout", "rinv", "resid"))
        out_stored = sem("out_stored")
        c_loaded_w, c_hi, c_lo, c_ones = sem("c_loaded_w"), sem("c_hi"), sem("c_lo"), sem("c_ones")
        c_head = sem("c_head")
        c_proj, c_copied = sem("c_proj"), sem("c_copied", 4)
        c_scores, c_masked, c_scaled, c_weights = sem("c_scores", 1), sem("c_masked", 1), sem("c_scaled"), sem("c_weights")
        c_o_ps, c_o_copied = sem("c_o_ps", 4), sem("c_o_copied", 2)
        g_stats, g_meanvar, g_vareps, g_rstd = (sem("g_" + n) for n in ("stats", "meanvar", "vareps", "rstd"))
        g_w_ps, g_w, g_ynorm, g_ygamma, g_y = (sem("g_" + n, free) for n, free in (
            ("w_ps", 0), ("w", 1), ("ynorm", 0), ("ygamma", 1), ("y", 0)))
        g_z, g_zT_ps, g_hi, g_lo, g_wo, g_resid = (
            sem("g_z", 1), sem("g_zT_ps", 1), sem("g_hi"), sem("g_lo", 1), sem("g_wo", 1), sem("g_resid", 1))

        def norm_sems(t):
            return {n: sem(f"{t}_{n}", free) for n, free in (("stats", 0), ("meanvar", 0), ("vareps", 0), ("rstd", 0),
                                                             ("xn", 0), ("xT_psum", 1), ("hi", 0), ("lo", 1))}
        nb = norm_sems("b")
        nr = norm_sems("r")
        nd = norm_sems("d")
        d_shared_loaded, d_w_loaded = sem("d_shared_loaded"), sem("d_w_loaded")
        d_sw_ps, d_sw_hi, d_sw_lo = sem("d_sw_ps"), sem("d_sw_hi"), sem("d_sw_lo", 4)
        d_ones, d_lower = sem("d_ones"), sem("d_lower")
        d_logits, d_route, d_exp, d_weights = (sem("d_" + n) for n in ("logits", "route", "exp", "weights"))
        d_whi, d_wlo = sem("d_whi"), sem("d_wlo", 1)
        d_gate_ps, d_up_ps, d_silu = (sem("d_" + n) for n in ("gate_ps", "up_ps", "silu"))
        d_prod, d_hhi, d_hlo = sem("d_prod", 2), sem("d_hhi"), sem("d_hlo", 2)
        d_y_ps, d_acc = sem("d_y_ps", 2 * GT), sem("d_acc", GT)

        raw_loaded = [sem(f"raw_loaded{i}") for i in range(RAW)]
        scales_loaded = sem("scales_loaded")
        w_expo, w_magic, w_sum = (sem("w_" + n) for n in ("expo", "magic", "sum"))
        w_quant = sem("w_quant", 1)
        b_gate_ps, b_up_ps, b_silu, b_flo, b_resid = (sem("b_" + n) for n in ("gate_ps", "up_ps", "silu", "flo", "resid"))
        b_fused, b_fhi, b_down = sem("b_fused", 2), sem("b_fhi", 2), sem("b_down", FR)
        b_scaled = sem("b_scaled", GT)

        def gate_chunk(i):
            return l0_gate.rearrange("(k p) f -> p k f", p=P)[:, :, i * P:(i + 1) * P]

        def up_chunk(i):
            return l0_up.rearrange("(k p) f -> p k f", p=P)[:, :, i * P:(i + 1) * P]

        waits_passed = sem("waits_passed")

        def hold(engine, semaphore, value):
            engine.wait_ge(semaphore, value)
            engine.sem_inc(waits_passed, 1)

        def sw_units():
            for t in range(2):
                for k in range(KC):
                    yield (bank[(t * KC + k) % 4][:, 0:HID], w1_hi[0][:, k, t * HID:(t + 1) * HID],
                           w1_lo[0][:, k, t * HID:(t + 1) * HID])
            for c, rows in enumerate(HC):
                yield bank[(2 * KC + c) % 4][0:rows, :], w2_hi[0][0:rows, c, :], w2_lo[0][0:rows, c, :]
            yield (bank[(2 * KC + len(HC)) % 4][:, 0:KC * EXPERTS].rearrange("p (k e) -> p k e", e=EXPERTS),
                   router_hi[:], router_lo[:])

        block = top.enter_context(nc.Block())

        @block.sync
        def _(sp):
            for s, free in free_at_start.values():
                if free:
                    sp.sem_inc(s, free)
            xv = x_in.rearrange("b (j p) d -> b p j d", p=P)
            cv = ctx_in.rearrange("b (j p) d -> b p j d", p=P)
            sp.dma_start(mask_u8[:], mask_in.partition_broadcast(P)).then_inc(mask_loaded, 16)
            for b in range(BATCH):
                sp.dma_start(x_res[:, ROWT * b:ROWT * (b + 1), :], xv[b]).then_inc(x_loaded[b], 16)
                sp.dma_start(ctx_nat[:, ROWT * b:ROWT * (b + 1), :], cv[b]).then_inc(c_loaded[b], 16)
            sp.dma_start(gscale[:], l0_gscale.rearrange("(c p) -> p c", p=P),
                         allow_slow_non_contiguous=True).then_inc(scales_loaded, 16)
            sp.dma_start(uscale[:], l0_uscale.rearrange("(c p) -> p c", p=P),
                         allow_slow_non_contiguous=True).then_inc(scales_loaded, 16)
            sp.dma_start(dscale[:], l0_dscale.partition_broadcast(P)).then_inc(scales_loaded, 16)

            def load_raw(i):
                slot = i % RAW
                rv = raw[:, slot, 0:2 * DIM].rearrange("p (t k f) -> p t k f", t=2, f=P)
                sp.dma_start(rv[:, 0], gate_chunk(i)).then_inc(raw_loaded[slot], 16)
                sp.dma_start(rv[:, 1], up_chunk(i)).then_inc(raw_loaded[slot], 16)
                sp.dma_start(raw[:, slot, 2 * DIM:QW], l0_down[i * P:(i + 1) * P, :]).then_inc(raw_loaded[slot], 16)
            for i in range(RAW):
                load_raw(i)
            for b in range(BATCH):
                sp.wait_ge(x_loaded[b], 16)
                sp.wait_ge(c_loaded[b], 16)
                sp.sem_inc(batches_loaded, 1)
            for i in range(RAW, FC):
                sp.wait_ge(w_quant, done(w_quant, i - RAW))
                load_raw(i)
            ov = out.rearrange("b (j p) d -> p (b j) d", p=P)
            sp.wait_ge(b_resid, TILES)
            sp.dma_start(wh_f32[:], wh_in.rearrange("h d e -> d h e")).then_inc(c_loaded_w, 16)
            sp.dma_start(wgo_f32[:, 0], wg_in.rearrange("(k p) n -> p k n", p=P)).then_inc(c_loaded_w, 16)
            sp.dma_start(wgo_f32[:, 1], wo_in.rearrange("(k p) n -> p k n", p=P)).then_inc(c_loaded_w, 16)
            sp.dma_start(decay[:], decay_in.rearrange("(j p) h s -> p j h s", p=P)).then_inc(c_loaded_w, 16)
            sp.dma_start(gamma[:], gamma_in.partition_broadcast(P)).then_inc(c_loaded_w, 16)
            sp.dma_start(beta[:], beta_in.partition_broadcast(P)).then_inc(c_loaded_w, 16)
            sp.wait_ge(g_resid, done(g_resid, TILES - 1))
            def hidden_rows(dst, src):
                sp.dma_start(dst[:, 0:2, :], src[0:2 * P, :].rearrange("(c p) n -> p c n", p=P)).then_inc(d_shared_loaded, 16)
                sp.dma_start(dst[0:HC[2], 2, :], src[2 * P:HID, :]).then_inc(d_shared_loaded, 16)
            sp.dma_start(router_f32[:], router_in).then_inc(d_shared_loaded, 16)
            hidden_rows(sw12_f32[:, 0], sw1_in)
            hidden_rows(sw12_f32[:, 1], sw2_in)
            sp.dma_start(sw3_f32[:], sw3_in.rearrange("(k p) n -> p k n", p=P)).then_inc(d_shared_loaded, 16)
            with sp.Fori(0, EXPERTS) as e:
                sp.wait_ge(d_wlo, room(d_wlo, e))
                sp.dma_start(w1_f32[:], w1_in.rearrange("e (k p) f -> p e k f", p=P)[:, e]).then_inc(d_w_loaded, 16)
                w2e = w2_in[e]
                sp.dma_start(w2_f32[:, 0:2, :], w2e[0:2 * P, :].rearrange("(c p) n -> p c n", p=P)).then_inc(d_w_loaded, 16)
                sp.dma_start(w2_f32[0:HC[2], 2, :], w2e[2 * P:HID, :]).then_inc(d_w_loaded, 16)
            sp.wait_ge(d_acc, done(d_acc, (EXPERTS + 1) * TILES - 1))
            sp.dma_start(ov, x_res[:]).then_inc(out_stored, 16)
            sp.wait_ge(out_stored, 16)

        @block.gpsimd
        def _(pool):
            pool.memset(ident[:], 0.0).then_inc(ident_zero, 1)
            pool.memset(minus_half[:], -0.5).then_inc(half_ready, 1)
            pool.wait_ge(ident_zero, 1)
            pool.affine_select(out=ident[:], in_=ident[:], compare_op=ALU.not_equal, fill=1.0, base=0,
                               pattern=[[-1, P]], channel_multiplier=1).then_inc(ident_ready, 1)
            pool.wait_ge(half_ready, 1)

            def inverse_deviation(n, s_meanvar, s_vareps, s_rstd, width):
                hold(pool, s_meanvar, n + 1)
                pool.tensor_scalar(vareps[:, 0:width], meanvar[:, 0:width, 1], LN_EPS, None, ALU.add).then_inc(s_vareps, 1)
                pool.wait_ge(s_vareps, n + 1)
                pool.tensor_tensor(rstd[:, 0:width], vareps[:, 0:width], minus_half[:, 0:width], ALU.pow).then_inc(s_rstd, 1)

            with pool.Fori(0, BATCH) as b:
                pool.wait_ge(batches_loaded, b + 1)
                pool.wait_ge(a_ctxT_psum, room(a_ctxT_psum, b))
                pool.tensor_copy(ctx_stage[:], ctx_nat[:, bass.ds(ROWT * b, ROWT), :]).then_inc(a_ctx_staged, 1)
                inverse_deviation(b, a_meanvar, a_vareps, a_rstd, ROWT)
            with pool.Fori(0, GROUPS) as g:
                inverse_deviation(g, nb["meanvar"], nb["vareps"], nb["rstd"], GT)
            with pool.Fori(0, GROUPS) as g:
                inverse_deviation(g, nr["meanvar"], nr["vareps"], nr["rstd"], GT)
            pool.wait_ge(b_resid, TILES)
            pool.memset(weightT[:], 1.0).then_inc(c_ones, 1)
            pool.wait_ge(c_loaded_w, 96)
            with pool.Fori(0, HEADS) as h:
                pool.wait_ge(c_scores, room(c_scores, h))
                pool.tensor_copy(wh_head[:], wh_f32[:, h, :]).then_inc(c_head, 1)

            def group_deviation(t):
                pool.wait_ge(g_vareps, t + 1)
                pool.tensor_tensor(gn_rstd[:, bass.ds(t, 1)], gn_vareps[:, bass.ds(t, 1)], minus_half[:, 0:1], ALU.pow).then_inc(g_rstd, 1)

            def gamma_beta(t):
                pool.wait_ge(g_ynorm, t + 1)
                pool.tensor_tensor(y_gamma[:], y_norm[:], gamma[:], ALU.mult).then_inc(g_ygamma, 1)
                pool.wait_ge(g_z, room(g_z, t))
                hold(pool, g_ygamma, done(g_ygamma, t))
                pool.tensor_tensor(y[:], y_gamma[:], beta[:], ALU.add).then_inc(g_y, 1)

            group_deviation(0)
            group_deviation(1)
            gamma_beta(0)
            with pool.Fori(0, TILES - 2) as t:
                group_deviation(t + 2)
                gamma_beta(t + 1)
            gamma_beta(TILES - 1)
            with pool.Fori(0, GROUPS) as g:
                inverse_deviation(g, nd["meanvar"], nd["vareps"], nd["rstd"], GT)
            pool.wait_ge(g_resid, done(g_resid, TILES - 1))
            pool.memset(lower[:], 1.0).then_inc(d_ones, 1)
            pool.wait_ge(d_ones, 1)
            pool.affine_select(out=lower[:], in_=lower[:], compare_op=ALU.is_gt, fill=0.0, base=0,
                               pattern=[[1, EXPERTS], [-1, EXPERTS]], channel_multiplier=0).then_inc(d_lower, 1)

        @block.tensor
        def _(pe):
            pe.wait_ge(ident_ready, 1)

            def transpose_inputs(b):
                pe.wait_ge(a_xn, b + 1)
                pe.wait_ge(a_xnT, room(a_xnT, b))
                for j in range(ROWT):
                    for k in range(KC):
                        last = pe.transpose(pair[0][:, j, k * P:(k + 1) * P], xn0[:, j, k * P:(k + 1) * P], ident[:])
                last.then_inc(a_xnT_psum, 1)
                pe.wait_ge(a_ctx_staged, b + 1)
                pe.wait_ge(a_ctxT, room(a_ctxT, b))
                for j in range(ROWT):
                    for k in range(KC):
                        last = pe.transpose(pair[1][:, j, k * P:(k + 1) * P],
                                            ctx_stage[:, j, k * P:(k + 1) * P], ident[:])
                last.then_inc(a_ctxT_psum, 1)

            def score(b):
                pe.wait_ge(a_xnT, done(a_xnT, b))
                pe.wait_ge(a_ctxT, done(a_ctxT, b))
                pe.wait_ge(a_masked, room(a_masked, b))
                for j in range(ROWT):
                    for k in range(KC):
                        last = pe.matmul(bank[4][:, j * CTX:(j + 1) * CTX], xnT0[:, k, j * P:(j + 1) * P],
                                         ctxT[:, k, bass.ds(b * CTX, CTX)], start=(k == 0), stop=(k == KC - 1))
                last.then_inc(a_scores, 1)

            def transpose_probs(b):
                pe.wait_ge(a_probs, done(a_probs, b))
                pe.wait_ge(a_probsT, room(a_probsT, b))
                for m in range(CTX // P):
                    for j in range(ROWT):
                        last = pe.transpose(bank[5][:, m * SEQ + j * P:m * SEQ + (j + 1) * P],
                                            probs[:, j, m * P:(m + 1) * P], ident[:])
                last.then_inc(a_probsT_psum, 1)

            def read_out(b):
                pe.wait_ge(a_probsT, done(a_probsT, b))
                pe.wait_ge(a_resid, room(a_resid, b))
                for j in range(ROWT):
                    for m in range(CTX // P):
                        last = pe.matmul(bank[6 + j][:], probsT[:, m, j * P:(j + 1) * P],
                                         ctx_nat[:, ROWT * b + m, :], start=(m == 0), stop=(m == CTX // P - 1))
                last.then_inc(a_readout, 1)

            transpose_inputs(0)
            score(0)
            transpose_inputs(1)
            transpose_probs(0)
            with pe.Fori(1, BATCH - 1) as b:
                score(b)
                transpose_inputs(b + 1)
                read_out(b - 1)
                transpose_probs(b)
            score(BATCH - 1)
            read_out(BATCH - 2)
            transpose_probs(BATCH - 1)
            read_out(BATCH - 1)

            def transpose_group(g, s):
                pe.wait_ge(s["xn"], g + 1)
                pe.wait_ge(s["lo"], room(s["lo"], g))
                for i in range(GT):
                    for k in range(KC):
                        last = pe.transpose(pair[i // 2][:, i % 2, k * P:(k + 1) * P], xn[:, i, k * P:(k + 1) * P], ident[:])
                last.then_inc(s["xT_psum"], 1)

            with pe.Fori(0, GROUPS) as g:
                transpose_group(g, nb)

            def gate_up(g, c):
                n = g * FC + c
                pe.wait_ge(w_quant, done(w_quant, c))
                pe.wait_ge(b_fused, room(b_fused, n))
                for t, (at, signal) in enumerate(((c % 2, b_gate_ps), (2 + c % 2, b_up_ps))):
                    for k in range(KC):
                        for part in (xT_hi, xT_lo):
                            last = pe.matmul(bank[at][:], wq[:, c, (t * KC + k) * P:(t * KC + k + 1) * P],
                                             part[:, k, bass.ds(g * GW, GW)],
                                             start=(k == 0 and part is xT_hi), stop=(k == KC - 1 and part is xT_lo))
                    last.then_inc(signal, 1)

            def down_chunk(g, c):
                n = g * FC + c
                pe.wait_ge(b_fhi, done(b_fhi, n))
                pe.wait_ge(b_flo, n + 1)
                if c == 0:
                    pe.wait_ge(b_scaled, room(b_scaled, GT * g + GT - 1))
                for i in range(GT):
                    for part in (fT_hi, fT_lo):
                        last = pe.matmul(bank[4 + i][:], part[:, c % FR, i * P:(i + 1) * P],
                                         wq[:, c, 2 * DIM:QW], start=(c == 0 and part is fT_hi),
                                         stop=(c == FC - 1 and part is fT_lo))
                last.then_inc(b_down, 1)

            pe.wait_ge(nb["lo"], done(nb["lo"], GROUPS - 1))
            with pe.Fori(0, GROUPS) as g:
                for c in range(FC):
                    gate_up(g, c)
                    if c:
                        down_chunk(g, c - 1)
                down_chunk(g, FC - 1)

            pe.wait_ge(b_scaled, done(b_scaled, TILES - 1))
            with pe.Fori(0, GROUPS) as g:
                transpose_group(g, nr)
            pe.wait_ge(nr["lo"], done(nr["lo"], GROUPS - 1))
            pe.wait_ge(c_lo, 3)
            pe.wait_ge(c_ones, 1)
            with pe.Fori(0, HEADS) as h:
                for i in range(GROUPS):
                    pe.wait_ge(c_copied, room(c_copied, h * 12 + i))
                    for n, (w, part) in enumerate(((wh_hi, xT_hi), (wh_hi, xT_lo), (wh_lo, xT_hi))):
                        last = pe.matmul(bank[i][:], w[:, h, :], part[:, h, i * GW:(i + 1) * GW],
                                         start=(n == 0), stop=(n == 2))
                    last.then_inc(c_proj, 1)
                pe.wait_ge(c_head, h + 1)
                for i in range(GROUPS):
                    pe.wait_ge(c_copied, room(c_copied, h * 12 + 4 + i))
                    pe.matmul(bank[i][:], wh_head[:], ctxT[:, h, i * GW:(i + 1) * GW],
                              start=True, stop=True).then_inc(c_proj, 1)
                for i in range(GROUPS):
                    pe.wait_ge(c_copied, done(c_copied, h * 12 + 4 + i))
                    for j in range(GT):
                        last = pe.transpose(bank[i][:, j * P:(j + 1) * P], kT[:, (GT * i + j) * P:(GT * i + j + 1) * P], ident[:])
                    last.then_inc(c_proj, 1)
                pe.wait_ge(c_masked, room(c_masked, h))
                for b in range(BATCH):
                    pe.matmul(bank[4][:, 0:SEQ], kT[:, b * SEQ:b * SEQ + P], qT[:, b * SEQ:(b + 1) * SEQ],
                              start=(b == 0), stop=(b == BATCH - 1))
                for b in range(BATCH):
                    last = pe.matmul(bank[5][:, 0:P], kT[:, b * SEQ + P:(b + 1) * SEQ], qT[:, b * SEQ + P:(b + 1) * SEQ],
                                     start=(b == 0), stop=(b == BATCH - 1))
                last.then_inc(c_scores, 1)
                pe.wait_ge(c_copied, done(c_copied, h * 12 + 11))
                pe.wait_ge(c_weights, h + 1)
                vv = v[:].rearrange("p (b j) e -> p j b e", j=ROWT)
                for j in range(ROWT):
                    for half in range(2):
                        o = 2 * j + half
                        pe.wait_ge(c_o_copied, room(c_o_copied, 4 * h + o))
                        for m in range(ROWT):
                            last = pe.matmul(bank[6 + half][:], weightT[:, m, j * P:(j + 1) * P],
                                             vv[:, m, 4 * half:4 * half + 4, :], start=(m == 0), stop=(m == ROWT - 1))
                        last.then_inc(c_o_ps, 1)

            def gate_project(t):
                pe.wait_ge(g_w, room(g_w, t))
                for k in range(KC):
                    tok = bass.ds(t * P, P)
                    for n, (part, w) in enumerate(((xT_hi, wgo_hi), (xT_hi, wgo_lo), (xT_lo, wgo_hi))):
                        last = pe.matmul(bank[0][:], part[:, k, tok], w[:, 0, k, :],
                                         start=(k == 0 and n == 0), stop=(k == KC - 1 and n == 2))
                last.then_inc(g_w_ps, 1)

            def transpose_z(t):
                pe.wait_ge(g_z, done(g_z, t))
                pe.wait_ge(g_lo, room(g_lo, t))
                for k in range(KC):
                    last = pe.transpose(bank[1][:, k * P:(k + 1) * P], z[:, k * P:(k + 1) * P], ident[:])
                last.then_inc(g_zT_ps, 1)

            def out_project(t):
                pe.wait_ge(g_lo, done(g_lo, t))
                pe.wait_ge(g_resid, room(g_resid, t))
                for k in range(KC):
                    for n, (part, w) in enumerate(((zT_hi, wgo_hi), (zT_hi, wgo_lo), (zT_lo, wgo_hi))):
                        last = pe.matmul(bank[2][:], part[:, k, :], w[:, 1, k, :],
                                         start=(k == 0 and n == 0), stop=(k == KC - 1 and n == 2))
                last.then_inc(g_wo, 1)

            pe.wait_ge(c_copied, done(c_copied, HEADS * 12 - 1))
            gate_project(0)
            gate_project(1)
            transpose_z(0)
            with pe.Fori(1, TILES - 1) as t:
                gate_project(t + 1)
                transpose_z(t)
                out_project(t - 1)
            transpose_z(TILES - 1)
            out_project(TILES - 2)
            out_project(TILES - 1)

            pe.wait_ge(g_resid, done(g_resid, TILES - 1))
            with pe.Fori(0, GROUPS) as g:
                transpose_group(g, nd)
            pe.wait_ge(nd["lo"], done(nd["lo"], GROUPS - 1))
            pe.wait_ge(d_shared_loaded, 16 * 6)
            n = 0
            for t in range(2):
                for k in range(KC):
                    pe.wait_ge(d_sw_lo, room(d_sw_lo, n))
                    for c, rows in enumerate(HC):
                        last = pe.transpose(bank[n % 4][:, c * P:c * P + rows], sw12_f32[0:rows, t, c, k * P:(k + 1) * P],
                                            ident[0:rows, 0:rows])
                    last.then_inc(d_sw_ps, 1)
                    n += 1
            for c, rows in enumerate(HC):
                pe.wait_ge(d_sw_lo, room(d_sw_lo, n))
                for k in range(KC):
                    last = pe.transpose(bank[n % 4][0:rows, k * P:(k + 1) * P], sw3_f32[:, k, c * P:c * P + rows], ident[:])
                last.then_inc(d_sw_ps, 1)
                n += 1
            pe.wait_ge(d_sw_lo, room(d_sw_lo, n))
            for k in range(KC):
                last = pe.transpose(bank[n % 4][:, k * EXPERTS:(k + 1) * EXPERTS], router_f32[:, k * P:(k + 1) * P],
                                    ident[0:EXPERTS, 0:EXPERTS])
            last.then_inc(d_sw_ps, 1)
            pe.wait_ge(d_sw_lo, done(d_sw_lo, n))
            for t in range(TILES):
                for k in range(KC):
                    tok = slice(t * P, (t + 1) * P)
                    for i, (part, w) in enumerate(((xT_hi, router_hi), (xT_hi, router_lo), (xT_lo, router_hi))):
                        last = pe.matmul(bank[4][:, t * EXPERTS:(t + 1) * EXPERTS], part[:, k, tok], w[:, k, :],
                                         start=(k == 0 and i == 0), stop=(k == KC - 1 and i == 2))
            last.then_inc(d_logits, 1)
            pe.wait_ge(d_route, 1)

            def expert_up(m, mod, slot):
                for c, rows in enumerate(HC):
                    q = m * 3 + c
                    r = (mod + c) % 2
                    pe.wait_ge(d_prod, room(d_prod, q))
                    for t, (at, signal) in enumerate(((r, d_gate_ps), (2 + r, d_up_ps))):
                        for k in range(KC):
                            cols = slice(t * HID + c * P, t * HID + c * P + rows)
                            for i, (w, part) in enumerate(((w1_hi, xT_hi), (w1_hi, xT_lo), (w1_lo, xT_hi))):
                                last = pe.matmul(bank[at][0:rows, :], w[slot][:, k, cols],
                                                 part[:, k, mod * GW:(mod + 1) * GW],
                                                 start=(k == 0 and i == 0), stop=(k == KC - 1 and i == 2))
                        last.then_inc(signal, 1)

            def expert_down(m, mod, slot):
                pe.wait_ge(d_hlo, done(d_hlo, m * 3 + 2))
                for i in range(GT):
                    pe.wait_ge(d_acc, room(d_acc, m * GT + i))
                    for c, rows in enumerate(HC):
                        for n, (part, w) in enumerate(((hT_hi, w2_hi), (hT_hi, w2_lo), (hT_lo, w2_hi))):
                            last = pe.matmul(bank[4 + i][:], part[0:rows, mod % 2, c, i * P:(i + 1) * P],
                                             w[slot][0:rows, c, :], start=(c == 0 and n == 0), stop=(c == 2 and n == 2))
                    last.then_inc(d_y_ps, 1)

            expert_up(0, 0, 0)
            for grp in range(1, GROUPS):
                expert_up(grp, grp, 0)
                expert_down(grp - 1, grp - 1, 0)
            with pe.Fori(0, EXPERTS // 2) as pair_i:
                for s in range(2):
                    for grp in range(GROUPS):
                        m = pair_i * (2 * GROUPS) + (GROUPS * (s + 1) + grp)
                        if grp == 0:
                            pe.wait_ge(d_wlo, done(d_wlo, pair_i * 2 + s))
                        expert_up(m, grp, (s + 1) % 2)
                        expert_down(m - 1, (grp - 1) % GROUPS, (s + 1) % 2 if grp else s % 2)
            expert_down((EXPERTS + 1) * GROUPS - 1, GROUPS - 1, EXPERTS % 2)

        @block.scalar
        def _(act):
            def copy_inputs(b):
                pv = pair[0][:].rearrange("p j (k c) -> p j k c", c=P)
                act.wait_ge(a_xnT_psum, done(a_xnT_psum, b))
                act.wait_ge(a_scores, room(a_scores, b))
                act.activation(xnT0[:].rearrange("p k (j c) -> p j k c", c=P), pv, ACT.Copy).then_inc(a_xnT, 1)
                act.wait_ge(a_ctxT_psum, done(a_ctxT_psum, b))
                act.activation(ctxT[:, :, bass.ds(b * CTX, CTX)].rearrange("p k (j c) -> p j k c", c=P),
                               pair[1][:].rearrange("p j (k c) -> p j k c", c=P), ACT.Copy).then_inc(a_ctxT, 1)

            def exponentials(b):
                act.wait_ge(a_negmax, b + 1)
                act.wait_ge(a_probsT_psum, room(a_probsT_psum, b))
                act.wait_ge(a_rinv, room(a_rinv, b))
                for j in range(ROWT):
                    last = act.activation(probs[:, j, :], scores_sb[:, j, :], ACT.Exp, bias=negmax[:, j:j + 1],
                                          scale=SCALE, accum_out=rowsum[:, j:j + 1])
                last.then_inc(a_probs, 1)

            def copy_probsT(b):
                act.wait_ge(a_probsT_psum, done(a_probsT_psum, b))
                act.wait_ge(a_readout, room(a_readout, b))
                act.activation(probsT[:].rearrange("p m s -> p (m s)"), bank[5][:], ACT.Copy).then_inc(a_probsT, 1)

            copy_inputs(0)
            with act.Fori(0, BATCH - 1) as b:
                copy_inputs(b + 1)
                exponentials(b)
                copy_probsT(b)
            exponentials(BATCH - 1)
            copy_probsT(BATCH - 1)

            def split_hi(g, s):
                act.wait_ge(s["xT_psum"], done(s["xT_psum"], g))
                for h in range(2):
                    last = act.activation(xT_hi[:, :, bass.ds((GT * g + 2 * h) * P, 2 * P)].rearrange("p k (j c) -> p j k c", c=P),
                                   pair[h][:].rearrange("p j (k c) -> p j k c", c=P),
                                   ACT.Copy)
                last.then_inc(s["hi"], 1)
            with act.Fori(0, GROUPS) as g:
                split_hi(g, nb)

            act.wait_ge(scales_loaded, 48)

            def gate(g, c):
                n = g * FC + c
                act.wait_ge(b_gate_ps, n + 1)
                act.wait_ge(b_fused, room(b_fused, n))
                act.activation(silu[:, c % 2, :], bank[c % 2][:], ACT.Silu, scale=gscale[:, c:c + 1]).then_inc(b_silu, 1)

            def fused_hi(g, c):
                n = g * FC + c
                act.wait_ge(b_fused, done(b_fused, n))
                act.wait_ge(b_down, room(b_down, n))
                act.activation(fT_hi[:, c % FR, :], fused[:, c % 2, :], ACT.Copy).then_inc(b_fhi, 1)

            with act.Fori(0, GROUPS) as g:
                for c in range(FC):
                    gate(g, c)
                    if c:
                        fused_hi(g, c - 1)
                fused_hi(g, FC - 1)

            with act.Fori(0, GROUPS) as g:
                split_hi(g, nr)
            act.wait_ge(c_loaded_w, 96)
            act.activation(wh_hi[:], wh_f32[:], ACT.Copy, scale=WS).then_inc(c_hi, 1)
            for i in range(2):
                act.activation(wgo_hi[:, i], wgo_f32[:, i], ACT.Copy, scale=WS).then_inc(c_hi, 1)

            with act.Fori(0, HEADS) as h:
                act.wait_ge(c_scores, room(c_scores, h))
                for i in range(3 * GROUPS):
                    if i == 2 * GROUPS:
                        act.wait_ge(c_o_ps, room(c_o_ps, 4 * h + 3))
                    act.wait_ge(c_proj, h * 12 + i + 1)
                    at = slice(i % GROUPS * GW, (i % GROUPS + 1) * GW)
                    dst = (qT[:, at], kT[:, at], v[:].rearrange("p t e -> p (t e)")[:, at])[i // GROUPS]
                    act.activation(dst, bank[i % GROUPS][:], ACT.Copy, scale=1.0 / WS if i < GROUPS else 1.0).then_inc(c_copied, 1)

            def relu_gate(t):
                act.wait_ge(g_w_ps, t + 1)
                act.wait_ge(g_z, room(g_z, t))
                act.activation(w_relu[:], bank[0][:], ACT.Relu, scale=1.0 / WS).then_inc(g_w, 1)

            def split_z(t):
                act.wait_ge(g_zT_ps, done(g_zT_ps, t))
                act.wait_ge(g_wo, room(g_wo, t))
                act.activation(zT_hi[:].rearrange("p k c -> p (k c)"), bank[1][:], ACT.Copy).then_inc(g_hi, 1)

            relu_gate(0)
            with act.Fori(0, TILES - 1) as t:
                relu_gate(t + 1)
                split_z(t)
            split_z(TILES - 1)

            with act.Fori(0, GROUPS) as g:
                split_hi(g, nd)
            for n, (src, hi, lo) in enumerate(sw_units()):
                act.wait_ge(d_sw_ps, n + 1)
                act.activation(hi, src, ACT.Copy, scale=WS).then_inc(d_sw_hi, 1)
            act.wait_ge(d_route, 2)
            act.activation(prob[:], prob[:], ACT.Exp).then_inc(d_exp, 1)

            def expert_hi(e, slot):
                act.wait_ge(d_w_loaded, 48 * e + 48)
                act.wait_ge(d_y_ps, GT * GROUPS * e + 2 * GT)
                act.activation(w1_hi[slot][:], w1_f32[:], ACT.Copy, scale=WS)
                act.activation(w2_hi[slot][:, 0:2], w2_f32[:, 0:2], ACT.Copy, scale=WS)
                act.activation(w2_hi[slot][0:HC[2], 2], w2_f32[0:HC[2], 2], ACT.Copy, scale=WS).then_inc(d_whi, 1)

            def expert_act(m, mod):
                for c in range(4):
                    if c < 3:
                        rows, q, r = HC[c], m * 3 + c, (mod + c) % 2
                        act.wait_ge(d_gate_ps, q + 1)
                        act.wait_ge(d_prod, room(d_prod, q))
                        act.activation(hg[0:rows, r, :], bank[r][0:rows, :], ACT.Silu, scale=1.0 / WS).then_inc(d_silu, 1)
                    if c:
                        rows, q, r = HC[c - 1], m * 3 + c - 1, (mod + c - 1) % 2
                        act.wait_ge(d_prod, done(d_prod, q))
                        if c == 1:
                            act.wait_ge(d_y_ps, room(d_y_ps, m * GT + GT - 1))
                        act.activation(hT_hi[0:rows, mod % 2, c - 1, :], hp[0:rows, r, :], ACT.Copy).then_inc(d_hhi, 1)

            for grp in range(GROUPS):
                expert_act(grp, grp)
                if grp == 1:
                    expert_hi(0, 1)
            with act.Fori(0, EXPERTS // 2 - 1) as pair_i:
                for s in range(2):
                    for grp in range(GROUPS):
                        expert_act(pair_i * (2 * GROUPS) + (GROUPS * (s + 1) + grp), grp)
                        if grp == 1:
                            expert_hi(pair_i * 2 + (s + 1), s % 2)
            for s in range(2):
                for grp in range(GROUPS):
                    expert_act((EXPERTS - 1 + s) * GROUPS + grp, grp)
                    if grp == 1 and s == 0:
                        expert_hi(EXPERTS - 1, 0)

        @block.vector
        def _(dve):
            dve.wait_ge(mask_loaded, 16)
            dve.tensor_scalar(maskbias[:], mask_u8[:], -MASKED, MASKED, ALU.mult, ALU.add).then_inc(a_bias, 1)
            dve.tensor_reduce(valid[:], mask_u8[:], AX.X, ALU.max).then_inc(a_valid, 1)

            def normalise0(b):
                dve.wait_ge(batches_loaded, b + 1)
                for j in range(ROWT):
                    dve.bn_stats(stats[:, j, :], x_res[:, ROWT * b + j, :]).then_inc(a_stats, 1)
                hold(dve, a_stats, ROWT * b + ROWT)
                for j in range(ROWT):
                    last = dve.bn_aggr(meanvar[:, j, :], stats[:, j, :])
                last.then_inc(a_meanvar, 1)
                dve.wait_ge(a_rstd, b + 1)
                dve.wait_ge(a_xnT_psum, room(a_xnT_psum, b))
                for j in range(ROWT):
                    last = dve.tensor_scalar(xn0[:, j, :], x_res[:, ROWT * b + j, :], meanvar[:, j, 0:1],
                                             rstd[:, j:j + 1], ALU.subtract, ALU.mult)
                last.then_inc(a_xn, 1)

            def mask_and_max(b):
                dve.wait_ge(a_scores, done(a_scores, b))
                dve.wait_ge(a_probs, room(a_probs, b))
                mb = maskbias[:, b, :]
                for j in range(ROWT):
                    last = dve.tensor_tensor(scores_sb[:, j, :], bank[4][:, j * CTX:(j + 1) * CTX], mb, ALU.add)
                last.then_inc(a_masked, 1)
                dve.wait_ge(a_masked, done(a_masked, b))
                dve.tensor_reduce(rowmax[:], scores_sb[:], AX.X, ALU.max).then_inc(a_rowmax, 1)
                dve.wait_ge(a_rowmax, b + 1)
                dve.tensor_scalar(negmax[:], rowmax[:], -SCALE, None, ALU.mult).then_inc(a_negmax, 1)

            def inverse_sums(b):
                dve.wait_ge(a_probs, done(a_probs, b))
                dve.reciprocal(rinv[:], rowsum[:]).then_inc(a_rinv, 1)
                dve.wait_ge(a_rinv, done(a_rinv, b))
                dve.tensor_scalar(rscale[:], rinv[:], valid[:, bass.ds(b, 1)], None, ALU.mult).then_inc(a_rscale, 1)

            def add_readout(b):
                dve.wait_ge(a_rscale, b + 1)
                dve.wait_ge(a_readout, done(a_readout, b))
                for j in range(ROWT):
                    t = ROWT * b + j
                    last = dve.scalar_tensor_tensor(x_res[:, t, :], bank[6 + j][:], rscale[:, j:j + 1], x_res[:, t, :],
                                                    ALU.mult, ALU.add)
                last.then_inc(a_resid, 1)

            dve.wait_ge(a_bias, 1)
            dve.wait_ge(a_valid, 1)
            normalise0(0)
            normalise0(1)
            mask_and_max(0)
            normalise0(2)
            with dve.Fori(1, BATCH - 2) as b:
                inverse_sums(b - 1)
                mask_and_max(b)
                normalise0(b + 2)
                add_readout(b - 1)
            inverse_sums(BATCH - 3)
            mask_and_max(BATCH - 2)
            add_readout(BATCH - 3)
            inverse_sums(BATCH - 2)
            mask_and_max(BATCH - 1)
            add_readout(BATCH - 2)
            inverse_sums(BATCH - 1)
            add_readout(BATCH - 1)

            def quantise(i, slot, lap):
                dve.wait_ge(raw_loaded[slot], 48 * lap + 48)
                dve.wait_ge(w_quant, room(w_quant, i))
                dve.tensor_scalar(expo[:].bitcast(U32), raw[:, slot, :].bitcast(U32), 0x7F800000, None,
                                  ALU.bitwise_and).then_inc(w_expo, 1)
                dve.wait_ge(w_expo, i + 1)
                dve.tensor_scalar(expo[:], expo[:], 2.0 ** -6, 1.5 * 2.0 ** 20, ALU.max, ALU.mult).then_inc(w_magic, 1)
                dve.wait_ge(w_magic, i + 1)
                dve.tensor_tensor(raw[:, slot, :], raw[:, slot, :], expo[:], ALU.add).then_inc(w_sum, 1)
                dve.wait_ge(w_sum, i + 1)
                dve.tensor_tensor(wq[:, i, :], raw[:, slot, :], expo[:], ALU.subtract).then_inc(w_quant, 1)

            with dve.Fori(0, FC // RAW) as lap:
                for slot in range(RAW):
                    quantise(lap * RAW + slot, slot, lap)

            def normalise(g, s):
                if s is nb:
                    dve.wait_ge(a_resid, done(a_resid, BATCH - 1))
                for i in range(GT):
                    dve.bn_stats(stats[:, i, :], x_res[:, GT * g + i, :]).then_inc(s["stats"], 1)
                hold(dve, s["stats"], GT * g + GT)
                for i in range(GT):
                    last = dve.bn_aggr(meanvar[:, i, :], stats[:, i, :])
                last.then_inc(s["meanvar"], 1)
                dve.wait_ge(s["rstd"], g + 1)
                dve.wait_ge(s["xT_psum"], room(s["xT_psum"], g))
                for i in range(GT):
                    last = dve.tensor_scalar(xn[:, i, :], x_res[:, GT * g + i, :], meanvar[:, i, 0:1],
                                             rstd[:, i:i + 1], ALU.subtract, ALU.mult)
                last.then_inc(s["xn"], 1)

            def split_lo(g, s):
                dve.wait_ge(s["hi"], g + 1)
                for i in range(GT):
                    at = bass.ds((GT * g + i) * P, P)
                    last = dve.tensor_tensor(xT_lo[:, :, at], pair[i // 2][:, i % 2, :].rearrange("p (k c) -> p k c", c=P),
                                             xT_hi[:, :, at], ALU.subtract)
                last.then_inc(s["lo"], 1)

            normalise(0, nb)
            with dve.Fori(0, GROUPS - 1) as g:
                split_lo(g, nb)
                normalise(g + 1, nb)
            split_lo(GROUPS - 1, nb)

            dve.wait_ge(scales_loaded, 48)

            def product(g, c):
                n = g * FC + c
                dve.wait_ge(b_silu, n + 1)
                dve.wait_ge(b_up_ps, n + 1)
                dve.wait_ge(b_fhi, room(b_fhi, n))
                dve.scalar_tensor_tensor(fused[:, c % 2, :], bank[2 + c % 2][:], uscale[:, c:c + 1], silu[:, c % 2, :],
                                         ALU.mult, ALU.mult).then_inc(b_fused, 1)

            def fused_lo(g, c):
                n = g * FC + c
                dve.wait_ge(b_fhi, done(b_fhi, n))
                dve.tensor_tensor(fT_lo[:, c % FR, :], fused[:, c % 2, :], fT_hi[:, c % FR, :],
                                  ALU.subtract).then_inc(b_flo, 1)

            def add_down(g):
                dve.wait_ge(b_down, done(b_down, FC * g + FC - 1))
                for i in range(GT):
                    t = GT * g + i
                    dve.tensor_tensor(down[:, i % 2, :], bank[4 + i][:], dscale[:], ALU.mult).then_inc(b_scaled, 1)
                    dve.wait_ge(b_scaled, done(b_scaled, GT * g + i))
                    dve.tensor_tensor(x_res[:, t, :], x_res[:, t, :], down[:, i % 2, :], ALU.add).then_inc(b_resid, 1)

            with dve.Fori(0, GROUPS) as g:
                for c in range(FC):
                    product(g, c)
                    if c:
                        fused_lo(g, c - 1)
                fused_lo(g, FC - 1)
                add_down(g)

            dve.wait_ge(b_resid, TILES)
            normalise(0, nr)
            with dve.Fori(0, GROUPS - 1) as g:
                split_lo(g, nr)
                normalise(g + 1, nr)
            split_lo(GROUPS - 1, nr)
            dve.wait_ge(c_hi, 3)
            dve.scalar_tensor_tensor(wh_lo[:], wh_f32[:], WS, wh_hi[:], ALU.mult, ALU.subtract).then_inc(c_lo, 1)
            for i in range(2):
                dve.scalar_tensor_tensor(wgo_lo[:, i], wgo_f32[:, i], WS, wgo_hi[:, i], ALU.mult, ALU.subtract).then_inc(c_lo, 1)

            oT = ctxT[:].rearrange("p h (b j e) -> p h b j e", j=ROWT, e=P)
            dve.wait_ge(c_ones, 1)
            with dve.Fori(0, HEADS) as h:
                dve.wait_ge(c_scores, done(c_scores, h))
                dve.tensor_tensor(scaled[:, 0:SEQ], bank[4][:, 0:SEQ], decay[:, 0, h, :], ALU.mult)
                dve.tensor_tensor(scaled[:, SEQ:], bank[5][:, 0:P], decay[:, 1, h, P:SEQ], ALU.mult).then_inc(c_masked, 1)
                dve.wait_ge(c_masked, done(c_masked, h))
                dve.wait_ge(c_o_ps, room(c_o_ps, 4 * h + 3))
                dve.tensor_scalar(floored[:], scaled[:], -1.0, 1.0, ALU.mult, ALU.max).then_inc(c_scaled, 1)
                dve.wait_ge(c_scaled, h + 1)
                dve.tensor_tensor(weightT[:, 0, :], floored[:, 0:SEQ], scaled[:, 0:SEQ], ALU.max)
                dve.tensor_tensor(weightT[:, 1, P:SEQ], floored[:, SEQ:], scaled[:, SEQ:], ALU.max).then_inc(c_weights, 1)
                for j in range(ROWT):
                    for half in range(2):
                        o = 2 * j + half
                        dve.wait_ge(c_o_ps, done(c_o_ps, 4 * h + o))
                        dve.tensor_copy(oT[:, h, 4 * half:4 * half + 4, j, :],
                                        bank[6 + half][:].rearrange("p (b e) -> p b e", e=P)).then_inc(c_o_copied, 1)

            o_tile = ctxT[:].rearrange("p h (t e) -> p t h e", e=P)

            def group_stats(t):
                dve.bn_stats(gn_stats[:], o_tile[:, t]).then_inc(g_stats, 1)
                hold(dve, g_stats, t + 1)
                dve.bn_aggr(gn_meanvar[:], gn_stats[:]).then_inc(g_meanvar, 1)
                dve.wait_ge(g_meanvar, t + 1)
                dve.tensor_copy(gn_mean[:, bass.ds(t, 1)], gn_meanvar[:, 0:1])
                dve.tensor_scalar(gn_vareps[:, bass.ds(t, 1)], gn_meanvar[:, 1:2], GN_EPS, None, ALU.add).then_inc(g_vareps, 1)

            def group_normalise(t):
                dve.wait_ge(g_rstd, t + 1)
                dve.wait_ge(g_ygamma, room(g_ygamma, t))
                dve.tensor_scalar(y_norm[:].rearrange("p (h e) -> p h e", e=P), o_tile[:, t], gn_mean[:, bass.ds(t, 1)],
                                  gn_rstd[:, bass.ds(t, 1)], ALU.subtract, ALU.mult).then_inc(g_ynorm, 1)

            def gate_product(t):
                dve.wait_ge(g_w, done(g_w, t))
                dve.wait_ge(g_y, t + 1)
                dve.wait_ge(g_zT_ps, room(g_zT_ps, t))
                dve.tensor_tensor(z[:], w_relu[:], y[:], ALU.mult).then_inc(g_z, 1)

            def split_z_lo(t):
                dve.wait_ge(g_hi, t + 1)
                dve.tensor_tensor(zT_lo[:].rearrange("p k c -> p (k c)"), bank[1][:], zT_hi[:].rearrange("p k c -> p (k c)"),
                                  ALU.subtract).then_inc(g_lo, 1)

            def add_output(t):
                dve.wait_ge(g_wo, done(g_wo, t))
                dve.scalar_tensor_tensor(x_res[:, t, :], bank[2][:], 1.0 / WS, x_res[:, t, :], ALU.mult, ALU.add).then_inc(g_resid, 1)

            dve.wait_ge(c_o_copied, done(c_o_copied, 4 * HEADS - 1))
            group_stats(0)
            group_stats(1)
            group_normalise(0)
            gate_product(0)
            group_stats(2)
            group_normalise(1)
            split_z_lo(0)
            with dve.Fori(1, TILES - 2) as t:
                gate_product(t)
                group_stats(t + 2)
                group_normalise(t + 1)
                split_z_lo(t)
                add_output(t - 1)
            gate_product(TILES - 2)
            group_normalise(TILES - 1)
            split_z_lo(TILES - 2)
            add_output(TILES - 3)
            gate_product(TILES - 1)
            split_z_lo(TILES - 1)
            add_output(TILES - 2)
            add_output(TILES - 1)

            dve.wait_ge(g_resid, done(g_resid, TILES - 1))
            normalise(0, nd)
            with dve.Fori(0, GROUPS - 1) as g:
                split_lo(g, nd)
                normalise(g + 1, nd)
            split_lo(GROUPS - 1, nd)
            for n, (src, hi, lo) in enumerate(sw_units()):
                dve.wait_ge(d_sw_hi, n + 1)
                dve.scalar_tensor_tensor(lo, src, WS, hi, ALU.mult, ALU.subtract).then_inc(d_sw_lo, 1)

            steps = [0]

            def route(instruction):
                instruction.then_inc(d_route, 1)
                steps[0] += 1
                dve.wait_ge(d_route, steps[0])

            per_tile = [P, TILES, EXPERTS]
            square = [P, TILES, EXPERTS, EXPERTS]
            dve.wait_ge(d_logits, 1)
            logits = bank[4][:, 0:NR].rearrange("p (t e) -> p t e", e=EXPERTS)
            dve.wait_ge(d_lower, 1)
            route(dve.tensor_scalar(rank[:], logits, 1.0 / WS, None, ALU.mult))
            dve.tensor_reduce(prob_max[:], rank[:], AX.X, ALU.max).then_inc(d_weights, 1)
            dve.wait_ge(d_weights, 1)
            route(dve.tensor_tensor(prob[:], rank[:], prob_max[:].unsqueeze(2).broadcast_to(per_tile), ALU.subtract))
            dve.wait_ge(d_exp, 1)
            route(dve.tensor_reduce(prob_sum[:], prob[:], AX.X, ALU.add))
            route(dve.reciprocal(prob_max[:], prob_sum[:]))
            route(dve.tensor_tensor(prob[:], prob[:], prob_max[:].unsqueeze(2).broadcast_to(per_tile), ALU.mult))
            own, other = prob[:].unsqueeze(3).broadcast_to(square), prob[:].unsqueeze(2).broadcast_to(square)
            route(dve.tensor_tensor(above[:], other, own, ALU.is_gt))
            route(dve.tensor_tensor(tied[:], other, own, ALU.is_equal))
            route(dve.tensor_tensor(tied[:], tied[:], lower[:].unsqueeze(1).broadcast_to(square), ALU.mult))
            route(dve.tensor_tensor(above[:], above[:], tied[:], ALU.add))
            route(dve.tensor_reduce(rank[:], above[:], AX.X, ALU.add))
            route(dve.scalar_tensor_tensor(prob[:], rank[:], 1.5, prob[:], ALU.is_lt, ALU.mult))
            route(dve.tensor_reduce(prob_sum[:], prob[:], AX.X, ALU.add))
            route(dve.tensor_scalar(prob_sum[:], prob_sum[:], 1e-20, WS, ALU.add, ALU.mult))
            route(dve.reciprocal(prob_max[:], prob_sum[:]))
            dve.tensor_tensor(expert_w[:], prob[:], prob_max[:].unsqueeze(2).broadcast_to(per_tile), ALU.mult).then_inc(d_weights, 1)
            dve.wait_ge(d_weights, 2)

            def expert_lo(e, slot):
                dve.wait_ge(d_whi, e + 1)
                dve.scalar_tensor_tensor(w1_lo[slot][:], w1_f32[:], WS, w1_hi[slot][:], ALU.mult, ALU.subtract)
                dve.scalar_tensor_tensor(w2_lo[slot][:, 0:2], w2_f32[:, 0:2], WS, w2_hi[slot][:, 0:2], ALU.mult, ALU.subtract)
                dve.scalar_tensor_tensor(w2_lo[slot][0:HC[2], 2], w2_f32[0:HC[2], 2], WS, w2_hi[slot][0:HC[2], 2],
                                         ALU.mult, ALU.subtract).then_inc(d_wlo, 1)

            def expert_dve(m, mod):
                for c in range(4):
                    if c < 3:
                        rows, q, r = HC[c], m * 3 + c, (mod + c) % 2
                        dve.wait_ge(d_silu, q + 1)
                        dve.wait_ge(d_up_ps, q + 1)
                        dve.wait_ge(d_hlo, room(d_hlo, q))
                        dve.scalar_tensor_tensor(hp[0:rows, r, :], bank[2 + r][0:rows, :], 1.0 / WS, hg[0:rows, r, :],
                                                 ALU.mult, ALU.mult).then_inc(d_prod, 1)
                    if c:
                        rows, q, r = HC[c - 1], m * 3 + c - 1, (mod + c - 1) % 2
                        dve.wait_ge(d_hhi, done(d_hhi, q))
                        dve.tensor_tensor(hT_lo[0:rows, mod % 2, c - 1, :], hp[0:rows, r, :],
                                          hT_hi[0:rows, mod % 2, c - 1, :], ALU.subtract).then_inc(d_hlo, 1)

            def expert_add(m, mod, e):
                for i in range(GT):
                    t = mod * GT + i
                    dve.wait_ge(d_y_ps, done(d_y_ps, m * GT + i))
                    scale = 1.0 / WS if e is None else expert_w[:, t, bass.ds(e, 1)]
                    dve.scalar_tensor_tensor(x_res[:, t, :], bank[4 + i][:], scale, x_res[:, t, :],
                                             ALU.mult, ALU.add).then_inc(d_acc, 1)

            expert_dve(0, 0)
            for grp in range(1, GROUPS):
                expert_dve(grp, grp)
                expert_add(grp - 1, grp - 1, None)
                if grp == 1:
                    expert_lo(0, 1)
            expert_dve(GROUPS, 0)
            expert_add(GROUPS - 1, GROUPS - 1, None)
            expert_dve(GROUPS + 1, 1)
            expert_add(GROUPS, 0, 0)
            expert_lo(1, 0)
            with dve.Fori(0, EXPERTS // 2 - 1) as pair_i:
                for u in range(2, 2 + 2 * GROUPS):
                    m = pair_i * (2 * GROUPS) + (GROUPS + u)
                    expert_dve(m, u % GROUPS)
                    expert_add(m - 1, (u - 1) % GROUPS, pair_i * 2 + (u - 1) // GROUPS)
                    if u == GROUPS + 1:
                        expert_lo(pair_i * 2 + 2, 1)
                    if u == 2 * GROUPS + 1:
                        expert_lo(pair_i * 2 + 3, 0)
            for u in range(2, 2 * GROUPS):
                m = (EXPERTS - 1) * GROUPS + u
                expert_dve(m, u % GROUPS)
                expert_add(m - 1, (u - 1) % GROUPS, EXPERTS - 2 + (u - 1) // GROUPS)
            expert_add((EXPERTS + 1) * GROUPS - 1, GROUPS - 1, EXPERTS - 1)


INPUTS = ["x", "ctx_2048", "mask_BxS2_bk0", "L0_ffn_gate_w", "L0_ffn_up_w", "L0_ffn_down_w", "L0_ffn_gate_scale",
          "L0_ffn_up_scale", "L0_ffn_down_scale", "L1_xattn_Wh", "L1_xattn_wg_w", "L1_xattn_wo_w",
          "L1_xattn_gn_gamma", "L1_xattn_gn_beta", "L1_ffn_gate_w", "L1_ffn_w1", "L1_ffn_w2", "L1_ffn_sw1",
          "L1_ffn_sw2", "L1_ffn_sw3"]


def decay_table(heads, seq, head_dim):
    import numpy as np
    gam = (1.0 - 2.0 ** (-5.0 - np.arange(heads, dtype=np.float32))).astype(np.float32)
    idx = np.arange(seq, dtype=np.float32)
    expo = idx[None, :] - idx[:, None]
    d = np.where(expo[None] <= 0, gam[:, None, None].astype(np.float64) ** np.minimum(expo, 0)[None], 0.0)
    d = d / np.sqrt(d.sum(axis=-1))[:, None, :] / np.sqrt(float(head_dim))
    return np.ascontiguousarray(d.transpose(2, 0, 1).astype(np.float32))


def kernel(**inputs):
    import numpy as np
    import concourse.bacc as bacc
    from concourse import mybir as mb
    from concourse.bass_utils import run_bass_kernel_spmd

    nc = bacc.Bacc("TRN2", target_bir_lowering=False, num_devices=1)
    arrays, args = {}, []
    for name in INPUTS:
        a = np.ascontiguousarray(inputs[name])
        arrays["in_" + name] = a
        args.append(nc.dram_tensor("in_" + name, a.shape, mb.dt.from_np(a.dtype), kind="ExternalInput").ap())
    heads, head_dim = inputs["L1_xattn_Wh"].shape[:2]
    decay = decay_table(heads, inputs["x"].shape[1], head_dim)
    arrays["in_decay"] = decay
    args.append(nc.dram_tensor("in_decay", decay.shape, mb.dt.float32, kind="ExternalInput").ap())
    out = nc.dram_tensor("out_0", inputs["x"].shape, mb.dt.float32, kind="ExternalOutput").ap()
    build_decoder_pair(nc, *args, out)
    r = run_bass_kernel_spmd(nc, [arrays], core_ids=[0])
    return r.results[0]["out_0"]
```

```python
import concourse.bass as bass
from concourse import mybir
from contextlib import ExitStack


def build_decoder_pair(nc, x_in, ctx_in, mask_in, l0_gate, l0_up, l0_down, l0_gscale, l0_uscale, l0_dscale,
                       wh_in, wg_in, wo_in, gamma_in, beta_in, router_in, w1_in, w2_in, sw1_in, sw2_in, sw3_in,
                       decay_in, out):
    F32, F16 = mybir.dt.float32, mybir.dt.float16
    U8, U32, I32 = mybir.dt.uint8, mybir.dt.uint32, mybir.dt.int32
    ALU, ACT, AX = mybir.AluOpType, mybir.ActivationFunctionType, mybir.AxisListType

    P = 128
    BATCH, SEQ, DIM = x_in.shape
    CTX = ctx_in.shape[1]
    ROWT = SEQ // P
    TILES = BATCH * ROWT
    TOK = BATCH * SEQ
    KC = DIM // P
    GT = 4
    GW = GT * P
    GROUPS = TILES // GT
    FFN = l0_gate.shape[1]
    FC = FFN // P
    QW = 3 * DIM
    SCALE = float(DIM) ** -0.5
    LN_EPS = 1e-5
    HEADS = wh_in.shape[0]
    GN_EPS = 1e-3
    EXPERTS = w1_in.shape[0]
    HID = w2_in.shape[1]
    HC = [P, P, HID - 2 * P]
    UNIT = 2 * HID + 3 * P
    BLOCK = KC * 2 * UNIT
    TOP_K = 2
    SLOTS = (TOK * TOP_K + EXPERTS * (P - 1)) // P
    WS = 32.0
    MASKED = -1e32

    ctx_stack = ExitStack()
    with ctx_stack as top:
        def sb(scope, name, shape, dt):
            return scope.enter_context(nc.sbuf_tensor(name, shape, dt))

        free_at_start = {}

        def sem(name, free=0):
            s = top.enter_context(nc.semaphore(name))
            free_at_start[name] = (s, free)
            return s

        def done(s, n):
            return n + 1 + next(free for t, free in free_at_start.values() if t is s)

        def room(s, n):
            return n + 1

        ident = sb(top, "ident", [P, P], F32)
        x_res = sb(top, "x_res", [P, TILES, DIM], F32)
        xn = sb(top, "xn", [P, GT, DIM], F32)
        stats = sb(top, "stats", [P, GT, 6], F32)
        meanvar = sb(top, "meanvar", [P, GT, 2], F32)
        vareps = sb(top, "vareps", [P, GT], F32)
        rstd = sb(top, "rstd", [P, GT], F32)
        zeros = sb(top, "zeros", [P, DIM], F32)
        minus_half = sb(top, "minus_half", [P, GT], F32)
        with ExitStack() as late:
            experts = sb(late, "experts", [P, EXPERTS, BLOCK], F16)
        with ExitStack() as late:
            xn_all = sb(late, "xn_all", [P, TILES, DIM], F32)
        ctxT = sb(top, "ctxT", [P, KC, TOK], F32)
        with ExitStack() as early:
            ctx_nat = sb(early, "ctx_nat", [P, TILES, DIM], F32)
        xT_hi = sb(top, "xT_hi", [P, KC, TOK], F16)
        xT_lo = sb(top, "xT_lo", [P, KC, TOK], F16)

        with ExitStack() as pairs:
            pair = [pairs.enter_context(nc.psum_tensor(f"pair{i}", [P, 2, 512], F32)) for i in range(4)]
        bank = [top.enter_context(nc.psum_tensor(f"bank{i}", [P, 512], F32)) for i in range(8)]

        ffn_w = ExitStack()
        RAW = 3
        raw = sb(ffn_w, "raw", [P, RAW, QW], F32)
        expo = sb(ffn_w, "expo", [P, QW], F32)
        wq = sb(ffn_w, "wq", [P, FC, QW], F16)
        gscale = sb(ffn_w, "gscale", [P, FC], F32)
        uscale = sb(ffn_w, "uscale", [P, FC], F32)
        dscale = sb(ffn_w, "dscale", [P, DIM], F32)

        att0 = ExitStack()
        ctx_stage = sb(att0, "ctx_stage", [P, ROWT, DIM], F32)
        xn0 = sb(att0, "xn0", [P, ROWT, DIM], F32)
        xnT0 = sb(att0, "xnT0", [P, KC, SEQ], F32)
        scores_sb = sb(att0, "scores_sb", [P, ROWT, CTX], F32)
        probs = sb(att0, "probs", [P, ROWT, CTX], F32)
        probsT = sb(att0, "probsT", [P, CTX // P, SEQ], F32)
        mask_u8 = sb(att0, "mask_u8", [P, BATCH, CTX], U8)
        maskbias = sb(att0, "maskbias", [P, BATCH, CTX], F32)
        valid = sb(att0, "valid", [P, BATCH], F32)
        rowmax = sb(att0, "rowmax", [P, ROWT], F32)
        negmax = sb(att0, "negmax", [P, ROWT], F32)
        rowsum = sb(att0, "rowsum", [P, ROWT], F32)
        rinv = sb(att0, "rinv", [P, ROWT], F32)
        rscale = sb(att0, "rscale", [P, ROWT], F32)
        att0.close()

        ffn = ExitStack()
        silu = sb(ffn, "silu", [P, 2, GW], F32)
        fused = sb(ffn, "fused", [P, 2, GW], F32)
        FR = 3
        fT_hi = sb(ffn, "fT_hi", [P, FR, GW], F16)
        fT_lo = sb(ffn, "fT_lo", [P, FR, GW], F16)
        down = sb(ffn, "down", [P, 2, DIM], F32)
        unit_f32 = sb(ffn, "unit_f32", [P, 2, UNIT], F32)
        unit_split = sb(ffn, "unit_split", [P, 2, 2, UNIT], F16)
        ffn.close()
        ffn_w.close()

        ret = ExitStack()
        wh_f32 = sb(ret, "wh_f32", [P, HEADS, P], F32)
        wh_head = sb(ret, "wh_head", [P, P], F32)
        wh_hi = sb(ret, "wh_hi", [P, HEADS, P], F16)
        wh_lo = sb(ret, "wh_lo", [P, HEADS, P], F16)
        wgo_f32 = sb(ret, "wgo_f32", [P, 2, KC, DIM], F32)
        wgo_hi = sb(ret, "wgo_hi", [P, 2, KC, DIM], F16)
        wgo_lo = sb(ret, "wgo_lo", [P, 2, KC, DIM], F16)
        decay = sb(ret, "decay", [P, ROWT, HEADS, SEQ], F32)
        gamma = sb(ret, "gamma", [P, DIM], F32)
        beta = sb(ret, "beta", [P, DIM], F32)
        qT = sb(ret, "qT", [P, TOK], F32)
        kT = sb(ret, "kT", [P, TOK], F32)
        v = sb(ret, "v", [P, TILES, P], F32)
        scaled = sb(ret, "scaled", [P, SEQ + P], F32)
        floored = sb(ret, "floored", [P, SEQ + P], F32)
        weightT = sb(ret, "weightT", [P, ROWT, SEQ], F32)
        gn_stats = sb(ret, "gn_stats", [P, 6], F32)
        gn_meanvar = sb(ret, "gn_meanvar", [P, 2], F32)
        gn_mean = sb(ret, "gn_mean", [P, TILES], F32)
        gn_vareps = sb(ret, "gn_vareps", [P, TILES], F32)
        gn_rstd = sb(ret, "gn_rstd", [P, TILES], F32)
        y_norm = sb(ret, "y_norm", [P, DIM], F32)
        y_gamma = sb(ret, "y_gamma", [P, DIM], F32)
        y = sb(ret, "y", [P, DIM], F32)
        w_relu = sb(ret, "w_relu", [P, DIM], F32)
        z = sb(ret, "z", [P, DIM], F32)
        zT_hi = sb(ret, "zT_hi", [P, KC, P], F16)
        zT_lo = sb(ret, "zT_lo", [P, KC, P], F16)
        ret.close()

        shared = ExitStack()
        sw_split = sb(shared, "sw_split", [P, KC, 2, UNIT], F16)
        hg = sb(shared, "hg", [P, 2, GW], F32)
        hp = sb(shared, "hp", [P, 2, GW], F32)
        hT_hi = sb(shared, "hT_hi", [P, 2, len(HC), GW], F16)
        hT_lo = sb(shared, "hT_lo", [P, 2, len(HC), GW], F16)
        shared.close()
        moe = ExitStack()
        sb(moe, "experts_room", [P, (EXPERTS * BLOCK - 4 * KC * TOK) // 2], F32)
        prob = sb(moe, "prob", [P, TILES, EXPERTS], F32)
        prob_max = sb(moe, "prob_max", [P, TILES], F32)
        prob_sum = sb(moe, "prob_sum", [P, TILES], F32)
        above = xn[:, 0:2, :].rearrange("p a (b e j) -> p (a b) e j", e=EXPERTS, j=EXPERTS)
        tied = xn[:, 2:4, :].rearrange("p a (b e j) -> p (a b) e j", e=EXPERTS, j=EXPERTS)
        lower = sb(moe, "lower", [P, EXPERTS, EXPERTS], F32)
        rank = sb(moe, "rank", [P, TILES, EXPERTS], F32)
        expert_w = sb(moe, "expert_w", [P, TILES, EXPERTS], F32)
        chosen = sb(moe, "chosen", [P, TILES * EXPERTS], F16)
        before = sb(moe, "before", [P, P], F16)
        ones16 = sb(moe, "ones16", [P, P], F16)
        tiles_of = sb(moe, "tiles_of", [P, EXPERTS], F32)
        tiles_low = sb(moe, "tiles_low", [P, EXPERTS, EXPERTS], F32)
        first_tile = sb(moe, "first_tile", [P, EXPERTS], F32)
        end_tile = sb(moe, "end_tile", [P, EXPERTS], F32)
        position = sb(moe, "position", [P, TILES, EXPERTS], F32)
        picked = sb(moe, "picked", [P, 2 * TOP_K, TILES, EXPERTS], F32)
        slot_f32 = sb(moe, "slot_f32", [P, 2 * TOP_K, TILES], F32)
        slot_u32 = sb(moe, "slot_u32", [P, TOP_K * TILES], U32)
        tile_no = sb(moe, "tile_no", [1, SLOTS], F32)
        tile_past = sb(moe, "tile_past", [1, SLOTS, EXPERTS], F32)
        tile_expert = sb(moe, "tile_expert", [1, SLOTS], F32)
        tile_expert_i = sb(moe, "tile_expert_i", [1, 2, SLOTS], I32)
        router_hi = sb(moe, "router_hi", [P, KC, EXPERTS], F16)
        router_lo = sb(moe, "router_lo", [P, KC, EXPERTS], F16)
        moe_in = ExitStack()
        sw12_f32 = sb(moe_in, "sw12_f32", [P, 2, len(HC), DIM], F32)
        sw3_f32 = sb(moe_in, "sw3_f32", [P, KC, HID], F32)
        router_f32 = sb(moe_in, "router_f32", [EXPERTS, DIM], F32)
        moe_in.close()
        XR = 3
        xg = sb(moe, "xg", [P, XR, DIM], F32)
        xgT_hi = sb(moe, "xgT_hi", [P, KC, P], F16)
        xgT_lo = sb(moe, "xgT_lo", [P, KC, P], F16)
        tg = sb(moe, "tg", [P, HID], F32)
        th = sb(moe, "th", [P, 3 * P], F32)
        thT_hi = sb(moe, "thT_hi", [P, 3, P], F16)
        thT_lo = sb(moe, "thT_lo", [P, 3, P], F16)
        ty = sb(moe, "ty", [P, XR, DIM], F32)
        YR = 4
        yg = xn
        moe.close()
        split_w = nc.dram_tensor("split_w", (EXPERTS, KC, P, 2 * UNIT), F16).ap()
        sorted_x = nc.dram_tensor("sorted_x", (SLOTS * P, DIM), F32).ap()
        sorted_y = nc.dram_tensor("sorted_y", (SLOTS * P, DIM), F32).ap()

        ident_zero, ident_ready = sem("ident_zero"), sem("ident_ready")
        half_ready = sem("half_ready")
        mask_loaded = sem("mask_loaded")
        loads = [sem(f"loads{i}") for i in range(max(BATCH, EXPERTS))]
        batches_loaded = sem("batches_loaded")
        a_stats, a_meanvar, a_vareps, a_rstd, a_xn = (sem("a_" + n) for n in ("stats", "meanvar", "vareps", "rstd", "xn"))
        a_xnT_psum, a_ctxT_psum, a_xnT, a_ctxT = (sem("a_" + n, 1) for n in ("xnT_psum", "ctxT_psum", "xnT", "ctxT"))
        a_ctx_staged = sem("a_ctx_staged")
        a_bias, a_valid, a_rowmax, a_negmax, a_rscale = (
            sem("a_" + n) for n in ("bias", "valid", "rowmax", "negmax", "rscale"))
        a_scores, a_masked, a_probs, a_probsT_psum, a_probsT, a_readout, a_rinv, a_resid = (
            sem("a_" + n, 1) for n in ("scores", "masked", "probs", "probsT_psum", "probsT", "readout", "rinv", "resid"))
        out_stored = sem("out_stored")
        weights_loaded, c_hi, c_lo = sem("weights_loaded"), sem("c_hi"), sem("c_lo")
        c_head = sem("c_head")
        c_proj, c_copied = sem("c_proj"), sem("c_copied", 4)
        c_scores, c_masked, c_scaled, c_weights = sem("c_scores", 1), sem("c_masked", 1), sem("c_scaled"), sem("c_weights")
        c_o_ps, c_o_copied = sem("c_o_ps", 4), sem("c_o_copied", 2)
        g_stats, g_meanvar, g_vareps, g_rstd = (sem("g_" + n) for n in ("stats", "meanvar", "vareps", "rstd"))
        g_w_ps, g_w, g_ynorm, g_ygamma, g_y = (sem("g_" + n, free) for n, free in (
            ("w_ps", 0), ("w", 1), ("ynorm", 0), ("ygamma", 1), ("y", 0)))
        g_z, g_zT_ps, g_hi, g_lo, g_wo, g_resid = (
            sem("g_z", 1), sem("g_zT_ps", 1), sem("g_hi"), sem("g_lo", 1), sem("g_wo", 1), sem("g_resid", 1))

        def norm_sems(t):
            return {n: sem(f"{t}_{n}", free) for n, free in (("stats", 0), ("meanvar", 0), ("vareps", 0), ("rstd", 0),
                                                             ("xn", 0), ("xT_psum", 1), ("hi", 0), ("lo", 1))}
        nb = norm_sems("b")
        nr = norm_sems("r")
        nd = norm_sems("d")
        u_loaded, u_stored = [sem(f"u_loaded{i}") for i in range(2)], [sem(f"u_stored{i}", 16) for i in range(2)]
        u_hi, u_lo = sem("u_hi"), sem("u_lo", 2)
        filled, d_filled = sem("filled"), sem("d_filled")
        d_sw_ps, d_sw_hi, d_sw_lo = sem("d_sw_ps"), sem("d_sw_hi"), sem("d_sw_lo", 4)
        d_ones, d_const = sem("d_ones"), sem("d_const")
        d_logits, d_route, d_exp, d_weights = (sem("d_" + n) for n in ("logits", "route", "exp", "weights"))
        d_place = sem("d_place")
        d_chosen, d_counts, d_slots, d_tile_expert = (sem("d_" + n) for n in ("chosen", "counts", "slots", "tile_expert"))
        d_scattered = sem("d_scattered")
        d_gate_ps, d_up_ps, d_silu = (sem("d_" + n) for n in ("gate_ps", "up_ps", "silu"))
        d_prod, d_hhi, d_hlo = sem("d_prod", 2), sem("d_hhi"), sem("d_hlo", 2)
        d_y_ps, d_acc = sem("d_y_ps", 2 * GT), sem("d_acc", GT)
        experts_loaded = sem("experts_loaded")
        t_y_stored = [sem(f"t_y_stored{i}", 16) for i in range(3)]
        t_xT, t_xhi, t_xlo, t_gu, t_silu = sem("t_xT"), sem("t_xhi"), sem("t_xlo", 1), sem("t_gu"), sem("t_silu")
        t_h, t_hT, t_hhi, t_hlo = sem("t_h", 1), sem("t_hT", 1), sem("t_hhi"), sem("t_hlo", 1)
        t_y, t_ycopy = sem("t_y"), sem("t_ycopy", 1)
        y_gathered = [sem(f"y_gathered{i}") for i in range(4)]
        y_added = sem("y_added")

        ring_loaded = [sem(f"ring_loaded{i}") for i in range(RAW)]
        scales_loaded = sem("scales_loaded")
        w_step = sem("w_step")
        w_quant = sem("w_quant", 1)
        b_gate_ps, b_up_ps, b_silu, b_flo, b_resid = (sem("b_" + n) for n in ("gate_ps", "up_ps", "silu", "flo", "resid"))
        b_fused, b_fhi, b_down = sem("b_fused", 2), sem("b_fhi", 2), sem("b_down", FR)
        b_scaled = sem("b_scaled", GT)

        def gate_chunk(i):
            return l0_gate.rearrange("(k p) f -> p k f", p=P)[:, :, i * P:(i + 1) * P]

        def up_chunk(i):
            return l0_up.rearrange("(k p) f -> p k f", p=P)[:, :, i * P:(i + 1) * P]

        waits_passed = sem("waits_passed")

        def hold(engine, semaphore, value):
            engine.wait_ge(semaphore, value)
            engine.sem_inc(waits_passed, 1)

        def sw_units():
            for t in range(2):
                for k in range(KC):
                    at = slice(t * HID, (t + 1) * HID)
                    yield bank[(t * KC + k) % 4][:, 0:HID], sw_split[:, k, 0, at], sw_split[:, k, 1, at]
            for c, rows in enumerate(HC):
                at = slice(2 * HID + c * P, 2 * HID + (c + 1) * P)
                yield (bank[(2 * KC + c) % 4][0:rows, :].rearrange("r (k n) -> r k n", n=P),
                       sw_split[0:rows, :, 0, at], sw_split[0:rows, :, 1, at])
            yield (bank[(2 * KC + len(HC)) % 4][:, 0:KC * EXPERTS].rearrange("p (k e) -> p k e", e=EXPERTS),
                   router_hi[:], router_lo[:])

        block = top.enter_context(nc.Block())

        @block.sync
        def _(sp):
            for s, free in free_at_start.values():
                if free:
                    sp.sem_inc(s, free)
            xv = x_in.rearrange("b (j p) d -> b p j d", p=P)
            cv = ctx_in.rearrange("b (j p) d -> b p j d", p=P)
            sp.dma_start(mask_u8[:], mask_in.partition_broadcast(P)).then_inc(mask_loaded, 16)
            for b in range(BATCH):
                sp.dma_start(x_res[:, ROWT * b:ROWT * (b + 1), :], xv[b]).then_inc(loads[b], 16)
                sp.dma_start(ctx_nat[:, ROWT * b:ROWT * (b + 1), :], cv[b]).then_inc(loads[b], 16)
            sp.dma_start(gscale[:], l0_gscale.rearrange("(c p) -> p c", p=P),
                         allow_slow_non_contiguous=True).then_inc(scales_loaded, 16)
            sp.dma_start(uscale[:], l0_uscale.rearrange("(c p) -> p c", p=P),
                         allow_slow_non_contiguous=True).then_inc(scales_loaded, 16)
            sp.dma_start(dscale[:], l0_dscale.partition_broadcast(P)).then_inc(scales_loaded, 16)

            def load_raw(i):
                slot = i % RAW
                rv = raw[:, slot, 0:2 * DIM].rearrange("p (t k f) -> p t k f", t=2, f=P)
                sp.dma_start(rv[:, 0], gate_chunk(i)).then_inc(ring_loaded[slot], 16)
                sp.dma_start(rv[:, 1], up_chunk(i)).then_inc(ring_loaded[slot], 16)
                sp.dma_start(raw[:, slot, 2 * DIM:QW], l0_down[i * P:(i + 1) * P, :]).then_inc(ring_loaded[slot], 16)
            for i in range(RAW):
                load_raw(i)

            def store_unit(e2, u):
                slot, k = u % 2, u % KC
                sp.wait_ge(u_lo, done(u_lo, e2 * 8 + u))
                dst = split_w.rearrange("(a b) k p u -> b k p a u", b=2)[u // KC, k, :, e2]
                sp.dma_start(dst, unit_split[:, slot].rearrange("p s u -> p (s u)")).then_inc(u_stored[slot], 16)
            sp.wait_ge(filled, 1)
            for i in range(3):
                n = SLOTS // 3
                sp.dma_start(sorted_x[i * n * P:(i + 1) * n * P, :].rearrange("(a p) d -> p a d", p=P),
                             zeros[:].unsqueeze(1).broadcast_to([P, n, DIM])).then_inc(d_filled, 16)
            for b in range(BATCH):
                sp.wait_ge(loads[b], 32)
                sp.sem_inc(batches_loaded, 1)
            for i in range(RAW, FC):
                sp.wait_ge(w_quant, done(w_quant, i - RAW))
                load_raw(i)
            ov = out.rearrange("b (j p) d -> p (b j) d", p=P)
            sp.wait_ge(filled, 2)
            with sp.Fori(0, EXPERTS * KC // 8) as e2:
                for u in range(8):
                    slot, k = u % 2, u % KC
                    sp.wait_ge(u_lo, room(u_lo, e2 * 8 + u))
                    w1e = w1_in.rearrange("(a b) (k p) f -> p b k a f", b=2, p=P)[:, u // KC, k, e2]
                    w2e = w2_in.rearrange("(a b) i n -> b i a n", b=2)[u // KC, :, e2, k * P:(k + 1) * P]
                    sp.dma_start(unit_f32[:, slot, 0:2 * HID], w1e).then_inc(u_loaded[slot], 16)
                    sp.dma_start(unit_f32[:, slot, 2 * HID:2 * HID + 2 * P].rearrange("p (c n) -> p c n", n=P),
                                 w2e[0:2 * P].rearrange("(c p) n -> p c n", p=P)).then_inc(u_loaded[slot], 16)
                    sp.dma_start(unit_f32[0:HC[2], slot, 2 * HID + 2 * P:UNIT], w2e[2 * P:HID]).then_inc(u_loaded[slot], 16)
                    if u:
                        store_unit(e2, u - 1)
                store_unit(e2, 7)
            sp.wait_ge(b_resid, TILES)
            sp.dma_start(wh_f32[:], wh_in.rearrange("h d e -> d h e")).then_inc(weights_loaded, 16)
            sp.dma_start(wgo_f32[:, 0], wg_in.rearrange("(k p) n -> p k n", p=P)).then_inc(weights_loaded, 16)
            sp.dma_start(wgo_f32[:, 1], wo_in.rearrange("(k p) n -> p k n", p=P)).then_inc(weights_loaded, 16)
            sp.dma_start(decay[:], decay_in.rearrange("(j p) h s -> p j h s", p=P)).then_inc(weights_loaded, 16)
            sp.dma_start(gamma[:], gamma_in.partition_broadcast(P)).then_inc(weights_loaded, 16)
            sp.dma_start(beta[:], beta_in.partition_broadcast(P)).then_inc(weights_loaded, 16)
            sp.wait_ge(g_resid, done(g_resid, TILES - 1))

            def hidden_rows(dst, src):
                sp.dma_start(dst[:, 0:2, :], src[0:2 * P, :].rearrange("(c p) n -> p c n", p=P)).then_inc(weights_loaded, 16)
                sp.dma_start(dst[0:HC[2], 2, :], src[2 * P:HID, :]).then_inc(weights_loaded, 16)
            sp.dma_start(router_f32[:], router_in).then_inc(weights_loaded, 16)
            hidden_rows(sw12_f32[:, 0], sw1_in)
            hidden_rows(sw12_f32[:, 1], sw2_in)
            sp.dma_start(sw3_f32[:], sw3_in.rearrange("(k p) n -> p k n", p=P)).then_inc(weights_loaded, 16)
            for i in range(2):
                sp.wait_ge(u_stored[i], 16 * (EXPERTS * KC // 2 + 1))
            for e in range(2):
                sp.dma_start(experts[:, EXPERTS - 1 - e, :].rearrange("p (k u) -> p k u", k=KC),
                             split_w[e].rearrange("k p u -> p k u")).then_inc(loads[e], 16)

            def load_tile(i, slot, lap):
                if lap is not None:
                    sp.wait_ge(t_xT, i - XR + 1)
                sp.dma_start(xg[:, slot, :], sorted_x[bass.ds(i * P, P), :]).then_inc(ring_loaded[slot], 16)

            def store_tile(i, slot):
                sp.wait_ge(t_ycopy, done(t_ycopy, i))
                sp.dma_start(sorted_y[bass.ds(i * P, P), :], ty[:, slot, :]).then_inc(t_y_stored[slot], 16)

            sp.wait_ge(d_scattered, 16 * TOP_K * TILES)
            sp.wait_ge(d_sw_lo, done(d_sw_lo, 11))
            for i in range(XR):
                load_tile(i, i, None)
            with sp.Fori(0, SLOTS // XR - 1) as lap:
                for slot in range(XR):
                    load_tile(lap * XR + (XR + slot), slot, lap)
                    store_tile(lap * XR + slot, slot)
            for slot in range(XR):
                store_tile(SLOTS - XR + slot, slot)
            ov = out.rearrange("b (j p) d -> p (b j) d", p=P)
            for t in range(TILES):
                sp.wait_ge(y_added, TOP_K * t + TOP_K)
                sp.dma_start(ov[:, t, :], x_res[:, t, :]).then_inc(out_stored, 16)
            sp.wait_ge(out_stored, 16 * TILES)

        @block.gpsimd
        def _(pool):
            pool.memset(ident[:], 0.0).then_inc(ident_zero, 1)
            pool.memset(minus_half[:], -0.5).then_inc(half_ready, 1)
            pool.memset(zeros[:], 0.0).then_inc(filled, 1)
            pool.wait_ge(ident_zero, 1)
            pool.affine_select(out=ident[:], in_=ident[:], compare_op=ALU.not_equal, fill=1.0, base=0,
                               pattern=[[-1, P]], channel_multiplier=1).then_inc(ident_ready, 1)
            pool.wait_ge(half_ready, 1)

            def inverse_deviation(n, s_meanvar, s_vareps, s_rstd, width):
                hold(pool, s_meanvar, n + 1)
                pool.tensor_scalar(vareps[:, 0:width], meanvar[:, 0:width, 1], LN_EPS, None, ALU.add).then_inc(s_vareps, 1)
                pool.wait_ge(s_vareps, n + 1)
                pool.tensor_tensor(rstd[:, 0:width], vareps[:, 0:width], minus_half[:, 0:width], ALU.pow).then_inc(s_rstd, 1)

            with pool.Fori(0, BATCH) as b:
                pool.wait_ge(batches_loaded, b + 1)
                pool.wait_ge(a_ctxT_psum, room(a_ctxT_psum, b))
                pool.tensor_copy(ctx_stage[:], ctx_nat[:, bass.ds(ROWT * b, ROWT), :]).then_inc(a_ctx_staged, 1)
                inverse_deviation(b, a_meanvar, a_vareps, a_rstd, ROWT)
            pool.wait_ge(a_resid, done(a_resid, BATCH - 1))
            pool.memset(unit_f32[:], 0.0).then_inc(filled, 1)
            with pool.Fori(0, GROUPS) as g:
                inverse_deviation(g, nb["meanvar"], nb["vareps"], nb["rstd"], GT)
            with pool.Fori(0, GROUPS) as g:
                inverse_deviation(g, nr["meanvar"], nr["vareps"], nr["rstd"], GT)
            pool.wait_ge(b_resid, TILES)
            pool.memset(weightT[:], 1.0).then_inc(filled, 1)
            pool.wait_ge(weights_loaded, 96)
            with pool.Fori(0, HEADS) as h:
                pool.wait_ge(c_scores, room(c_scores, h))
                pool.tensor_copy(wh_head[:], wh_f32[:, h, :]).then_inc(c_head, 1)

            def group_deviation(t):
                pool.wait_ge(g_vareps, t + 1)
                pool.tensor_tensor(gn_rstd[:, bass.ds(t, 1)], gn_vareps[:, bass.ds(t, 1)], minus_half[:, 0:1], ALU.pow).then_inc(g_rstd, 1)

            def gamma_beta(t):
                pool.wait_ge(g_ynorm, t + 1)
                pool.tensor_tensor(y_gamma[:], y_norm[:], gamma[:], ALU.mult).then_inc(g_ygamma, 1)
                pool.wait_ge(g_z, room(g_z, t))
                hold(pool, g_ygamma, done(g_ygamma, t))
                pool.tensor_tensor(y[:], y_gamma[:], beta[:], ALU.add).then_inc(g_y, 1)

            group_deviation(0)
            group_deviation(1)
            gamma_beta(0)
            with pool.Fori(0, TILES - 2) as t:
                group_deviation(t + 2)
                gamma_beta(t + 1)
            gamma_beta(TILES - 1)
            with pool.Fori(0, GROUPS) as g:
                inverse_deviation(g, nd["meanvar"], nd["vareps"], nd["rstd"], GT)
            pool.wait_ge(g_resid, done(g_resid, TILES - 1))
            pool.memset(lower[:], 1.0).then_inc(d_ones, 1)
            pool.memset(before[:], 1.0).then_inc(d_ones, 1)
            pool.wait_ge(d_ones, 2)
            pool.affine_select(out=lower[:], in_=lower[:], compare_op=ALU.is_gt, fill=0.0, base=0,
                               pattern=[[1, EXPERTS], [-1, EXPERTS]], channel_multiplier=0).then_inc(d_const, 1)
            pool.affine_select(out=before[:], in_=before[:], compare_op=ALU.is_gt, fill=0.0, base=0,
                               pattern=[[1, P]], channel_multiplier=-1).then_inc(d_const, 1)
            pool.memset(ones16[:], 1.0).then_inc(d_const, 1)
            pool.iota(tile_no[:], [[1, SLOTS]], base=0, channel_multiplier=0,
                      allow_small_or_imprecise_dtypes=True).then_inc(d_const, 1)

            pool.wait_ge(d_filled, 48)
            pool.wait_ge(d_slots, 1)
            for t in range(TILES):
                for c in range(TOP_K):
                    at = c * TILES + t
                    pool.indirect_dma_start(
                        sorted_x, bass.IndirectOffsetOnAxis(slot_u32[:, at:at + 1], 0), xn_all[:, t, :], None,
                    ).then_inc(d_scattered, 16)
            pool.wait_ge(d_sw_lo, done(d_sw_lo, 11))
            pool.memset(th[:], 0.0).then_inc(filled, 1)
            for e in range(EXPERTS):
                pool.wait_ge(loads[e], 48)
                pool.sem_inc(experts_loaded, 1)
            for i in range(XR):
                pool.wait_ge(t_y_stored[i], 16 * (SLOTS // XR + 1))
            for n in range(TOP_K * TILES):
                t, c = n // TOP_K, n % TOP_K
                if n >= YR:
                    pool.wait_ge(y_added, n - YR + 1)
                at = c * TILES + t
                pool.indirect_dma_start(
                    yg[:, n % YR, :], None, sorted_y, bass.IndirectOffsetOnAxis(slot_u32[:, at:at + 1], 0),
                ).then_inc(y_gathered[n % YR], 16)

        @block.tensor
        def _(pe):
            pe.wait_ge(ident_ready, 1)

            def transpose_inputs(b):
                pe.wait_ge(a_xn, b + 1)
                pe.wait_ge(a_xnT, room(a_xnT, b))
                for j in range(ROWT):
                    for k in range(KC):
                        last = pe.transpose(pair[0][:, j, k * P:(k + 1) * P], xn0[:, j, k * P:(k + 1) * P], ident[:])
                last.then_inc(a_xnT_psum, 1)
                pe.wait_ge(a_ctx_staged, b + 1)
                pe.wait_ge(a_ctxT, room(a_ctxT, b))
                for j in range(ROWT):
                    for k in range(KC):
                        last = pe.transpose(pair[1][:, j, k * P:(k + 1) * P],
                                            ctx_stage[:, j, k * P:(k + 1) * P], ident[:])
                last.then_inc(a_ctxT_psum, 1)

            def score(b):
                pe.wait_ge(a_xnT, done(a_xnT, b))
                pe.wait_ge(a_ctxT, done(a_ctxT, b))
                pe.wait_ge(a_masked, room(a_masked, b))
                for j in range(ROWT):
                    for k in range(KC):
                        last = pe.matmul(bank[4][:, j * CTX:(j + 1) * CTX], xnT0[:, k, j * P:(j + 1) * P],
                                         ctxT[:, k, bass.ds(b * CTX, CTX)], start=(k == 0), stop=(k == KC - 1))
                last.then_inc(a_scores, 1)

            def transpose_probs(b):
                pe.wait_ge(a_probs, done(a_probs, b))
                pe.wait_ge(a_probsT, room(a_probsT, b))
                for m in range(CTX // P):
                    for j in range(ROWT):
                        last = pe.transpose(bank[5][:, m * SEQ + j * P:m * SEQ + (j + 1) * P],
                                            probs[:, j, m * P:(m + 1) * P], ident[:])
                last.then_inc(a_probsT_psum, 1)

            def read_out(b):
                pe.wait_ge(a_probsT, done(a_probsT, b))
                pe.wait_ge(a_resid, room(a_resid, b))
                for j in range(ROWT):
                    for m in range(CTX // P):
                        last = pe.matmul(bank[6 + j][:], probsT[:, m, j * P:(j + 1) * P],
                                         ctx_nat[:, ROWT * b + m, :], start=(m == 0), stop=(m == CTX // P - 1))
                last.then_inc(a_readout, 1)

            transpose_inputs(0)
            score(0)
            transpose_inputs(1)
            transpose_probs(0)
            with pe.Fori(1, BATCH - 1) as b:
                score(b)
                transpose_inputs(b + 1)
                read_out(b - 1)
                transpose_probs(b)
            score(BATCH - 1)
            read_out(BATCH - 2)
            transpose_probs(BATCH - 1)
            read_out(BATCH - 1)

            def transpose_group(g, s):
                pe.wait_ge(s["xn"], g + 1)
                pe.wait_ge(s["lo"], room(s["lo"], g))
                for i in range(GT):
                    for k in range(KC):
                        last = pe.transpose(pair[i // 2][:, i % 2, k * P:(k + 1) * P], xn[:, i, k * P:(k + 1) * P], ident[:])
                last.then_inc(s["xT_psum"], 1)

            with pe.Fori(0, GROUPS) as g:
                transpose_group(g, nb)

            def gate_up(g, c):
                n = g * FC + c
                pe.wait_ge(w_quant, done(w_quant, c))
                pe.wait_ge(b_fused, room(b_fused, n))
                for t, (at, signal) in enumerate(((c % 2, b_gate_ps), (2 + c % 2, b_up_ps))):
                    for k in range(KC):
                        for part in (xT_hi, xT_lo):
                            last = pe.matmul(bank[at][:], wq[:, c, (t * KC + k) * P:(t * KC + k + 1) * P],
                                             part[:, k, bass.ds(g * GW, GW)],
                                             start=(k == 0 and part is xT_hi), stop=(k == KC - 1 and part is xT_lo))
                    last.then_inc(signal, 1)

            def down_chunk(g, c):
                n = g * FC + c
                pe.wait_ge(b_fhi, done(b_fhi, n))
                pe.wait_ge(b_flo, n + 1)
                if c == 0:
                    pe.wait_ge(b_scaled, room(b_scaled, GT * g + GT - 1))
                for i in range(GT):
                    for part in (fT_hi, fT_lo):
                        last = pe.matmul(bank[4 + i][:], part[:, c % FR, i * P:(i + 1) * P],
                                         wq[:, c, 2 * DIM:QW], start=(c == 0 and part is fT_hi),
                                         stop=(c == FC - 1 and part is fT_lo))
                last.then_inc(b_down, 1)

            pe.wait_ge(nb["lo"], done(nb["lo"], GROUPS - 1))
            with pe.Fori(0, GROUPS) as g:
                for c in range(FC):
                    gate_up(g, c)
                    if c:
                        down_chunk(g, c - 1)
                down_chunk(g, FC - 1)

            pe.wait_ge(b_scaled, done(b_scaled, TILES - 1))
            with pe.Fori(0, GROUPS) as g:
                transpose_group(g, nr)
            pe.wait_ge(nr["lo"], done(nr["lo"], GROUPS - 1))
            pe.wait_ge(c_lo, 3)
            pe.wait_ge(filled, 3)
            with pe.Fori(0, HEADS) as h:
                for i in range(GROUPS):
                    pe.wait_ge(c_copied, room(c_copied, h * 12 + i))
                    for n, (w, part) in enumerate(((wh_hi, xT_hi), (wh_hi, xT_lo), (wh_lo, xT_hi))):
                        last = pe.matmul(bank[i][:], w[:, h, :], part[:, h, i * GW:(i + 1) * GW],
                                         start=(n == 0), stop=(n == 2))
                    last.then_inc(c_proj, 1)
                pe.wait_ge(c_head, h + 1)
                for i in range(GROUPS):
                    pe.wait_ge(c_copied, room(c_copied, h * 12 + 4 + i))
                    pe.matmul(bank[i][:], wh_head[:], ctxT[:, h, i * GW:(i + 1) * GW],
                              start=True, stop=True).then_inc(c_proj, 1)
                for i in range(GROUPS):
                    pe.wait_ge(c_copied, done(c_copied, h * 12 + 4 + i))
                    for j in range(GT):
                        last = pe.transpose(bank[i][:, j * P:(j + 1) * P], kT[:, (GT * i + j) * P:(GT * i + j + 1) * P], ident[:])
                    last.then_inc(c_proj, 1)
                pe.wait_ge(c_masked, room(c_masked, h))
                for b in range(BATCH):
                    pe.matmul(bank[4][:, 0:SEQ], kT[:, b * SEQ:b * SEQ + P], qT[:, b * SEQ:(b + 1) * SEQ],
                              start=(b == 0), stop=(b == BATCH - 1))
                for b in range(BATCH):
                    last = pe.matmul(bank[5][:, 0:P], kT[:, b * SEQ + P:(b + 1) * SEQ], qT[:, b * SEQ + P:(b + 1) * SEQ],
                                     start=(b == 0), stop=(b == BATCH - 1))
                last.then_inc(c_scores, 1)
                pe.wait_ge(c_copied, done(c_copied, h * 12 + 11))
                pe.wait_ge(c_weights, h + 1)
                vv = v[:].rearrange("p (b j) e -> p j b e", j=ROWT)
                for j in range(ROWT):
                    for half in range(2):
                        o = 2 * j + half
                        pe.wait_ge(c_o_copied, room(c_o_copied, 4 * h + o))
                        for m in range(ROWT):
                            last = pe.matmul(bank[6 + half][:], weightT[:, m, j * P:(j + 1) * P],
                                             vv[:, m, 4 * half:4 * half + 4, :], start=(m == 0), stop=(m == ROWT - 1))
                        last.then_inc(c_o_ps, 1)

            def gate_project(t):
                pe.wait_ge(g_w, room(g_w, t))
                for k in range(KC):
                    tok = bass.ds(t * P, P)
                    for n, (part, w) in enumerate(((xT_hi, wgo_hi), (xT_hi, wgo_lo), (xT_lo, wgo_hi))):
                        last = pe.matmul(bank[0][:], part[:, k, tok], w[:, 0, k, :],
                                         start=(k == 0 and n == 0), stop=(k == KC - 1 and n == 2))
                last.then_inc(g_w_ps, 1)

            def transpose_z(t):
                pe.wait_ge(g_z, done(g_z, t))
                pe.wait_ge(g_lo, room(g_lo, t))
                for k in range(KC):
                    last = pe.transpose(bank[1][:, k * P:(k + 1) * P], z[:, k * P:(k + 1) * P], ident[:])
                last.then_inc(g_zT_ps, 1)

            def out_project(t):
                pe.wait_ge(g_lo, done(g_lo, t))
                pe.wait_ge(g_resid, room(g_resid, t))
                for k in range(KC):
                    for n, (part, w) in enumerate(((zT_hi, wgo_hi), (zT_hi, wgo_lo), (zT_lo, wgo_hi))):
                        last = pe.matmul(bank[2][:], part[:, k, :], w[:, 1, k, :],
                                         start=(k == 0 and n == 0), stop=(k == KC - 1 and n == 2))
                last.then_inc(g_wo, 1)

            pe.wait_ge(c_copied, done(c_copied, HEADS * 12 - 1))
            gate_project(0)
            gate_project(1)
            transpose_z(0)
            with pe.Fori(1, TILES - 1) as t:
                gate_project(t + 1)
                transpose_z(t)
                out_project(t - 1)
            transpose_z(TILES - 1)
            out_project(TILES - 2)
            out_project(TILES - 1)

            for g in range(GROUPS):
                pe.wait_ge(nd["xn"], g + 1)
                pe.wait_ge(nd["lo"], room(nd["lo"], g))
                for i in range(GT):
                    for k in range(KC):
                        last = pe.transpose(pair[i // 2][:, i % 2, k * P:(k + 1) * P],
                                            xn_all[:, GT * g + i, k * P:(k + 1) * P], ident[:])
                last.then_inc(nd["xT_psum"], 1)
            pe.wait_ge(nd["lo"], done(nd["lo"], GROUPS - 1))
            pe.wait_ge(weights_loaded, 96 + 16 * 6)
            n = 0
            for t in range(2):
                for k in range(KC):
                    pe.wait_ge(d_sw_lo, room(d_sw_lo, n))
                    for c, rows in enumerate(HC):
                        last = pe.transpose(bank[n % 4][:, c * P:c * P + rows], sw12_f32[0:rows, t, c, k * P:(k + 1) * P],
                                            ident[0:rows, 0:rows])
                    last.then_inc(d_sw_ps, 1)
                    n += 1
            for c, rows in enumerate(HC):
                pe.wait_ge(d_sw_lo, room(d_sw_lo, n))
                for k in range(KC):
                    last = pe.transpose(bank[n % 4][0:rows, k * P:(k + 1) * P], sw3_f32[:, k, c * P:c * P + rows], ident[:])
                last.then_inc(d_sw_ps, 1)
                n += 1
            pe.wait_ge(d_sw_lo, room(d_sw_lo, n))
            for k in range(KC):
                last = pe.transpose(bank[n % 4][:, k * EXPERTS:(k + 1) * EXPERTS], router_f32[:, k * P:(k + 1) * P],
                                    ident[0:EXPERTS, 0:EXPERTS])
            last.then_inc(d_sw_ps, 1)
            pe.wait_ge(d_sw_lo, done(d_sw_lo, n))
            for t in range(TILES):
                for k in range(KC):
                    tok = slice(t * P, (t + 1) * P)
                    for i, (part, w) in enumerate(((xT_hi, router_hi), (xT_hi, router_lo), (xT_lo, router_hi))):
                        last = pe.matmul(bank[7][:, t * EXPERTS:(t + 1) * EXPERTS], part[:, k, tok], w[:, k, :],
                                         start=(k == 0 and i == 0), stop=(k == KC - 1 and i == 2))
            last.then_inc(d_logits, 1)

            def w1_part(part, k, at, width):
                return sw_split[:, k, part, at:at + width]

            def w2_part(part, c, rows):
                return sw_split[0:rows, :, part, 2 * HID + c * P:2 * HID + (c + 1) * P]

            def shared_up(m):
                for c, rows in enumerate(HC):
                    q = m * 3 + c
                    pe.wait_ge(d_prod, room(d_prod, q))
                    for t, (at, signal) in enumerate(((q % 2, d_gate_ps), (2 + q % 2, d_up_ps))):
                        for k in range(KC):
                            for i, (w, part) in enumerate(((0, xT_hi), (0, xT_lo), (1, xT_hi))):
                                last = pe.matmul(bank[at][0:rows, :], w1_part(w, k, t * HID + c * P, rows),
                                                 part[:, k, m * GW:(m + 1) * GW],
                                                 start=(k == 0 and i == 0), stop=(k == KC - 1 and i == 2))
                        last.then_inc(signal, 1)

            def shared_down(m):
                pe.wait_ge(d_hlo, done(d_hlo, m * 3 + 2))
                for i in range(GT):
                    pe.wait_ge(d_acc, room(d_acc, m * GT + i))
                    for c, rows in enumerate(HC):
                        for n, (part, w) in enumerate(((hT_hi, 0), (hT_hi, 1), (hT_lo, 0))):
                            last = pe.matmul(bank[4 + i][:], part[0:rows, m % 2, c, i * P:(i + 1) * P],
                                             w2_part(w, c, rows), start=(c == 0 and n == 0), stop=(c == 2 and n == 2))
                    last.then_inc(d_y_ps, 1)

            shared_up(0)
            pe.wait_ge(d_chosen, 1)
            NR = TILES * EXPERTS
            pe.matmul(bank[7][:, 0:NR], before[:], chosen[:], start=True, stop=False)
            for d in range(1, TILES):
                pe.matmul(bank[7][:, d * EXPERTS:NR], ones16[:], chosen[:, 0:NR - d * EXPERTS],
                          start=False, stop=(d == TILES - 1))
            for t in range(TILES):
                last = pe.matmul(bank[7][:, NR:NR + EXPERTS], ones16[:], chosen[:, t * EXPERTS:(t + 1) * EXPERTS],
                                 start=(t == 0), stop=(t == TILES - 1))
            last.then_inc(d_counts, 1)
            shared_up(1)
            pe.wait_ge(d_slots, 1)
            shared_down(0)
            for m in range(2, GROUPS):
                shared_up(m)
                shared_down(m - 1)
            shared_down(GROUPS - 1)

            def tile_transpose(i, slot, lap):
                pe.wait_ge(ring_loaded[slot], 16 * lap + (48 * (FC // RAW) + 16))
                pe.wait_ge(t_xlo, room(t_xlo, i))
                for k in range(KC):
                    last = pe.transpose(bank[0][:, k * P:(k + 1) * P], xg[:, slot, k * P:(k + 1) * P], ident[:])
                last.then_inc(t_xT, 1)

            def tile_up(i, room_of):
                pe.wait_ge(t_xlo, done(t_xlo, i))
                pe.wait_ge(t_h, room(t_h, i))
                for k in range(KC):
                    for part, w in ((xgT_hi, 0), (xgT_hi, 1), (xgT_lo, 0)):
                        at = (2 * k + w) * UNIT
                        first, end = k == 0 and part is xgT_hi and w == 0, k == KC - 1 and part is xgT_lo
                        pe.matmul(bank[1][:, 0:HID], part[:, k, :], experts[:, room_of, at:at + HID], start=first, stop=end)
                        last = pe.matmul(bank[2][:, 0:HID], part[:, k, :], experts[:, room_of, at + HID:at + 2 * HID],
                                         start=first, stop=end)
                last.then_inc(t_gu, 1)

            def tile_hidden(i):
                pe.wait_ge(t_h, done(t_h, i))
                pe.wait_ge(t_hlo, room(t_hlo, i))
                for c in range(3):
                    last = pe.transpose(bank[3][:, c * P:(c + 1) * P], th[:, c * P:(c + 1) * P], ident[:])
                last.then_inc(t_hT, 1)

            def tile_down(i, room_of):
                pe.wait_ge(t_hlo, done(t_hlo, i))
                pe.wait_ge(t_ycopy, room(t_ycopy, i))
                block = experts[:, room_of, :].rearrange("p (k s u) -> p k s u", k=KC, s=2)
                for c in range(3):
                    for n, (part, w) in enumerate(((thT_hi, 0), (thT_hi, 1), (thT_lo, 0))):
                        last = pe.matmul(bank[4][:], part[:, c, :], block[:, :, w, 2 * HID + c * P:2 * HID + (c + 1) * P],
                                         start=(c == 0 and n == 0), stop=(c == 2 and n == 2))
                last.then_inc(t_y, 1)

            def expert_of(i):
                loads_of = pe.value_load(tile_expert_i[0:1, 1, bass.ds(i, 1)], min_val=1, max_val=EXPERTS)
                hold(pe, experts_loaded, loads_of)
                return pe.value_load(tile_expert_i[0:1, 0, bass.ds(i, 1)], min_val=0, max_val=EXPERTS - 1)

            pe.wait_ge(d_tile_expert, 2)
            pe.wait_ge(d_acc, done(d_acc, TILES - 1))
            pe.wait_ge(filled, 4)
            tile_transpose(0, 0, 0)
            for i in (0,):
                tile_up(i, expert_of(i))
                tile_transpose(1, 1, 0)
                tile_hidden(i)
            with pe.Fori(0, SLOTS // XR - 1) as lap:
                for s in range(XR):
                    i = lap * XR + (s + 1)
                    tile_up(i, expert_of(i))
                    tile_transpose(i + 1, (s + 2) % XR, lap + (s + 2) // XR)
                    tile_down(i - 1, expert_of(i - 1))
                    tile_hidden(i)
            for i in range(SLOTS - XR + 1, SLOTS):
                tile_up(i, expert_of(i))
                if i + 1 < SLOTS:
                    tile_transpose(i + 1, (i + 1) % XR, (i + 1) // XR)
                tile_down(i - 1, expert_of(i - 1))
                tile_hidden(i)
            tile_down(SLOTS - 1, expert_of(SLOTS - 1))

        @block.scalar
        def _(act):
            def copy_inputs(b):
                pv = pair[0][:].rearrange("p j (k c) -> p j k c", c=P)
                act.wait_ge(a_xnT_psum, done(a_xnT_psum, b))
                act.wait_ge(a_scores, room(a_scores, b))
                act.activation(xnT0[:].rearrange("p k (j c) -> p j k c", c=P), pv, ACT.Copy).then_inc(a_xnT, 1)
                act.wait_ge(a_ctxT_psum, done(a_ctxT_psum, b))
                act.activation(ctxT[:, :, bass.ds(b * CTX, CTX)].rearrange("p k (j c) -> p j k c", c=P),
                               pair[1][:].rearrange("p j (k c) -> p j k c", c=P), ACT.Copy).then_inc(a_ctxT, 1)

            def exponentials(b):
                act.wait_ge(a_negmax, b + 1)
                act.wait_ge(a_probsT_psum, room(a_probsT_psum, b))
                act.wait_ge(a_rinv, room(a_rinv, b))
                for j in range(ROWT):
                    last = act.activation(probs[:, j, :], scores_sb[:, j, :], ACT.Exp, bias=negmax[:, j:j + 1],
                                          scale=SCALE, accum_out=rowsum[:, j:j + 1])
                last.then_inc(a_probs, 1)

            def copy_probsT(b):
                act.wait_ge(a_probsT_psum, done(a_probsT_psum, b))
                act.wait_ge(a_readout, room(a_readout, b))
                act.activation(probsT[:].rearrange("p m s -> p (m s)"), bank[5][:], ACT.Copy).then_inc(a_probsT, 1)

            copy_inputs(0)
            with act.Fori(0, BATCH - 1) as b:
                copy_inputs(b + 1)
                exponentials(b)
                copy_probsT(b)
            exponentials(BATCH - 1)
            copy_probsT(BATCH - 1)

            def split_hi(g, s):
                act.wait_ge(s["xT_psum"], done(s["xT_psum"], g))
                for h in range(2):
                    last = act.activation(xT_hi[:, :, bass.ds((GT * g + 2 * h) * P, 2 * P)].rearrange("p k (j c) -> p j k c", c=P),
                                   pair[h][:].rearrange("p j (k c) -> p j k c", c=P),
                                   ACT.Copy)
                last.then_inc(s["hi"], 1)
            with act.Fori(0, GROUPS) as g:
                split_hi(g, nb)

            act.wait_ge(scales_loaded, 48)

            def unit_hi(n, slot, lap):
                act.wait_ge(u_loaded[slot], 48 * lap + 48)
                act.wait_ge(u_stored[slot], 16 * lap + 16)
                act.activation(unit_split[:, slot, 0, :], unit_f32[:, slot, :], ACT.Copy, scale=WS).then_inc(u_hi, 1)

            def gate(g, c):
                n = g * FC + c
                act.wait_ge(b_gate_ps, n + 1)
                act.wait_ge(b_fused, room(b_fused, n))
                act.activation(silu[:, c % 2, :], bank[c % 2][:], ACT.Silu, scale=gscale[:, c:c + 1]).then_inc(b_silu, 1)

            def fused_hi(g, c):
                n = g * FC + c
                act.wait_ge(b_fused, done(b_fused, n))
                act.wait_ge(b_down, room(b_down, n))
                act.activation(fT_hi[:, c % FR, :], fused[:, c % 2, :], ACT.Copy).then_inc(b_fhi, 1)

            with act.Fori(0, GROUPS) as g:
                for c in range(FC):
                    gate(g, c)
                    if c:
                        fused_hi(g, c - 1)
                    if c < EXPERTS * KC // GROUPS:
                        unit_hi(g * (EXPERTS * KC // GROUPS) + c, c % 2, g * (EXPERTS * KC // GROUPS // 2) + c // 2)
                fused_hi(g, FC - 1)

            with act.Fori(0, GROUPS) as g:
                split_hi(g, nr)
            act.wait_ge(weights_loaded, 96)
            act.activation(wh_hi[:], wh_f32[:], ACT.Copy, scale=WS).then_inc(c_hi, 1)
            for i in range(2):
                act.activation(wgo_hi[:, i], wgo_f32[:, i], ACT.Copy, scale=WS).then_inc(c_hi, 1)

            with act.Fori(0, HEADS) as h:
                act.wait_ge(c_scores, room(c_scores, h))
                for i in range(3 * GROUPS):
                    if i == 2 * GROUPS:
                        act.wait_ge(c_o_ps, room(c_o_ps, 4 * h + 3))
                    act.wait_ge(c_proj, h * 12 + i + 1)
                    at = slice(i % GROUPS * GW, (i % GROUPS + 1) * GW)
                    dst = (qT[:, at], kT[:, at], v[:].rearrange("p t e -> p (t e)")[:, at])[i // GROUPS]
                    act.activation(dst, bank[i % GROUPS][:], ACT.Copy, scale=1.0 / WS if i < GROUPS else 1.0).then_inc(c_copied, 1)

            def relu_gate(t):
                act.wait_ge(g_w_ps, t + 1)
                act.wait_ge(g_z, room(g_z, t))
                act.activation(w_relu[:], bank[0][:], ACT.Relu, scale=1.0 / WS).then_inc(g_w, 1)

            def split_z(t):
                act.wait_ge(g_zT_ps, done(g_zT_ps, t))
                act.wait_ge(g_wo, room(g_wo, t))
                act.activation(zT_hi[:].rearrange("p k c -> p (k c)"), bank[1][:], ACT.Copy).then_inc(g_hi, 1)

            relu_gate(0)
            with act.Fori(0, TILES - 1) as t:
                relu_gate(t + 1)
                split_z(t)
            split_z(TILES - 1)

            with act.Fori(0, GROUPS) as g:
                split_hi(g, nd)
            for n, (src, hi, lo) in enumerate(sw_units()):
                act.wait_ge(d_sw_ps, n + 1)
                act.activation(hi, src, ACT.Copy, scale=WS).then_inc(d_sw_hi, 1)
            act.wait_ge(d_route, 2)
            act.activation(prob[:], prob[:], ACT.Exp).then_inc(d_exp, 1)

            for m in range(GROUPS):
                for c in range(4):
                    if c < 3:
                        rows, q = HC[c], m * 3 + c
                        act.wait_ge(d_gate_ps, q + 1)
                        act.wait_ge(d_prod, room(d_prod, q))
                        act.activation(hg[0:rows, q % 2, :], bank[q % 2][0:rows, :], ACT.Silu, scale=1.0 / WS).then_inc(d_silu, 1)
                    if c:
                        rows, q = HC[c - 1], m * 3 + c - 1
                        act.wait_ge(d_prod, done(d_prod, q))
                        if c == 1:
                            act.wait_ge(d_y_ps, room(d_y_ps, m * GT + GT - 1))
                        act.activation(hT_hi[0:rows, m % 2, c - 1, :], hp[0:rows, q % 2, :], ACT.Copy).then_inc(d_hhi, 1)
            act.wait_ge(d_acc, done(d_acc, TILES - 1))
            act.wait_ge(d_scattered, 16 * TOP_K * TILES)
            for e in range(2, EXPERTS):
                act.dma_start(experts[:, EXPERTS - 1 - e, :].rearrange("p (k u) -> p k u", k=KC),
                              split_w[e].rearrange("k p u -> p k u")).then_inc(loads[e], 16)

            def tile_x_hi(i):
                act.wait_ge(t_xT, i + 1)
                act.activation(xgT_hi[:].rearrange("p k c -> p (k c)"), bank[0][:], ACT.Copy).then_inc(t_xhi, 1)

            def tile_silu(i):
                act.wait_ge(t_gu, i + 1)
                act.wait_ge(t_h, room(t_h, i))
                act.activation(tg[:], bank[1][:, 0:HID], ACT.Silu, scale=1.0 / WS).then_inc(t_silu, 1)

            def tile_h_hi(i):
                act.wait_ge(t_hT, done(t_hT, i))
                act.activation(thT_hi[:].rearrange("p k c -> p (k c)"), bank[3][:, 0:3 * P], ACT.Copy).then_inc(t_hhi, 1)

            def tile_y(i, slot, lap):
                act.wait_ge(t_y, i + 1)
                act.wait_ge(t_y_stored[slot], 16 * lap + 16)
                act.activation(ty[:, slot, :], bank[4][:], ACT.Copy, scale=1.0 / WS).then_inc(t_ycopy, 1)

            tile_x_hi(0)
            tile_silu(0)
            tile_x_hi(1)
            tile_h_hi(0)
            with act.Fori(0, SLOTS // XR - 1) as lap:
                for s in range(XR):
                    i = lap * XR + (s + 1)
                    tile_silu(i)
                    tile_x_hi(i + 1)
                    tile_y(i - 1, s, lap)
                    tile_h_hi(i)
            for i in range(SLOTS - XR + 1, SLOTS):
                tile_silu(i)
                if i + 1 < SLOTS:
                    tile_x_hi(i + 1)
                tile_y(i - 1, (i - 1) % XR, (i - 1) // XR)
                tile_h_hi(i)
            tile_y(SLOTS - 1, (SLOTS - 1) % XR, (SLOTS - 1) // XR)

        @block.vector
        def _(dve):
            dve.wait_ge(mask_loaded, 16)
            dve.tensor_scalar(maskbias[:], mask_u8[:], -MASKED, MASKED, ALU.mult, ALU.add).then_inc(a_bias, 1)
            dve.tensor_reduce(valid[:], mask_u8[:], AX.X, ALU.max).then_inc(a_valid, 1)

            def normalise0(b):
                dve.wait_ge(batches_loaded, b + 1)
                for j in range(ROWT):
                    dve.bn_stats(stats[:, j, :], x_res[:, ROWT * b + j, :]).then_inc(a_stats, 1)
                hold(dve, a_stats, ROWT * b + ROWT)
                for j in range(ROWT):
                    last = dve.bn_aggr(meanvar[:, j, :], stats[:, j, :])
                last.then_inc(a_meanvar, 1)
                dve.wait_ge(a_rstd, b + 1)
                dve.wait_ge(a_xnT_psum, room(a_xnT_psum, b))
                for j in range(ROWT):
                    last = dve.tensor_scalar(xn0[:, j, :], x_res[:, ROWT * b + j, :], meanvar[:, j, 0:1],
                                             rstd[:, j:j + 1], ALU.subtract, ALU.mult)
                last.then_inc(a_xn, 1)

            def mask_and_max(b):
                dve.wait_ge(a_scores, done(a_scores, b))
                dve.wait_ge(a_probs, room(a_probs, b))
                mb = maskbias[:, b, :]
                for j in range(ROWT):
                    last = dve.tensor_tensor(scores_sb[:, j, :], bank[4][:, j * CTX:(j + 1) * CTX], mb, ALU.add)
                last.then_inc(a_masked, 1)
                dve.wait_ge(a_masked, done(a_masked, b))
                dve.tensor_reduce(rowmax[:], scores_sb[:], AX.X, ALU.max).then_inc(a_rowmax, 1)
                dve.wait_ge(a_rowmax, b + 1)
                dve.tensor_scalar(negmax[:], rowmax[:], -SCALE, None, ALU.mult).then_inc(a_negmax, 1)

            def inverse_sums(b):
                dve.wait_ge(a_probs, done(a_probs, b))
                dve.reciprocal(rinv[:], rowsum[:]).then_inc(a_rinv, 1)
                dve.wait_ge(a_rinv, done(a_rinv, b))
                dve.tensor_scalar(rscale[:], rinv[:], valid[:, bass.ds(b, 1)], None, ALU.mult).then_inc(a_rscale, 1)

            def add_readout(b):
                dve.wait_ge(a_rscale, b + 1)
                dve.wait_ge(a_readout, done(a_readout, b))
                for j in range(ROWT):
                    t = ROWT * b + j
                    last = dve.scalar_tensor_tensor(x_res[:, t, :], bank[6 + j][:], rscale[:, j:j + 1], x_res[:, t, :],
                                                    ALU.mult, ALU.add)
                last.then_inc(a_resid, 1)

            dve.wait_ge(a_bias, 1)
            dve.wait_ge(a_valid, 1)
            normalise0(0)
            normalise0(1)
            mask_and_max(0)
            normalise0(2)
            with dve.Fori(1, BATCH - 2) as b:
                inverse_sums(b - 1)
                mask_and_max(b)
                normalise0(b + 2)
                add_readout(b - 1)
            inverse_sums(BATCH - 3)
            mask_and_max(BATCH - 2)
            add_readout(BATCH - 3)
            inverse_sums(BATCH - 2)
            mask_and_max(BATCH - 1)
            add_readout(BATCH - 2)
            inverse_sums(BATCH - 1)
            add_readout(BATCH - 1)

            def quantise(i, slot, lap):
                dve.wait_ge(ring_loaded[slot], 48 * lap + 48)
                dve.wait_ge(w_quant, room(w_quant, i))
                dve.tensor_scalar(expo[:].bitcast(U32), raw[:, slot, :].bitcast(U32), 0x7F800000, None,
                                  ALU.bitwise_and).then_inc(w_step, 1)
                dve.wait_ge(w_step, i * 3 + 1)
                dve.tensor_scalar(expo[:], expo[:], 2.0 ** -6, 1.5 * 2.0 ** 20, ALU.max, ALU.mult).then_inc(w_step, 1)
                dve.wait_ge(w_step, i * 3 + 2)
                dve.tensor_tensor(raw[:, slot, :], raw[:, slot, :], expo[:], ALU.add).then_inc(w_step, 1)
                dve.wait_ge(w_step, i * 3 + 3)
                dve.tensor_tensor(wq[:, i, :], raw[:, slot, :], expo[:], ALU.subtract).then_inc(w_quant, 1)

            with dve.Fori(0, FC // RAW) as lap:
                for slot in range(RAW):
                    quantise(lap * RAW + slot, slot, lap)

            def normalise(g, s):
                if s is nb:
                    dve.wait_ge(a_resid, done(a_resid, BATCH - 1))
                for i in range(GT):
                    dve.bn_stats(stats[:, i, :], x_res[:, GT * g + i, :]).then_inc(s["stats"], 1)
                hold(dve, s["stats"], GT * g + GT)
                for i in range(GT):
                    last = dve.bn_aggr(meanvar[:, i, :], stats[:, i, :])
                last.then_inc(s["meanvar"], 1)
                dve.wait_ge(s["rstd"], g + 1)
                dve.wait_ge(s["xT_psum"], room(s["xT_psum"], g))
                for i in range(GT):
                    last = dve.tensor_scalar(xn[:, i, :], x_res[:, GT * g + i, :], meanvar[:, i, 0:1],
                                             rstd[:, i:i + 1], ALU.subtract, ALU.mult)
                last.then_inc(s["xn"], 1)

            def split_lo(g, s):
                dve.wait_ge(s["hi"], g + 1)
                for i in range(GT):
                    at = bass.ds((GT * g + i) * P, P)
                    last = dve.tensor_tensor(xT_lo[:, :, at], pair[i // 2][:, i % 2, :].rearrange("p (k c) -> p k c", c=P),
                                             xT_hi[:, :, at], ALU.subtract)
                last.then_inc(s["lo"], 1)

            normalise(0, nb)
            with dve.Fori(0, GROUPS - 1) as g:
                split_lo(g, nb)
                normalise(g + 1, nb)
            split_lo(GROUPS - 1, nb)

            dve.wait_ge(scales_loaded, 48)
            dve.wait_ge(filled, 2)

            def unit_lo(n, slot):
                dve.wait_ge(u_hi, n + 1)
                dve.scalar_tensor_tensor(unit_split[:, slot, 1, :], unit_f32[:, slot, :], WS, unit_split[:, slot, 0, :],
                                         ALU.mult, ALU.subtract).then_inc(u_lo, 1)

            def product(g, c):
                n = g * FC + c
                dve.wait_ge(b_silu, n + 1)
                dve.wait_ge(b_up_ps, n + 1)
                dve.wait_ge(b_fhi, room(b_fhi, n))
                dve.scalar_tensor_tensor(fused[:, c % 2, :], bank[2 + c % 2][:], uscale[:, c:c + 1], silu[:, c % 2, :],
                                         ALU.mult, ALU.mult).then_inc(b_fused, 1)

            def fused_lo(g, c):
                n = g * FC + c
                dve.wait_ge(b_fhi, done(b_fhi, n))
                dve.tensor_tensor(fT_lo[:, c % FR, :], fused[:, c % 2, :], fT_hi[:, c % FR, :],
                                  ALU.subtract).then_inc(b_flo, 1)

            def add_down(g):
                dve.wait_ge(b_down, done(b_down, FC * g + FC - 1))
                for i in range(GT):
                    t = GT * g + i
                    dve.tensor_tensor(down[:, i % 2, :], bank[4 + i][:], dscale[:], ALU.mult).then_inc(b_scaled, 1)
                    dve.wait_ge(b_scaled, done(b_scaled, GT * g + i))
                    dve.tensor_tensor(x_res[:, t, :], x_res[:, t, :], down[:, i % 2, :], ALU.add).then_inc(b_resid, 1)

            with dve.Fori(0, GROUPS) as g:
                for c in range(FC):
                    product(g, c)
                    if c:
                        fused_lo(g, c - 1)
                    if c < EXPERTS * KC // GROUPS:
                        unit_lo(g * (EXPERTS * KC // GROUPS) + c, c % 2)
                fused_lo(g, FC - 1)
                add_down(g)

            dve.wait_ge(b_resid, TILES)
            normalise(0, nr)
            with dve.Fori(0, GROUPS - 1) as g:
                split_lo(g, nr)
                normalise(g + 1, nr)
            split_lo(GROUPS - 1, nr)
            dve.wait_ge(c_hi, 3)
            dve.scalar_tensor_tensor(wh_lo[:], wh_f32[:], WS, wh_hi[:], ALU.mult, ALU.subtract).then_inc(c_lo, 1)
            for i in range(2):
                dve.scalar_tensor_tensor(wgo_lo[:, i], wgo_f32[:, i], WS, wgo_hi[:, i], ALU.mult, ALU.subtract).then_inc(c_lo, 1)

            oT = ctxT[:].rearrange("p h (b j e) -> p h b j e", j=ROWT, e=P)
            dve.wait_ge(filled, 3)
            with dve.Fori(0, HEADS) as h:
                dve.wait_ge(c_scores, done(c_scores, h))
                dve.tensor_tensor(scaled[:, 0:SEQ], bank[4][:, 0:SEQ], decay[:, 0, h, :], ALU.mult)
                dve.tensor_tensor(scaled[:, SEQ:], bank[5][:, 0:P], decay[:, 1, h, P:SEQ], ALU.mult).then_inc(c_masked, 1)
                dve.wait_ge(c_masked, done(c_masked, h))
                dve.wait_ge(c_o_ps, room(c_o_ps, 4 * h + 3))
                dve.tensor_scalar(floored[:], scaled[:], -1.0, 1.0, ALU.mult, ALU.max).then_inc(c_scaled, 1)
                dve.wait_ge(c_scaled, h + 1)
                dve.tensor_tensor(weightT[:, 0, :], floored[:, 0:SEQ], scaled[:, 0:SEQ], ALU.max)
                dve.tensor_tensor(weightT[:, 1, P:SEQ], floored[:, SEQ:], scaled[:, SEQ:], ALU.max).then_inc(c_weights, 1)
                for j in range(ROWT):
                    for half in range(2):
                        o = 2 * j + half
                        dve.wait_ge(c_o_ps, done(c_o_ps, 4 * h + o))
                        dve.tensor_copy(oT[:, h, 4 * half:4 * half + 4, j, :],
                                        bank[6 + half][:].rearrange("p (b e) -> p b e", e=P)).then_inc(c_o_copied, 1)

            o_tile = ctxT[:].rearrange("p h (t e) -> p t h e", e=P)

            def group_stats(t):
                dve.bn_stats(gn_stats[:], o_tile[:, t]).then_inc(g_stats, 1)
                hold(dve, g_stats, t + 1)
                dve.bn_aggr(gn_meanvar[:], gn_stats[:]).then_inc(g_meanvar, 1)
                dve.wait_ge(g_meanvar, t + 1)
                dve.tensor_copy(gn_mean[:, bass.ds(t, 1)], gn_meanvar[:, 0:1])
                dve.tensor_scalar(gn_vareps[:, bass.ds(t, 1)], gn_meanvar[:, 1:2], GN_EPS, None, ALU.add).then_inc(g_vareps, 1)

            def group_normalise(t):
                dve.wait_ge(g_rstd, t + 1)
                dve.wait_ge(g_ygamma, room(g_ygamma, t))
                dve.tensor_scalar(y_norm[:].rearrange("p (h e) -> p h e", e=P), o_tile[:, t], gn_mean[:, bass.ds(t, 1)],
                                  gn_rstd[:, bass.ds(t, 1)], ALU.subtract, ALU.mult).then_inc(g_ynorm, 1)

            def gate_product(t):
                dve.wait_ge(g_w, done(g_w, t))
                dve.wait_ge(g_y, t + 1)
                dve.wait_ge(g_zT_ps, room(g_zT_ps, t))
                dve.tensor_tensor(z[:], w_relu[:], y[:], ALU.mult).then_inc(g_z, 1)

            def split_z_lo(t):
                dve.wait_ge(g_hi, t + 1)
                dve.tensor_tensor(zT_lo[:].rearrange("p k c -> p (k c)"), bank[1][:], zT_hi[:].rearrange("p k c -> p (k c)"),
                                  ALU.subtract).then_inc(g_lo, 1)

            def add_output(t):
                dve.wait_ge(g_wo, done(g_wo, t))
                dve.scalar_tensor_tensor(x_res[:, t, :], bank[2][:], 1.0 / WS, x_res[:, t, :], ALU.mult, ALU.add).then_inc(g_resid, 1)

            dve.wait_ge(c_o_copied, done(c_o_copied, 4 * HEADS - 1))
            group_stats(0)
            group_stats(1)
            group_normalise(0)
            gate_product(0)
            group_stats(2)
            group_normalise(1)
            split_z_lo(0)
            with dve.Fori(1, TILES - 2) as t:
                gate_product(t)
                group_stats(t + 2)
                group_normalise(t + 1)
                split_z_lo(t)
                add_output(t - 1)
            gate_product(TILES - 2)
            group_normalise(TILES - 1)
            split_z_lo(TILES - 2)
            add_output(TILES - 3)
            gate_product(TILES - 1)
            split_z_lo(TILES - 1)
            add_output(TILES - 2)
            add_output(TILES - 1)

            dve.wait_ge(g_resid, done(g_resid, TILES - 1))
            for g in range(GROUPS):
                for i in range(GT):
                    dve.bn_stats(stats[:, i, :], x_res[:, GT * g + i, :]).then_inc(nd["stats"], 1)
                dve.wait_ge(nd["stats"], GT * g + GT)
                for i in range(GT):
                    last = dve.bn_aggr(meanvar[:, i, :], stats[:, i, :])
                last.then_inc(nd["meanvar"], 1)
                dve.wait_ge(nd["rstd"], g + 1)
                for i in range(GT):
                    last = dve.tensor_scalar(xn_all[:, GT * g + i, :], x_res[:, GT * g + i, :], meanvar[:, i, 0:1],
                                             rstd[:, i:i + 1], ALU.subtract, ALU.mult)
                last.then_inc(nd["xn"], 1)
                split_lo(g, nd)
            for n, (src, hi, lo) in enumerate(sw_units()):
                dve.wait_ge(d_sw_hi, n + 1)
                dve.scalar_tensor_tensor(lo, src, WS, hi, ALU.mult, ALU.subtract).then_inc(d_sw_lo, 1)

            steps = [0]

            def route(instruction):
                instruction.then_inc(d_route, 1)
                steps[0] += 1
                dve.wait_ge(d_route, steps[0])

            per_tile = [P, TILES, EXPERTS]
            square = [P, TILES, EXPERTS, EXPERTS]
            dve.wait_ge(d_logits, 1)
            NR = TILES * EXPERTS
            logits = bank[7][:, 0:NR].rearrange("p (t e) -> p t e", e=EXPERTS)
            dve.wait_ge(d_const, 4)
            route(dve.tensor_scalar(rank[:], logits, 1.0 / WS, None, ALU.mult))
            dve.tensor_reduce(prob_max[:], rank[:], AX.X, ALU.max).then_inc(d_weights, 1)
            dve.wait_ge(d_weights, 1)
            route(dve.tensor_tensor(prob[:], rank[:], prob_max[:].unsqueeze(2).broadcast_to(per_tile), ALU.subtract))
            dve.wait_ge(d_exp, 1)
            route(dve.tensor_reduce(prob_sum[:], prob[:], AX.X, ALU.add))
            route(dve.reciprocal(prob_max[:], prob_sum[:]))
            route(dve.tensor_tensor(prob[:], prob[:], prob_max[:].unsqueeze(2).broadcast_to(per_tile), ALU.mult))
            own, other = prob[:].unsqueeze(3).broadcast_to(square), prob[:].unsqueeze(2).broadcast_to(square)
            route(dve.tensor_tensor(above[:], other, own, ALU.is_gt))
            route(dve.tensor_tensor(tied[:], other, own, ALU.is_equal))
            route(dve.tensor_tensor(tied[:], tied[:], lower[:].unsqueeze(1).broadcast_to(square), ALU.mult))
            route(dve.tensor_tensor(above[:], above[:], tied[:], ALU.add))
            route(dve.tensor_reduce(rank[:], above[:], AX.X, ALU.add))
            dve.tensor_scalar(chosen[:], rank[:].rearrange("p t e -> p (t e)"), 1.5, None, ALU.is_lt).then_inc(d_chosen, 1)
            route(dve.scalar_tensor_tensor(prob[:], rank[:], 1.5, prob[:], ALU.is_lt, ALU.mult))
            route(dve.tensor_reduce(prob_sum[:], prob[:], AX.X, ALU.add))
            route(dve.tensor_scalar(prob_sum[:], prob_sum[:], 1e-20, None, ALU.add))
            route(dve.reciprocal(prob_max[:], prob_sum[:]))
            dve.tensor_tensor(expert_w[:], prob[:], prob_max[:].unsqueeze(2).broadcast_to(per_tile), ALU.mult).then_inc(d_weights, 1)
            dve.wait_ge(d_weights, 2)

            def shared_hidden(m):
                for c in range(4):
                    if c < 3:
                        rows, q = HC[c], m * 3 + c
                        dve.wait_ge(d_silu, q + 1)
                        dve.wait_ge(d_up_ps, q + 1)
                        dve.wait_ge(d_hlo, room(d_hlo, q))
                        dve.scalar_tensor_tensor(hp[0:rows, q % 2, :], bank[2 + q % 2][0:rows, :], 1.0 / WS, hg[0:rows, q % 2, :],
                                                 ALU.mult, ALU.mult).then_inc(d_prod, 1)
                    if c:
                        rows, q = HC[c - 1], m * 3 + c - 1
                        dve.wait_ge(d_hhi, q + 1)
                        dve.tensor_tensor(hT_lo[0:rows, m % 2, c - 1, :], hp[0:rows, q % 2, :],
                                          hT_hi[0:rows, m % 2, c - 1, :], ALU.subtract).then_inc(d_hlo, 1)

            def shared_add(m):
                for i in range(GT):
                    t = m * GT + i
                    dve.wait_ge(d_y_ps, done(d_y_ps, m * GT + i))
                    dve.scalar_tensor_tensor(x_res[:, t, :], bank[4 + i][:], 1.0 / WS, x_res[:, t, :],
                                             ALU.mult, ALU.add).then_inc(d_acc, 1)

            shared_hidden(0)

            order = [0]

            def place(instruction):
                instruction.then_inc(d_place, 1)
                order[0] += 1
                dve.wait_ge(d_place, order[0])

            dve.wait_ge(d_counts, 1)
            place(dve.tensor_scalar(tiles_of[:], bank[7][:, NR:NR + EXPERTS], 1.0 / P, (P - 1.0) / P - 0.5 + 0.5 / P,
                                    ALU.mult, ALU.add))
            place(dve.tensor_scalar(tiles_of[:], tiles_of[:], 2.0 ** 23, -2.0 ** 23, ALU.add, ALU.add))
            place(dve.tensor_tensor(tiles_low[:], lower[:], tiles_of[:].unsqueeze(1).broadcast_to([P, EXPERTS, EXPERTS]), ALU.mult))
            place(dve.tensor_reduce(first_tile[:], tiles_low[:], AX.X, ALU.add))
            place(dve.tensor_tensor(end_tile[:], first_tile[:], tiles_of[:], ALU.add))
            place(dve.scalar_tensor_tensor(position[:], first_tile[:].unsqueeze(1).broadcast_to(per_tile), float(P),
                                           bank[7][:, 0:NR].rearrange("p (t e) -> p t e", e=EXPERTS), ALU.mult, ALU.add))
            for c in range(TOP_K):
                place(dve.scalar_tensor_tensor(picked[:, c], rank[:], float(c), position[:], ALU.is_equal, ALU.mult))
                place(dve.scalar_tensor_tensor(picked[:, TOP_K + c], rank[:], float(c), expert_w[:], ALU.is_equal, ALU.mult))
            place(dve.tensor_reduce(slot_f32[:], picked[:], AX.X, ALU.add))
            dve.tensor_copy(slot_u32[:], slot_f32[:, 0:TOP_K].rearrange("p c t -> p (c t)")).then_inc(d_slots, 1)
            sq = [1, SLOTS, EXPERTS]
            place(dve.tensor_tensor(tile_past[:], end_tile[0:1].unsqueeze(1).broadcast_to(sq),
                                    tile_no[:].unsqueeze(2).broadcast_to(sq), ALU.is_le))
            place(dve.tensor_reduce(tile_expert[:], tile_past[:], AX.X, ALU.add))
            place(dve.tensor_scalar(tile_expert[:], tile_expert[:], EXPERTS - 1.0, None, ALU.min))
            dve.tensor_scalar(tile_expert_i[:, 0], tile_expert[:], -1.0, EXPERTS - 1.0, ALU.mult, ALU.add).then_inc(d_tile_expert, 1)
            dve.tensor_scalar(tile_expert_i[:, 1], tile_expert[:], 1.0, None, ALU.add).then_inc(d_tile_expert, 1)

            for m in range(1, GROUPS):
                shared_hidden(m)
                shared_add(m - 1)
            shared_add(GROUPS - 1)

            def tile_x_lo(i):
                dve.wait_ge(t_xhi, i + 1)
                dve.tensor_tensor(xgT_lo[:].rearrange("p k c -> p (k c)"), bank[0][:], xgT_hi[:].rearrange("p k c -> p (k c)"),
                                  ALU.subtract).then_inc(t_xlo, 1)

            def tile_product(i):
                dve.wait_ge(t_silu, i + 1)
                dve.wait_ge(t_hT, room(t_hT, i))
                dve.scalar_tensor_tensor(th[:, 0:HID], bank[2][:, 0:HID], 1.0 / WS, tg[:], ALU.mult, ALU.mult).then_inc(t_h, 1)

            def tile_h_lo(i):
                dve.wait_ge(t_hhi, i + 1)
                dve.tensor_tensor(thT_lo[:].rearrange("p k c -> p (k c)"), bank[3][:, 0:3 * P],
                                  thT_hi[:].rearrange("p k c -> p (k c)"), ALU.subtract).then_inc(t_hlo, 1)

            dve.wait_ge(filled, 4)
            tile_x_lo(0)
            tile_product(0)
            tile_x_lo(1)
            tile_h_lo(0)
            with dve.Fori(1, SLOTS - 1) as i:
                tile_product(i)
                tile_x_lo(i + 1)
                tile_h_lo(i)
            tile_product(SLOTS - 1)
            tile_h_lo(SLOTS - 1)

            for n in range(TOP_K * TILES):
                t, c = n // TOP_K, n % TOP_K
                dve.wait_ge(y_gathered[n % YR], 16 * (n // YR) + 16)
                if c:
                    dve.wait_ge(y_added, n)
                dve.scalar_tensor_tensor(x_res[:, t, :], yg[:, n % YR, :], slot_f32[:, TOP_K + c, t:t + 1], x_res[:, t, :],
                                         ALU.mult, ALU.add).then_inc(y_added, 1)


INPUTS = ["x", "ctx_2048", "mask_BxS2_bk0", "L0_ffn_gate_w", "L0_ffn_up_w", "L0_ffn_down_w", "L0_ffn_gate_scale",
          "L0_ffn_up_scale", "L0_ffn_down_scale", "L1_xattn_Wh", "L1_xattn_wg_w", "L1_xattn_wo_w",
          "L1_xattn_gn_gamma", "L1_xattn_gn_beta", "L1_ffn_gate_w", "L1_ffn_w1", "L1_ffn_w2", "L1_ffn_sw1",
          "L1_ffn_sw2", "L1_ffn_sw3"]


def decay_table(heads, seq, head_dim):
    import numpy as np
    gam = (1.0 - 2.0 ** (-5.0 - np.arange(heads, dtype=np.float32))).astype(np.float32)
    idx = np.arange(seq, dtype=np.float32)
    expo = idx[None, :] - idx[:, None]
    d = np.where(expo[None] <= 0, gam[:, None, None].astype(np.float64) ** np.minimum(expo, 0)[None], 0.0)
    d = d / np.sqrt(d.sum(axis=-1))[:, None, :] / np.sqrt(float(head_dim))
    return np.ascontiguousarray(d.transpose(2, 0, 1).astype(np.float32))


def kernel(**inputs):
    import numpy as np
    import concourse.bacc as bacc
    from concourse import mybir as mb
    from concourse.bass_utils import run_bass_kernel_spmd

    nc = bacc.Bacc("TRN2", target_bir_lowering=False, num_devices=1)
    arrays, args = {}, []
    for name in INPUTS:
        a = np.ascontiguousarray(inputs[name])
        arrays["in_" + name] = a
        args.append(nc.dram_tensor("in_" + name, a.shape, mb.dt.from_np(a.dtype), kind="ExternalInput").ap())
    heads, head_dim = inputs["L1_xattn_Wh"].shape[:2]
    decay = decay_table(heads, inputs["x"].shape[1], head_dim)
    arrays["in_decay"] = decay
    args.append(nc.dram_tensor("in_decay", decay.shape, mb.dt.float32, kind="ExternalInput").ap())
    out = nc.dram_tensor("out_0", inputs["x"].shape, mb.dt.float32, kind="ExternalOutput").ap()
    build_decoder_pair(nc, *args, out)
    r = run_bass_kernel_spmd(nc, [arrays], core_ids=[0])
    return r.results[0]["out_0"]
```

```python
import concourse.bass as bass
from concourse import mybir
from contextlib import ExitStack


def build_decoder_pair(nc, x_in, ctx_in, mask_in, l0_gate, l0_up, l0_down, l0_gscale, l0_uscale, l0_dscale,
                       wh_in, wg_in, wo_in, gamma_in, beta_in, router_in, w1_in, w2_in, sw1_in, sw2_in, sw3_in,
                       decay_in, out):
    F32, F16 = mybir.dt.float32, mybir.dt.float16
    U8, U32, I32 = mybir.dt.uint8, mybir.dt.uint32, mybir.dt.int32
    ALU, ACT, AX = mybir.AluOpType, mybir.ActivationFunctionType, mybir.AxisListType

    P = 128
    BATCH, SEQ, DIM = x_in.shape
    CTX = ctx_in.shape[1]
    ROWT = SEQ // P
    TILES = BATCH * ROWT
    TOK = BATCH * SEQ
    KC = DIM // P
    GT = 4
    GW = GT * P
    GROUPS = TILES // GT
    FFN = l0_gate.shape[1]
    FC = FFN // P
    QW = 3 * DIM
    SCALE = float(DIM) ** -0.5
    LN_EPS = 1e-5
    HEADS = wh_in.shape[0]
    GN_EPS = 1e-3
    EXPERTS = w1_in.shape[0]
    HID = w2_in.shape[1]
    HC = [P, P, HID - 2 * P]
    UNIT = 2 * HID + 3 * P
    BLOCK = KC * 2 * UNIT
    TOP_K = 2
    SLOTS = (TOK * TOP_K + EXPERTS * (P - 1)) // P
    WS = 32.0
    MASKED = -1e32

    ctx_stack = ExitStack()
    with ctx_stack as top:
        def sb(scope, name, shape, dt):
            return scope.enter_context(nc.sbuf_tensor(name, shape, dt))

        free_at_start = {}

        def sem(name, free=0):
            s = top.enter_context(nc.semaphore(name))
            free_at_start[name] = (s, free)
            return s

        def done(s, n):
            return n + 1 + next(free for t, free in free_at_start.values() if t is s)

        def room(s, n):
            return n + 1

        ident = sb(top, "ident", [P, P], F32)
        ident16 = sb(top, "ident16", [P, P], F16)
        x_res = sb(top, "x_res", [P, TILES, DIM], F32)
        xn = sb(top, "xn", [P, GT, DIM], F32)
        stats = sb(top, "stats", [P, GT, 6], F32)
        meanvar = sb(top, "meanvar", [P, GT, 2], F32)
        vareps = sb(top, "vareps", [P, GT], F32)
        rstd = sb(top, "rstd", [P, GT], F32)
        zeros = sb(top, "zeros", [P, 2 * DIM], F16)
        minus_half = sb(top, "minus_half", [P, GT], F32)
        row_mean = sb(top, "row_mean", [P, TILES], F32)
        row_vareps = sb(top, "row_vareps", [P, TILES], F32)
        row_rstd = sb(top, "row_rstd", [P, TILES], F32)
        with ExitStack() as late:
            experts = sb(late, "experts", [P, EXPERTS, BLOCK], F16)
        with ExitStack() as late:
            xn_all = sb(late, "xn_all", [P, TILES, 2 * DIM], F16)
        ctxT = sb(top, "ctxT", [P, KC, TOK], F32)
        with ExitStack() as early:
            ctx_nat = sb(early, "ctx_nat", [P, TILES, DIM], F32)
        xT_hi = sb(top, "xT_hi", [P, KC, TOK], F16)
        xT_lo = sb(top, "xT_lo", [P, KC, TOK], F16)

        with ExitStack() as pairs:
            pair = [pairs.enter_context(nc.psum_tensor(f"pair{i}", [P, 2, 512], F32)) for i in range(4)]
        bank = [top.enter_context(nc.psum_tensor(f"bank{i}", [P, 512], F32)) for i in range(8)]

        ffn_w = ExitStack()
        RAW = 3
        raw = sb(ffn_w, "raw", [P, RAW, QW], F32)
        expo = sb(ffn_w, "expo", [P, QW], F32)
        wq = sb(ffn_w, "wq", [P, FC, QW], F16)
        gscale = sb(ffn_w, "gscale", [P, FC], F32)
        uscale = sb(ffn_w, "uscale", [P, FC], F32)
        dscale = sb(ffn_w, "dscale", [P, DIM], F32)

        att0 = ExitStack()
        ctx_stage = sb(att0, "ctx_stage", [P, ROWT, DIM], F32)
        xn0 = sb(att0, "xn0", [P, ROWT, DIM], F32)
        xnT0 = sb(att0, "xnT0", [P, KC, SEQ], F32)
        scores_sb = sb(att0, "scores_sb", [P, ROWT, CTX], F32)
        probs = sb(att0, "probs", [P, ROWT, CTX], F32)
        probsT = sb(att0, "probsT", [P, CTX // P, SEQ], F32)
        mask_u8 = sb(att0, "mask_u8", [P, BATCH, CTX], U8)
        maskbias = sb(att0, "maskbias", [P, BATCH, CTX], F32)
        valid = sb(att0, "valid", [P, BATCH], F32)
        rowmax = sb(att0, "rowmax", [P, ROWT], F32)
        negmax = sb(att0, "negmax", [P, ROWT], F32)
        rowsum = sb(att0, "rowsum", [P, ROWT], F32)
        rinv = sb(att0, "rinv", [P, ROWT], F32)
        rscale = sb(att0, "rscale", [P, ROWT], F32)
        att0.close()

        ffn = ExitStack()
        silu = sb(ffn, "silu", [P, 2, GW], F32)
        fused = sb(ffn, "fused", [P, 2, GW], F32)
        FR = 3
        fT_hi = sb(ffn, "fT_hi", [P, FR, GW], F16)
        fT_lo = sb(ffn, "fT_lo", [P, FR, GW], F16)
        down = sb(ffn, "down", [P, 2, DIM], F32)
        with ExitStack() as first:
            expo_odd = sb(first, "expo_odd", [P, QW], F32)
        unit_f32 = sb(ffn, "unit_f32", [P, 2, UNIT], F32)
        unit_split = sb(ffn, "unit_split", [P, 2, 2, UNIT], F16)
        ffn.close()
        ffn_w.close()

        ret = ExitStack()
        wgo_f32 = sb(ret, "wgo_f32", [P, 2, KC, DIM], F32)
        wh_f32 = sb(ret, "wh_f32", [P, HEADS, P], F32)
        wh_head = sb(ret, "wh_head", [P, P], F32)
        wh_hi = sb(ret, "wh_hi", [P, HEADS, P], F16)
        wh_lo = sb(ret, "wh_lo", [P, HEADS, P], F16)
        kT = sb(ret, "kT", [P, TOK], F32)
        v = sb(ret, "v", [P, TILES, P], F32)
        wgo_hi = sb(ret, "wgo_hi", [P, 2, KC, DIM], F16)
        wgo_lo = sb(ret, "wgo_lo", [P, 2, KC, DIM], F16)
        gamma = sb(ret, "gamma", [P, DIM], F32)
        beta = sb(ret, "beta", [P, DIM], F32)
        with ExitStack() as sw:
            sw12_f32 = sb(sw, "sw12_f32", [P, 2, len(HC), DIM], F32)
            sw3_f32 = sb(sw, "sw3_f32", [P, KC, HID], F32)
            router_f32 = sb(sw, "router_f32", [EXPERTS, DIM], F32)
        decay = sb(ret, "decay", [P, ROWT, HEADS, SEQ], F32)
        qT = sb(ret, "qT", [P, TOK], F32)
        scaled = sb(ret, "scaled", [P, SEQ + P], F32)
        floored = sb(ret, "floored", [P, SEQ + P], F32)
        weightT = sb(ret, "weightT", [P, ROWT, SEQ], F32)
        gn_stats = sb(ret, "gn_stats", [P, 6], F32)
        gn_meanvar = sb(ret, "gn_meanvar", [P, 2], F32)
        gn_mean = sb(ret, "gn_mean", [P, TILES], F32)
        gn_vareps = sb(ret, "gn_vareps", [P, TILES], F32)
        gn_rstd = sb(ret, "gn_rstd", [P, TILES], F32)
        y_norm = sb(ret, "y_norm", [P, DIM], F32)
        y_gamma = sb(ret, "y_gamma", [P, DIM], F32)
        y = sb(ret, "y", [P, DIM], F32)
        w_relu = sb(ret, "w_relu", [P, DIM], F32)
        z = sb(ret, "z", [P, DIM], F32)
        row_parts = sb(ret, "row_parts", [P, 2, DIM], F16)
        zT_hi = sb(ret, "zT_hi", [P, KC, P], F16)
        zT_lo = sb(ret, "zT_lo", [P, KC, P], F16)
        ret.close()

        shared = ExitStack()
        sw_split = sb(shared, "sw_split", [P, KC, 2, UNIT], F16)
        hg = sb(shared, "hg", [P, 2, GW], F32)
        hp = sb(shared, "hp", [P, 2, GW], F32)
        hT_hi = sb(shared, "hT_hi", [P, 2, len(HC), GW], F16)
        hT_lo = sb(shared, "hT_lo", [P, 2, len(HC), GW], F16)
        shared.close()
        moe = ExitStack()
        sb(moe, "experts_room", [P, (EXPERTS * BLOCK - 4 * KC * TOK) // 2], F32)
        prob = sb(moe, "prob", [P, TILES, EXPERTS], F32)
        prob_max = sb(moe, "prob_max", [P, TILES], F32)
        prob_sum = sb(moe, "prob_sum", [P, TILES], F32)
        above = xn[:, 0:2, :].rearrange("p a (b e j) -> p (a b) e j", e=EXPERTS, j=EXPERTS)
        tied = xn[:, 2:4, :].rearrange("p a (b e j) -> p (a b) e j", e=EXPERTS, j=EXPERTS)
        lower = sb(moe, "lower", [P, EXPERTS, EXPERTS], F32)
        rank = sb(moe, "rank", [P, TILES, EXPERTS], F32)
        expert_w = sb(moe, "expert_w", [P, TILES, EXPERTS], F32)
        chosen = sb(moe, "chosen", [P, TILES * EXPERTS], F16)
        before = sb(moe, "before", [P, P], F16)
        ones16 = sb(moe, "ones16", [P, P], F16)
        tiles_of = sb(moe, "tiles_of", [P, EXPERTS], F32)
        tiles_low = sb(moe, "tiles_low", [P, EXPERTS, EXPERTS], F32)
        first_tile = sb(moe, "first_tile", [P, EXPERTS], F32)
        end_tile = sb(moe, "end_tile", [P, EXPERTS], F32)
        position = sb(moe, "position", [P, TILES, EXPERTS], F32)
        picked = sb(moe, "picked", [P, 2 * TOP_K, TILES, EXPERTS], F32)
        slot_f32 = sb(moe, "slot_f32", [P, 2 * TOP_K, TILES], F32)
        slot_u32 = sb(moe, "slot_u32", [P, TOP_K * TILES], U32)
        tile_no = sb(moe, "tile_no", [1, SLOTS], F32)
        tile_past = sb(moe, "tile_past", [1, SLOTS, EXPERTS], F32)
        tile_expert = sb(moe, "tile_expert", [1, SLOTS], F32)
        tile_expert_i = sb(moe, "tile_expert_i", [1, SLOTS], I32)
        router_hi = sb(moe, "router_hi", [P, KC, EXPERTS], F16)
        router_lo = sb(moe, "router_lo", [P, KC, EXPERTS], F16)
        XR = 3
        xg = sb(moe, "xg", [P, XR, 2, DIM], F16)
        xgT_hi = sb(moe, "xgT_hi", [P, KC, P], F16)
        xgT_lo = sb(moe, "xgT_lo", [P, KC, P], F16)
        tg = sb(moe, "tg", [P, HID], F32)
        th = sb(moe, "th", [P, 3 * P], F32)
        th_parts = sb(moe, "th_parts", [P, 2, 3 * P], F16)
        thT_hi = sb(moe, "thT_hi", [P, 3, P], F16)
        thT_lo = sb(moe, "thT_lo", [P, 3, P], F16)
        ty = sb(moe, "ty", [P, XR, DIM], F32)
        YR = 4
        yg = xn
        moe.close()
        split_w = nc.dram_tensor("split_w", (EXPERTS, KC, P, 2 * UNIT), F16).ap()
        row_store = nc.dram_tensor("row_store", (TOK, 2 * DIM), F16).ap()
        sorted_x = nc.dram_tensor("sorted_x", (SLOTS * P, 2 * DIM), F16).ap()
        sorted_y = nc.dram_tensor("sorted_y", (SLOTS * P, DIM), F32).ap()

        ident_zero, ident_ready = sem("ident_zero"), sem("ident_ready")
        mask_loaded = sem("mask_loaded")
        loads = [sem(f"loads{i}") for i in range(max(BATCH, EXPERTS))]
        batches_loaded = sem("batches_loaded")
        a_stats, a_meanvar, a_vareps, a_rstd, a_xn = (sem("a_" + n) for n in ("stats", "meanvar", "vareps", "rstd", "xn"))
        a_xnT_psum, a_ctxT_psum, a_xnT, a_ctxT = (sem("a_" + n, 1) for n in ("xnT_psum", "ctxT_psum", "xnT", "ctxT"))
        a_ctx_staged = sem("a_ctx_staged")
        a_bias, a_valid, a_rowmax, a_negmax, a_rscale = (
            sem("a_" + n) for n in ("bias", "valid", "rowmax", "negmax", "rscale"))
        a_scores, a_masked, a_probs, a_probsT_psum, a_probsT, a_readout, a_rinv, a_resid = (
            sem("a_" + n, 1) for n in ("scores", "masked", "probs", "probsT_psum", "probsT", "readout", "rinv", "resid"))
        out_stored = sem("out_stored")
        weights_loaded, c_hi, c_lo = sem("weights_loaded"), sem("c_hi"), sem("c_lo")
        c_head = sem("c_head")
        c_proj, c_copied = sem("c_proj"), sem("c_copied", 4)
        c_scores, c_masked, c_scaled, c_weights = sem("c_scores", 1), sem("c_masked", 1), sem("c_scaled"), sem("c_weights")
        c_o_ps, c_o_copied = sem("c_o_ps", 4), sem("c_o_copied", 2)
        g_stats, g_meanvar, g_vareps, g_rstd = (sem("g_" + n) for n in ("stats", "meanvar", "vareps", "rstd"))
        g_w_ps, g_w, g_ynorm, g_ygamma, g_y = (sem("g_" + n, free) for n, free in (
            ("w_ps", 0), ("w", 1), ("ynorm", 0), ("ygamma", 1), ("y", 0)))
        g_z, g_zT_ps, g_hi, g_lo, g_wo, g_resid = (
            sem("g_z", 1), sem("g_zT_ps", 1), sem("g_hi"), sem("g_lo", 1), sem("g_wo", 1), sem("g_resid", 1))

        def norm_sems(t):
            return {n: sem(f"{t}_{n}", free) for n, free in (("stats", 0), ("meanvar", 0), ("vareps", 0), ("rstd", 0),
                                                             ("xn", 0), ("xT_psum", 1), ("hi", 0), ("lo", 1))}
        nb = norm_sems("b")
        nr = {n: sem("r_" + n) for n in ("stats", "meanvar", "vareps", "rstd", "xn")}
        nr |= {n: nb[n] for n in ("xT_psum", "hi", "lo")}
        nd = norm_sems("d")
        u_loaded, u_stored = [sem(f"u_loaded{i}") for i in range(2)], [sem(f"u_stored{i}", 16) for i in range(2)]
        u_hi, u_lo = sem("u_hi"), sem("u_lo", 2)
        filled, d_filled = sem("filled"), sem("d_filled")
        d_sw_ps, d_sw_hi, d_sw_lo = sem("d_sw_ps"), sem("d_sw_hi"), sem("d_sw_lo", 4)
        d_ones, d_const = sem("d_ones"), sem("d_const")
        d_logits, d_route, d_exp, d_weights = (sem("d_" + n) for n in ("logits", "route", "exp", "weights"))
        d_place = sem("d_place")
        d_chosen, d_counts, d_slots, d_tile_expert = (sem("d_" + n) for n in ("chosen", "counts", "slots", "tile_expert"))
        d_scattered = sem("d_scattered")
        d_gate_ps, d_up_ps, d_silu = (sem("d_" + n) for n in ("gate_ps", "up_ps", "silu"))
        d_prod, d_hhi, d_hlo = sem("d_prod", 2), sem("d_hhi"), sem("d_hlo", 2)
        d_y_ps, d_acc = sem("d_y_ps", 2 * GT), sem("d_acc", GT)
        experts_loaded = sem("experts_loaded", 32)
        row_hi, row_lo, row_stored = sem("row_hi"), sem("row_lo", 1), sem("row_stored", 16)
        t_thi, t_tlo = sem("t_thi"), sem("t_tlo", 1)
        t_y_stored = [sem(f"t_y_stored{i}", 16) for i in range(3)]
        t_xT, t_xhi, t_xlo, t_gu, t_silu = sem("t_xT"), sem("t_xhi"), sem("t_xlo", 1), sem("t_gu"), sem("t_silu")
        t_h, t_hT, t_hhi, t_hlo = sem("t_h", 1), sem("t_hT", 1), sem("t_hhi"), sem("t_hlo", 1)
        t_y, t_ycopy = sem("t_y"), sem("t_ycopy", 1)
        y_gathered = [sem(f"y_gathered{i}") for i in range(4)]
        y_added = sem("y_added")

        ring_loaded = [sem(f"ring_loaded{i}") for i in range(RAW)]
        scales_loaded = sem("scales_loaded")
        w_step = sem("w_step")
        w_quant = sem("w_quant", 1)
        b_gate_ps, b_up_ps, b_silu, b_flo, b_resid = (sem("b_" + n) for n in ("gate_ps", "up_ps", "silu", "flo", "resid"))
        b_fused, b_fhi, b_down = sem("b_fused", 2), sem("b_fhi", 2), sem("b_down", FR)
        b_scaled = sem("b_scaled", GT)

        AFTER_B, AFTER_C = (4, 5), (8, 9)

        def ffn_items(g, b_rows, c_rows):
            n = 0 if isinstance(g, int) and g == 0 else g * (FC + 4) - 2
            i = 0
            for c in range(FC):
                yield "chunk", c, n, i % 2
                n, i = n + 1, i + 1
                if b_rows and c in AFTER_B:
                    yield "b", AFTER_B.index(c), n, i % 2
                    n, i = n + 1, i + 1
                if c_rows and c in AFTER_C:
                    yield "c", AFTER_C.index(c), n, i % 2
                    n, i = n + 1, i + 1

        def gate_chunk(i):
            return l0_gate.rearrange("(k p) f -> p k f", p=P)[:, :, i * P:(i + 1) * P]

        def up_chunk(i):
            return l0_up.rearrange("(k p) f -> p k f", p=P)[:, :, i * P:(i + 1) * P]

        waits_passed = sem("waits_passed")

        def hold(engine, semaphore, value):
            engine.wait_ge(semaphore, value)
            engine.sem_inc(waits_passed, 1)

        def inside(t):
            return not isinstance(t, int) or 0 <= t < TILES

        def sw_units():
            for t in range(2):
                for k in range(KC):
                    at = slice(t * HID, (t + 1) * HID)
                    yield bank[4 + (t * KC + k) % 4][:, 0:HID], sw_split[:, k, 0, at], sw_split[:, k, 1, at]
            for c, rows in enumerate(HC):
                at = slice(2 * HID + c * P, 2 * HID + (c + 1) * P)
                yield (bank[4 + (2 * KC + c) % 4][0:rows, :].rearrange("r (k n) -> r k n", n=P),
                       sw_split[0:rows, :, 0, at], sw_split[0:rows, :, 1, at])
            yield (bank[4 + (2 * KC + len(HC)) % 4][:, 0:KC * EXPERTS].rearrange("p (k e) -> p k e", e=EXPERTS),
                   router_hi[:], router_lo[:])

        def units_of_step(t):
            n = t - (TILES - 1)
            return range(3 * n, min(3 * n + 3, 2 * KC + len(HC)))

        block = top.enter_context(nc.Block())

        @block.sync
        def _(sp):
            for s, free in free_at_start.values():
                if free:
                    sp.sem_inc(s, free)
            xv = x_in.rearrange("b (j p) d -> b p j d", p=P)
            cv = ctx_in.rearrange("b (j p) d -> b p j d", p=P)
            sp.dma_start(mask_u8[:], mask_in.partition_broadcast(P)).then_inc(mask_loaded, 16)
            for b in range(BATCH):
                sp.dma_start(x_res[:, ROWT * b:ROWT * (b + 1), :], xv[b]).then_inc(loads[b], 16)
                sp.dma_start(ctx_nat[:, ROWT * b:ROWT * (b + 1), :], cv[b]).then_inc(loads[b], 16)
            for b in range(BATCH):
                sp.wait_ge(loads[b], 32)
                sp.sem_inc(batches_loaded, 1)
            sp.dma_start(gscale[:], l0_gscale.rearrange("(c p) -> p c", p=P),
                         allow_slow_non_contiguous=True).then_inc(scales_loaded, 16)
            sp.dma_start(uscale[:], l0_uscale.rearrange("(c p) -> p c", p=P),
                         allow_slow_non_contiguous=True).then_inc(scales_loaded, 16)
            sp.dma_start(dscale[:], l0_dscale.partition_broadcast(P)).then_inc(scales_loaded, 16)

            def load_raw(i):
                slot = i % RAW
                rv = raw[:, slot, 0:2 * DIM].rearrange("p (t k f) -> p t k f", t=2, f=P)
                sp.dma_start(rv[:, 0], gate_chunk(i)).then_inc(ring_loaded[slot], 16)
                sp.dma_start(rv[:, 1], up_chunk(i)).then_inc(ring_loaded[slot], 16)
                sp.dma_start(raw[:, slot, 2 * DIM:QW], l0_down[i * P:(i + 1) * P, :]).then_inc(ring_loaded[slot], 16)
            for i in range(RAW):
                load_raw(i)

            def store_unit(e2, u):
                slot, k = u % 2, u % KC
                sp.wait_ge(u_lo, done(u_lo, e2 * 8 + u))
                dst = split_w.rearrange("(a b) k p u -> b k p a u", b=2)[u // KC, k, :, e2]
                sp.dma_start(dst, unit_split[:, slot].rearrange("p s u -> p (s u)")).then_inc(u_stored[slot], 16)
            for slot in range(RAW):
                sp.wait_ge(ring_loaded[slot], 48)
                sp.sem_inc(batches_loaded, 1)
            for i in range(RAW, FC):
                sp.wait_ge(w_quant, done(w_quant, i - RAW))
                load_raw(i)
            sp.wait_ge(w_quant, done(w_quant, FC - 1))
            sp.dma_start(wh_f32[:], wh_in.rearrange("h d e -> d h e")).then_inc(weights_loaded, 16)
            sp.dma_start(wgo_f32[:, 0], wg_in.rearrange("(k p) n -> p k n", p=P)).then_inc(weights_loaded, 16)
            sp.dma_start(wgo_f32[:, 1], wo_in.rearrange("(k p) n -> p k n", p=P)).then_inc(weights_loaded, 16)
            sp.wait_ge(filled, 2)
            with sp.Fori(0, EXPERTS * KC // 8) as e2:
                for u in range(8):
                    slot, k = u % 2, u % KC
                    sp.wait_ge(u_lo, room(u_lo, e2 * 8 + u))
                    w1e = w1_in.rearrange("(a b) (k p) f -> p b k a f", b=2, p=P)[:, u // KC, k, e2]
                    w2e = w2_in.rearrange("(a b) i n -> b i a n", b=2)[u // KC, :, e2, k * P:(k + 1) * P]
                    sp.dma_start(unit_f32[:, slot, 0:2 * HID], w1e).then_inc(u_loaded[slot], 16)
                    sp.dma_start(unit_f32[:, slot, 2 * HID:2 * HID + 2 * P].rearrange("p (c n) -> p c n", n=P),
                                 w2e[0:2 * P].rearrange("(c p) n -> p c n", p=P)).then_inc(u_loaded[slot], 16)
                    sp.dma_start(unit_f32[0:HC[2], slot, 2 * HID + 2 * P:UNIT], w2e[2 * P:HID]).then_inc(u_loaded[slot], 16)
                    if u:
                        store_unit(e2, u - 1)
                store_unit(e2, 7)
            sp.wait_ge(b_resid, TILES)
            sp.dma_start(decay[:], decay_in.rearrange("(j p) h s -> p j h s", p=P)).then_inc(weights_loaded, 16)
            sp.dma_start(gamma[:], gamma_in.partition_broadcast(P)).then_inc(weights_loaded, 16)
            sp.dma_start(beta[:], beta_in.partition_broadcast(P)).then_inc(weights_loaded, 16)
            sp.wait_ge(filled, 1)
            for i in range(3):
                n = SLOTS // 3
                sp.dma_start(sorted_x[i * n * P:(i + 1) * n * P, :].rearrange("(a p) d -> p a d", p=P),
                             zeros[:].unsqueeze(1).broadcast_to([P, n, 2 * DIM])).then_inc(d_filled, 16)
            sp.wait_ge(c_o_ps, done(c_o_ps, 4 * HEADS - 1))

            def hidden_rows(dst, src):
                sp.dma_start(dst[:, 0:2, :], src[0:2 * P, :].rearrange("(c p) n -> p c n", p=P)).then_inc(weights_loaded, 16)
                sp.dma_start(dst[0:HC[2], 2, :], src[2 * P:HID, :]).then_inc(weights_loaded, 16)
            sp.dma_start(router_f32[:], router_in).then_inc(weights_loaded, 16)
            hidden_rows(sw12_f32[:, 0], sw1_in)
            hidden_rows(sw12_f32[:, 1], sw2_in)
            sp.dma_start(sw3_f32[:], sw3_in.rearrange("(k p) n -> p k n", p=P)).then_inc(weights_loaded, 16)
            with sp.Fori(0, TILES) as t:
                sp.wait_ge(row_lo, done(row_lo, t))
                sp.dma_start(row_store[bass.ds(t * P, P), :], row_parts[:].rearrange("p s d -> p (s d)")).then_inc(row_stored, 16)
            sp.wait_ge(row_stored, 16 * TILES + 16)
            sp.dma_start(xn_all[:], row_store.rearrange("(t p) d -> p t d", p=P)).then_inc(d_filled, 16)
            sp.wait_ge(d_sw_lo, done(d_sw_lo, 11))
            for i in range(2):
                sp.wait_ge(u_stored[i], 16 * (EXPERTS * KC // 2 + 1))
            for e in range(2):
                sp.dma_start(experts[:, EXPERTS - 1 - e, :].rearrange("p (k u) -> p k u", k=KC),
                             split_w[e].rearrange("k p u -> p k u")).then_inc(loads[e], 16)

            def load_tile(i, slot, lap):
                if lap is not None:
                    sp.wait_ge(t_xT, i - XR + 1)
                sp.dma_start(xg[:, slot].rearrange("p s d -> p (s d)"), sorted_x[bass.ds(i * P, P), :]).then_inc(ring_loaded[slot], 16)

            def store_tile(i, slot):
                sp.wait_ge(t_ycopy, done(t_ycopy, i))
                sp.dma_start(sorted_y[bass.ds(i * P, P), :], ty[:, slot, :]).then_inc(t_y_stored[slot], 16)

            sp.wait_ge(d_scattered, 16 * TOP_K * TILES)
            for i in range(XR):
                load_tile(i, i, None)
            with sp.Fori(0, SLOTS // XR - 1) as lap:
                for slot in range(XR):
                    load_tile(lap * XR + (XR + slot), slot, lap)
                    store_tile(lap * XR + slot, slot)
            for slot in range(XR):
                store_tile(SLOTS - XR + slot, slot)
            ov = out.rearrange("b (j p) d -> p (b j) d", p=P)
            for t in range(TILES):
                sp.wait_ge(y_added, TOP_K * t + TOP_K)
                sp.dma_start(ov[:, t, :], x_res[:, t, :]).then_inc(out_stored, 16)
            sp.wait_ge(out_stored, 16 * TILES)

        @block.gpsimd
        def _(pool):
            pool.memset(ident[:], 0.0).then_inc(ident_zero, 1)
            pool.memset(minus_half[:], -0.5).then_inc(ident_zero, 1)
            pool.memset(zeros[:], 0.0).then_inc(filled, 1)
            pool.wait_ge(ident_zero, 1)
            pool.affine_select(out=ident[:], in_=ident[:], compare_op=ALU.not_equal, fill=1.0, base=0,
                               pattern=[[-1, P]], channel_multiplier=1).then_inc(ident_ready, 1)
            pool.wait_ge(ident_ready, 1)
            pool.tensor_copy(ident16[:], ident[:]).then_inc(ident_ready, 1)
            pool.wait_ge(ident_zero, 2)

            def inverse_deviation(n, s_meanvar, s_vareps, s_rstd, width):
                hold(pool, s_meanvar, n + 1)
                pool.tensor_scalar(vareps[:, 0:width], meanvar[:, 0:width, 1], LN_EPS, None, ALU.add).then_inc(s_vareps, 1)
                pool.wait_ge(s_vareps, n + 1)
                pool.tensor_tensor(rstd[:, 0:width], vareps[:, 0:width], minus_half[:, 0:width], ALU.pow).then_inc(s_rstd, 1)

            with pool.Fori(0, BATCH) as b:
                pool.wait_ge(batches_loaded, b + 1)
                inverse_deviation(b, a_meanvar, a_vareps, a_rstd, ROWT)
                pool.wait_ge(a_ctxT_psum, room(a_ctxT_psum, b))
                pool.tensor_copy(ctx_stage[:], ctx_nat[:, bass.ds(ROWT * b, ROWT), :]).then_inc(a_ctx_staged, 1)

            def group_inverse(g, s):
                inverse_deviation(g, s["meanvar"], s["vareps"], s["rstd"], GT)
            group_inverse(0, nb)
            pool.wait_ge(a_resid, done(a_resid, BATCH - 1))
            def quantise_last(i):
                pool.wait_ge(w_step, i * 3 + 3)
                pool.tensor_tensor(wq[:, i, :], raw[:, i % RAW, :], (expo, expo_odd)[i % 2][:], ALU.subtract).then_inc(w_quant, 1)
            for i in range(RAW + 1, RAW + 4):
                quantise_last(i)
            group_inverse(1, nb)
            for i in range(RAW + 4, FC):
                quantise_last(i)
            pool.wait_ge(w_quant, done(w_quant, FC - 1))
            pool.memset(unit_f32[:], 0.0).then_inc(filled, 1)
            with pool.Fori(1, GROUPS - 1) as g:
                group_inverse(g + 1, nb)
                group_inverse(g - 1, nr)
            group_inverse(GROUPS - 2, nr)
            pool.wait_ge(weights_loaded, 48)
            pool.tensor_copy(wh_head[:], wh_f32[:, 0, :]).then_inc(c_head, 1)
            group_inverse(GROUPS - 1, nr)
            pool.wait_ge(b_resid, TILES)
            pool.memset(weightT[:], 1.0).then_inc(filled, 1)
            with pool.Fori(1, HEADS) as h:
                hold(pool, c_proj, h * 12 - 8)
                pool.tensor_copy(wh_head[:], wh_f32[:, h, :]).then_inc(c_head, 1)

            def group_deviation(t):
                pool.wait_ge(g_vareps, t + 1)
                pool.tensor_tensor(gn_rstd[:, bass.ds(t, 1)], gn_vareps[:, bass.ds(t, 1)], minus_half[:, 0:1], ALU.pow).then_inc(g_rstd, 1)

            def gamma_beta(t):
                pool.wait_ge(g_ynorm, t + 1)
                pool.tensor_tensor(y_gamma[:], y_norm[:], gamma[:], ALU.mult).then_inc(g_ygamma, 1)
                pool.wait_ge(g_z, room(g_z, t))
                hold(pool, g_ygamma, done(g_ygamma, t))
                pool.tensor_tensor(y[:], y_gamma[:], beta[:], ALU.add).then_inc(g_y, 1)

            def row_deviation(t):
                pool.wait_ge(nd["vareps"], t + 1)
                pool.tensor_tensor(row_rstd[:, bass.ds(t, 1)], row_vareps[:, bass.ds(t, 1)], minus_half[:, 0:1], ALU.pow).then_inc(nd["rstd"], 1)

            group_deviation(0)
            group_deviation(1)
            gamma_beta(0)

            def tile_steps(t):
                if inside(t + 1):
                    gamma_beta(t + 1)
                if inside(t + 2):
                    group_deviation(t + 2)
                if inside(t - 1):
                    row_deviation(t - 1)

            tile_steps(0)
            with pool.Fori(1, TILES - 2) as t:
                tile_steps(t)
            for t in range(TILES - 2, TILES + 1):
                tile_steps(t)
            pool.wait_ge(g_resid, done(g_resid, TILES - 1))
            pool.wait_ge(d_sw_ps, 12)
            pool.memset(lower[:], 1.0).then_inc(d_ones, 1)
            pool.memset(before[:], 1.0).then_inc(d_ones, 1)
            pool.wait_ge(d_ones, 2)
            pool.affine_select(out=lower[:], in_=lower[:], compare_op=ALU.is_gt, fill=0.0, base=0,
                               pattern=[[1, EXPERTS], [-1, EXPERTS]], channel_multiplier=0).then_inc(d_const, 1)
            pool.affine_select(out=before[:], in_=before[:], compare_op=ALU.is_gt, fill=0.0, base=0,
                               pattern=[[1, P]], channel_multiplier=-1).then_inc(d_const, 1)
            pool.memset(ones16[:], 1.0).then_inc(d_const, 1)
            pool.iota(tile_no[:], [[1, SLOTS]], base=0, channel_multiplier=0,
                      allow_small_or_imprecise_dtypes=True).then_inc(d_const, 1)

            pool.wait_ge(d_filled, 48 + 16)
            pool.wait_ge(d_slots, 1)
            for t in range(TILES):
                for c in range(TOP_K):
                    at = c * TILES + t
                    pool.indirect_dma_start(
                        sorted_x, bass.IndirectOffsetOnAxis(slot_u32[:, at:at + 1], 0), xn_all[:, t, :], None,
                    ).then_inc(d_scattered, 16)
            pool.wait_ge(d_sw_lo, done(d_sw_lo, 11))
            pool.memset(th[:], 0.0).then_inc(filled, 1)
            for i in range(XR):
                pool.wait_ge(t_y_stored[i], 16 * (SLOTS // XR + 1))
            for n in range(TOP_K * TILES):
                t, c = n // TOP_K, n % TOP_K
                if n >= YR:
                    pool.wait_ge(y_added, n - YR + 1)
                at = c * TILES + t
                pool.indirect_dma_start(
                    yg[:, n % YR, :], None, sorted_y, bass.IndirectOffsetOnAxis(slot_u32[:, at:at + 1], 0),
                ).then_inc(y_gathered[n % YR], 16)

        @block.tensor
        def _(pe):
            pe.wait_ge(ident_ready, 1)

            def transpose_parts(to, parts, k):
                for part in range(2):
                    last = pe.matmul(to, parts[:, part, k * P:(k + 1) * P], ident16[:], start=(part == 0), stop=(part == 1))
                return last

            def transpose_inputs(b):
                pe.wait_ge(a_xn, b + 1)
                pe.wait_ge(a_xnT, room(a_xnT, b))
                for j in range(ROWT):
                    for k in range(KC):
                        last = pe.transpose(pair[0][:, j, k * P:(k + 1) * P], xn0[:, j, k * P:(k + 1) * P], ident[:])
                last.then_inc(a_xnT_psum, 1)
                pe.wait_ge(a_ctx_staged, b + 1)
                pe.wait_ge(a_ctxT, room(a_ctxT, b))
                for j in range(ROWT):
                    for k in range(KC):
                        last = pe.transpose(pair[1][:, j, k * P:(k + 1) * P],
                                            ctx_stage[:, j, k * P:(k + 1) * P], ident[:])
                last.then_inc(a_ctxT_psum, 1)

            def score(b):
                pe.wait_ge(a_xnT, done(a_xnT, b))
                pe.wait_ge(a_ctxT, done(a_ctxT, b))
                pe.wait_ge(a_masked, room(a_masked, b))
                for j in range(ROWT):
                    for k in range(KC):
                        last = pe.matmul(bank[4][:, j * CTX:(j + 1) * CTX], xnT0[:, k, j * P:(j + 1) * P],
                                         ctxT[:, k, bass.ds(b * CTX, CTX)], start=(k == 0), stop=(k == KC - 1))
                last.then_inc(a_scores, 1)

            def transpose_probs(b):
                pe.wait_ge(a_probs, done(a_probs, b))
                pe.wait_ge(a_probsT, room(a_probsT, b))
                for m in range(CTX // P):
                    for j in range(ROWT):
                        last = pe.transpose(bank[5][:, m * SEQ + j * P:m * SEQ + (j + 1) * P],
                                            probs[:, j, m * P:(m + 1) * P], ident[:])
                last.then_inc(a_probsT_psum, 1)

            def read_out(b):
                pe.wait_ge(a_probsT, done(a_probsT, b))
                pe.wait_ge(a_resid, room(a_resid, b))
                for j in range(ROWT):
                    for m in range(CTX // P):
                        last = pe.matmul(bank[6 + j][:], probsT[:, m, j * P:(j + 1) * P],
                                         ctx_nat[:, ROWT * b + m, :], start=(m == 0), stop=(m == CTX // P - 1))
                last.then_inc(a_readout, 1)

            transpose_inputs(0)
            score(0)
            transpose_inputs(1)
            transpose_probs(0)
            with pe.Fori(1, BATCH - 1) as b:
                score(b)
                transpose_inputs(b + 1)
                read_out(b - 1)
                transpose_probs(b)
            score(BATCH - 1)
            read_out(BATCH - 2)
            transpose_probs(BATCH - 1)

            def transpose_group(g, s):
                for i in range(GT):
                    if i % 2 == 0:
                        pe.wait_ge(s["xn"], 2 * g + i // 2 + 1)
                    for k in range(KC):
                        last = pe.transpose(pair[i // 2][:, i % 2, k * P:(k + 1) * P], xn[:, i, k * P:(k + 1) * P], ident[:])
                    if i % 2:
                        last.then_inc(s["xT_psum"], 1)

            transpose_group(0, nb)
            read_out(BATCH - 1)

            def gate_up(g, c, n, slot):
                pe.wait_ge(w_quant, done(w_quant, c))
                pe.wait_ge(b_fused, room(b_fused, n))
                for t, (at, signal) in enumerate(((slot, b_gate_ps), (2 + slot, b_up_ps))):
                    for k in range(KC):
                        for part in (xT_hi, xT_lo):
                            last = pe.matmul(bank[at][:], wq[:, c, (t * KC + k) * P:(t * KC + k + 1) * P],
                                             part[:, k, bass.ds(g * GW, GW)],
                                             start=(k == 0 and part is xT_hi), stop=(k == KC - 1 and part is xT_lo))
                    last.then_inc(signal, 1)

            def transpose_half(g, half, s, n, slot):
                pe.wait_ge(s["xn"], g * 2 + (half + 1))
                pe.wait_ge(b_fused, room(b_fused, n))
                for at, i, signal in ((slot, 2 * half, b_gate_ps), (2 + slot, 2 * half + 1, b_up_ps)):
                    for k in range(KC):
                        last = pe.transpose(bank[at][:, k * P:(k + 1) * P], xn[:, i, k * P:(k + 1) * P], ident[:])
                    last.then_inc(signal, 1)

            def down_chunk(g, c):
                n = g * FC + c
                pe.wait_ge(b_fhi, done(b_fhi, n))
                pe.wait_ge(b_flo, n + 1)
                for i in range(GT):
                    if c == 0:
                        pe.wait_ge(b_scaled, room(b_scaled, GT * g + i))
                    for part in (fT_hi, fT_lo):
                        last = pe.matmul(bank[4 + i][:], part[:, c % FR, i * P:(i + 1) * P],
                                         wq[:, c, 2 * DIM:QW], start=(c == 0 and part is fT_hi),
                                         stop=(c == FC - 1 and part is fT_lo))
                last.then_inc(b_down, 1)

            def ffn_group(g, b_rows=True, c_rows=True):
                for kind, c, n, slot in ffn_items(g, b_rows, c_rows):
                    if kind == "b":
                        transpose_half(g + 1, c, nb, n, slot)
                    elif kind == "c":
                        transpose_half(g - 1, c, nr, n, slot)
                    else:
                        gate_up(g, c, n, slot)
                        if c:
                            down_chunk(g, c - 1)
                        elif c_rows:
                            down_chunk(g - 1, FC - 1)

            pe.wait_ge(nb["lo"], done(nb["lo"], 0))
            ffn_group(0, c_rows=False)
            with pe.Fori(1, GROUPS - 1) as g:
                ffn_group(g)
            ffn_group(GROUPS - 1, b_rows=False)
            down_chunk(GROUPS - 1, FC - 1)

            def keys(h):
                pe.wait_ge(c_head, h + 1)
                for i in range(GROUPS):
                    pe.wait_ge(c_copied, room(c_copied, h * 12 + i))
                    pe.matmul(bank[i][:], wh_head[:], ctxT[:, h, i * GW:(i + 1) * GW],
                              start=True, stop=True).then_inc(c_proj, 1)

            def values(h):
                for i in range(GROUPS):
                    pe.wait_ge(c_copied, done(c_copied, h * 12 + i))
                    for j in range(GT):
                        last = pe.transpose(bank[i][:, j * P:(j + 1) * P], kT[:, (GT * i + j) * P:(GT * i + j + 1) * P], ident[:])
                    last.then_inc(c_proj, 1)

            def queries_scores(h):
                for i in range(GROUPS):
                    pe.wait_ge(c_copied, room(c_copied, h * 12 + 8 + i))
                    for n, (w, part) in enumerate(((wh_hi, xT_hi), (wh_hi, xT_lo), (wh_lo, xT_hi))):
                        last = pe.matmul(bank[i][:], w[:, h, :], part[:, h, i * GW:(i + 1) * GW],
                                         start=(n == 0), stop=(n == 2))
                    last.then_inc(c_proj, 1)
                pe.wait_ge(c_copied, done(c_copied, h * 12 + 11))
                pe.wait_ge(c_masked, room(c_masked, h))
                for b in range(BATCH):
                    pe.matmul(bank[4][:, 0:SEQ], kT[:, b * SEQ:b * SEQ + P], qT[:, b * SEQ:(b + 1) * SEQ],
                              start=(b == 0), stop=(b == BATCH - 1))
                for b in range(BATCH):
                    last = pe.matmul(bank[5][:, 0:P], kT[:, b * SEQ + P:(b + 1) * SEQ], qT[:, b * SEQ + P:(b + 1) * SEQ],
                                     start=(b == 0), stop=(b == BATCH - 1))
                last.then_inc(c_scores, 1)

            def outputs(h):
                pe.wait_ge(c_weights, h + 1)
                vv = v[:].rearrange("p (b j) e -> p j b e", j=ROWT)
                for j in range(ROWT):
                    for half in range(2):
                        o = 2 * j + half
                        pe.wait_ge(c_o_copied, room(c_o_copied, h * 4 + o))
                        for m in range(ROWT):
                            last = pe.matmul(bank[6 + half][:], weightT[:, m, j * P:(j + 1) * P],
                                             vv[:, m, 4 * half:4 * half + 4, :], start=(m == 0), stop=(m == ROWT - 1))
                        last.then_inc(c_o_ps, 1)

            keys(0)
            values(0)
            pe.wait_ge(c_copied, done(c_copied, 7))
            transpose_group(GROUPS - 1, nr)
            pe.wait_ge(nr["lo"], done(nr["lo"], 1))
            pe.wait_ge(c_lo, 1)
            pe.wait_ge(b_scaled, done(b_scaled, TILES - 1))
            pe.wait_ge(filled, 3)
            queries_scores(0)
            with pe.Fori(1, HEADS) as h:
                keys(h)
                outputs(h - 1)
                values(h)
                queries_scores(h)

            def gate_project(t):
                pe.wait_ge(g_w, room(g_w, t))
                for k in range(KC):
                    tok = bass.ds(t * P, P)
                    for n, (part, w) in enumerate(((xT_hi, wgo_hi), (xT_hi, wgo_lo), (xT_lo, wgo_hi))):
                        last = pe.matmul(bank[0][:], part[:, k, tok], w[:, 0, k, :],
                                         start=(k == 0 and n == 0), stop=(k == KC - 1 and n == 2))
                last.then_inc(g_w_ps, 1)

            def transpose_z(t):
                pe.wait_ge(g_z, done(g_z, t))
                pe.wait_ge(g_lo, room(g_lo, t))
                for k in range(KC):
                    last = pe.transpose(bank[1][:, k * P:(k + 1) * P], z[:, k * P:(k + 1) * P], ident[:])
                last.then_inc(g_zT_ps, 1)

            def out_project(t):
                pe.wait_ge(g_lo, done(g_lo, t))
                pe.wait_ge(g_resid, room(g_resid, t))
                for k in range(KC):
                    for n, (part, w) in enumerate(((zT_hi, wgo_hi), (zT_hi, wgo_lo), (zT_lo, wgo_hi))):
                        last = pe.matmul(bank[2][:], part[:, k, :], w[:, 1, k, :],
                                         start=(k == 0 and n == 0), stop=(k == KC - 1 and n == 2))
                last.then_inc(g_wo, 1)

            def transpose_rows(t):
                pe.wait_ge(row_lo, done(row_lo, t))
                pe.wait_ge(nd["lo"], room(nd["lo"], t))
                for k in range(KC):
                    last = transpose_parts(bank[3][:, k * P:(k + 1) * P], row_parts, k)
                last.then_inc(nd["xT_psum"], 1)

            def tile_steps(t):
                if inside(t - 1):
                    out_project(t - 1)
                if inside(t):
                    transpose_z(t)
                if inside(t - 3):
                    transpose_rows(t - 3)
                if inside(t + 1):
                    gate_project(t + 1)

            def transpose_unit(n):
                pe.wait_ge(d_sw_lo, room(d_sw_lo, n))
                to = bank[4 + n % 4]
                if n < 2 * KC:
                    t, k = n // KC, n % KC
                    for c, rows in enumerate(HC):
                        last = pe.transpose(to[:, c * P:c * P + rows], sw12_f32[0:rows, t, c, k * P:(k + 1) * P],
                                            ident[0:rows, 0:rows])
                elif n < 2 * KC + len(HC):
                    c = n - 2 * KC
                    for k in range(KC):
                        last = pe.transpose(to[0:HC[c], k * P:(k + 1) * P], sw3_f32[:, k, c * P:c * P + HC[c]], ident[:])
                else:
                    for k in range(KC):
                        last = pe.transpose(to[:, k * EXPERTS:(k + 1) * EXPERTS], router_f32[:, k * P:(k + 1) * P],
                                            ident[0:EXPERTS, 0:EXPERTS])
                last.then_inc(d_sw_ps, 1)

            pe.wait_ge(c_copied, done(c_copied, HEADS * 12 - 1))
            pe.wait_ge(c_lo, 3)
            pe.wait_ge(ident_ready, 2)
            gate_project(0)
            outputs(HEADS - 1)
            for t in range(3):
                tile_steps(t)
            with pe.Fori(3, TILES - 1) as t:
                tile_steps(t)
            pe.wait_ge(c_o_copied, done(c_o_copied, 4 * HEADS - 1))
            pe.wait_ge(weights_loaded, 96 + 16 * 6)
            for t in range(TILES - 1, TILES + 3):
                tile_steps(t)
                for n in units_of_step(t):
                    transpose_unit(n)

            pe.wait_ge(nd["lo"], done(nd["lo"], TILES - 1))
            transpose_unit(2 * KC + len(HC))
            pe.wait_ge(d_sw_lo, done(d_sw_lo, 2 * KC + len(HC)))
            for t in range(TILES):
                for k in range(KC):
                    tok = slice(t * P, (t + 1) * P)
                    for i, (part, w) in enumerate(((xT_hi, router_hi), (xT_hi, router_lo), (xT_lo, router_hi))):
                        last = pe.matmul(bank[7][:, t * EXPERTS:(t + 1) * EXPERTS], part[:, k, tok], w[:, k, :],
                                         start=(k == 0 and i == 0), stop=(k == KC - 1 and i == 2))
            last.then_inc(d_logits, 1)

            def w1_part(part, k, at, width):
                return sw_split[:, k, part, at:at + width]

            def w2_part(part, c, rows):
                return sw_split[0:rows, :, part, 2 * HID + c * P:2 * HID + (c + 1) * P]

            def shared_up(m):
                for c, rows in enumerate(HC):
                    q = m * 3 + c
                    pe.wait_ge(d_prod, room(d_prod, q))
                    for t, (at, signal) in enumerate(((q % 2, d_gate_ps), (2 + q % 2, d_up_ps))):
                        for k in range(KC):
                            for i, (w, part) in enumerate(((0, xT_hi), (0, xT_lo), (1, xT_hi))):
                                last = pe.matmul(bank[at][0:rows, :], w1_part(w, k, t * HID + c * P, rows),
                                                 part[:, k, m * GW:(m + 1) * GW],
                                                 start=(k == 0 and i == 0), stop=(k == KC - 1 and i == 2))
                        last.then_inc(signal, 1)

            def shared_down(m):
                pe.wait_ge(d_hlo, done(d_hlo, m * 3 + 2))
                for i in range(GT):
                    pe.wait_ge(d_acc, room(d_acc, m * GT + i))
                    for c, rows in enumerate(HC):
                        for n, (part, w) in enumerate(((hT_hi, 0), (hT_hi, 1), (hT_lo, 0))):
                            last = pe.matmul(bank[4 + i][:], part[0:rows, m % 2, c, i * P:(i + 1) * P],
                                             w2_part(w, c, rows), start=(c == 0 and n == 0), stop=(c == 2 and n == 2))
                    last.then_inc(d_y_ps, 1)

            shared_up(0)
            pe.wait_ge(d_chosen, 1)
            NR = TILES * EXPERTS
            pe.matmul(bank[7][:, 0:NR], before[:], chosen[:], start=True, stop=False)
            for d in range(1, TILES):
                pe.matmul(bank[7][:, d * EXPERTS:NR], ones16[:], chosen[:, 0:NR - d * EXPERTS],
                          start=False, stop=(d == TILES - 1))
            for t in range(TILES):
                last = pe.matmul(bank[7][:, NR:NR + EXPERTS], ones16[:], chosen[:, t * EXPERTS:(t + 1) * EXPERTS],
                                 start=(t == 0), stop=(t == TILES - 1))
            last.then_inc(d_counts, 1)
            shared_up(1)
            pe.wait_ge(d_slots, 1)
            shared_down(0)
            for m in range(2, GROUPS):
                shared_up(m)
                shared_down(m - 1)
            shared_down(GROUPS - 1)

            def tile_transpose(i, slot, lap):
                pe.wait_ge(ring_loaded[slot], 16 * lap + (48 * (FC // RAW) + 16))
                pe.wait_ge(t_xlo, room(t_xlo, i))
                for k in range(KC):
                    last = transpose_parts(bank[0][:, k * P:(k + 1) * P], xg[:, slot], k)
                last.then_inc(t_xT, 1)

            def tile_up(i, expert):
                pe.wait_ge(t_xlo, done(t_xlo, i))
                hold(pe, t_h, room(t_h, i))
                for k in range(KC):
                    for part, w in ((xgT_hi, 0), (xgT_hi, 1), (xgT_lo, 0)):
                        at = (2 * k + w) * UNIT
                        first, end = k == 0 and part is xgT_hi and w == 0, k == KC - 1 and part is xgT_lo
                        pe.matmul(bank[1][:, 0:HID], part[:, k, :], experts[:, EXPERTS - 1 - expert, at:at + HID], start=first, stop=end)
                        last = pe.matmul(bank[2][:, 0:HID], part[:, k, :], experts[:, EXPERTS - 1 - expert, at + HID:at + 2 * HID],
                                         start=first, stop=end)
                last.then_inc(t_gu, 1)

            def tile_hidden(i):
                pe.wait_ge(t_tlo, done(t_tlo, i))
                pe.wait_ge(t_hlo, room(t_hlo, i))
                for c in range(3):
                    last = transpose_parts(bank[3][:, c * P:(c + 1) * P], th_parts, c)
                last.then_inc(t_hT, 1)

            def tile_down(i, expert):
                pe.wait_ge(t_hlo, done(t_hlo, i))
                hold(pe, t_ycopy, room(t_ycopy, i))
                block = experts[:, EXPERTS - 1 - expert, :].rearrange("p (k s u) -> p k s u", k=KC, s=2)
                for c in range(3):
                    for n, (part, w) in enumerate(((thT_hi, 0), (thT_hi, 1), (thT_lo, 0))):
                        last = pe.matmul(bank[4][:], part[:, c, :], block[:, :, w, 2 * HID + c * P:2 * HID + (c + 1) * P],
                                         start=(c == 0 and n == 0), stop=(c == 2 and n == 2))
                last.then_inc(t_y, 1)

            def expert_of(i):
                return pe.value_load(tile_expert_i[0:1, bass.ds(i, 1)], min_val=0, max_val=EXPERTS - 1)

            def loaded_expert(i):
                expert = expert_of(i)
                hold(pe, experts_loaded, expert * 16 + 16)
                return expert

            pe.wait_ge(d_tile_expert, 1)
            for e in range(2):
                pe.wait_ge(loads[e], 48)
            pe.wait_ge(filled, 4)
            tile_transpose(0, 0, 0)
            tile_up(0, loaded_expert(0))
            tile_transpose(1, 1, 0)
            tile_hidden(0)
            pe.wait_ge(d_acc, done(d_acc, TILES - 1))
            with pe.Fori(0, (SLOTS // XR - 1) // 4) as lap:
                last_expert = expert_of(lap * (4 * XR))
                expert = loaded_expert(lap * (4 * XR) + 1)
                for s in range(4 * XR):
                    i = lap * (4 * XR) + (s + 1)
                    tile_up(i, expert)
                    tile_transpose(i + 1, (s + 2) % XR, lap * 4 + (s + 2) // XR)
                    if s < 4 * XR - 1:
                        next_expert = loaded_expert(i + 1)
                    tile_down(i - 1, last_expert)
                    tile_hidden(i)
                    last_expert, expert = expert, next_expert
            last_expert = expert_of(SLOTS - XR)
            for i in range(SLOTS - XR + 1, SLOTS):
                expert = loaded_expert(i)
                tile_up(i, expert)
                if i + 1 < SLOTS:
                    tile_transpose(i + 1, (i + 1) % XR, (i + 1) // XR)
                tile_down(i - 1, last_expert)
                tile_hidden(i)
                last_expert = expert
            tile_down(SLOTS - 1, last_expert)

        @block.scalar
        def _(act):
            def copy_inputs(b):
                pv = pair[0][:].rearrange("p j (k c) -> p j k c", c=P)
                act.wait_ge(a_xnT_psum, done(a_xnT_psum, b))
                act.wait_ge(a_scores, room(a_scores, b))
                act.activation(xnT0[:].rearrange("p k (j c) -> p j k c", c=P), pv, ACT.Copy).then_inc(a_xnT, 1)
                act.wait_ge(a_ctxT_psum, done(a_ctxT_psum, b))
                act.activation(ctxT[:, :, bass.ds(b * CTX, CTX)].rearrange("p k (j c) -> p j k c", c=P),
                               pair[1][:].rearrange("p j (k c) -> p j k c", c=P), ACT.Copy).then_inc(a_ctxT, 1)

            def exponentials(b):
                act.wait_ge(a_negmax, b + 1)
                act.wait_ge(a_probsT_psum, room(a_probsT_psum, b))
                act.wait_ge(a_rinv, room(a_rinv, b))
                for j in range(ROWT):
                    last = act.activation(probs[:, j, :], scores_sb[:, j, :], ACT.Exp, bias=negmax[:, j:j + 1],
                                          scale=SCALE, accum_out=rowsum[:, j:j + 1])
                last.then_inc(a_probs, 1)

            def copy_probsT(b):
                act.wait_ge(a_probsT_psum, done(a_probsT_psum, b))
                act.wait_ge(a_readout, room(a_readout, b))
                act.activation(probsT[:].rearrange("p m s -> p (m s)"), bank[5][:], ACT.Copy).then_inc(a_probsT, 1)

            copy_inputs(0)
            with act.Fori(0, BATCH - 1) as b:
                copy_inputs(b + 1)
                exponentials(b)
                copy_probsT(b)
            exponentials(BATCH - 1)
            copy_probsT(BATCH - 1)

            def split_hi(g, s, n=0):
                for h in range(2):
                    act.wait_ge(s["xT_psum"], done(s["xT_psum"], 2 * n + h))
                    act.activation(xT_hi[:, :, bass.ds((GT * g + 2 * h) * P, 2 * P)].rearrange("p k (j c) -> p j k c", c=P),
                                   pair[h][:].rearrange("p j (k c) -> p j k c", c=P),
                                   ACT.Copy).then_inc(s["hi"], 1)
            split_hi(0, nb)

            act.wait_ge(scales_loaded, 48)

            def unit_hi(n, slot, lap):
                act.wait_ge(u_loaded[slot], 48 * lap + 48)
                act.wait_ge(u_stored[slot], 16 * lap + 16)
                act.activation(unit_split[:, slot, 0, :], unit_f32[:, slot, :], ACT.Copy, scale=WS).then_inc(u_hi, 1)

            def gate(c, n, slot):
                act.wait_ge(b_gate_ps, n + 1)
                act.wait_ge(b_fused, room(b_fused, n))
                act.activation(silu[:, slot, :], bank[slot][:], ACT.Silu, scale=gscale[:, c:c + 1]).then_inc(b_silu, 1)

            def half_hi(g, half, n, slot):
                act.wait_ge(b_up_ps, n + 1)
                act.wait_ge(b_fused, room(b_fused, n))
                for at, i in ((slot, 2 * half), (2 + slot, 2 * half + 1)):
                    last = act.activation(xT_hi[:, :, bass.ds((GT * g + i) * P, P)],
                                          bank[at][:].rearrange("p (k c) -> p k c", c=P), ACT.Copy)
                last.then_inc(b_silu, 1)

            def fused_hi(g, c, n):
                act.wait_ge(b_fused, done(b_fused, n))
                act.wait_ge(b_down, room(b_down, g * FC + c))
                act.activation(fT_hi[:, c % FR, :], fused[:, c % 2, :], ACT.Copy).then_inc(b_fhi, 1)

            def ffn_group(g, b_rows=True, c_rows=True, units=12):
                for kind, c, n, slot in ffn_items(g, b_rows, c_rows):
                    if kind == "b":
                        half_hi(g + 1, c, n, slot)
                    elif kind == "c":
                        half_hi(g - 1, c, n, slot)
                    else:
                        if c:
                            fused_hi(g, c - 1, last_chunk)
                        gate(c, n, slot)
                        last_chunk = n
                        if c < units:
                            unit_hi((g - 1) * FC + c, c % 2, (g - 1) * (FC // 2) + c // 2)
                fused_hi(g, FC - 1, last_chunk)

            ffn_group(0, c_rows=False, units=0)
            with act.Fori(1, GROUPS - 1) as g:
                ffn_group(g)
            ffn_group(GROUPS - 1, b_rows=False, units=EXPERTS * KC - (GROUPS - 2) * FC)

            act.wait_ge(weights_loaded, 48)
            act.activation(wh_hi[:], wh_f32[:], ACT.Copy, scale=WS).then_inc(c_hi, 1)

            def copy_projections(h, items):
                for i in items:
                    if i == 0:
                        act.wait_ge(c_scores, room(c_scores, h))
                    if i == GROUPS:
                        act.wait_ge(c_o_ps, room(c_o_ps, 4 * h + 3))
                    act.wait_ge(c_proj, h * 12 + i + 1)
                    at = slice(i % GROUPS * GW, (i % GROUPS + 1) * GW)
                    dst = (kT[:, at], v[:].rearrange("p t e -> p (t e)")[:, at], qT[:, at])[i // GROUPS]
                    act.activation(dst, bank[i % GROUPS][:], ACT.Copy,
                                   scale=1.0 / WS if i >= 2 * GROUPS else 1.0).then_inc(c_copied, 1)

            act.wait_ge(b_down, done(b_down, GROUPS * FC - 1))
            copy_projections(0, range(2 * GROUPS))
            for i in range(2):
                act.activation(wgo_hi[:, i], wgo_f32[:, i], ACT.Copy, scale=WS).then_inc(c_hi, 1)
            split_hi(GROUPS - 1, nr, 1)
            copy_projections(0, range(2 * GROUPS, 3 * GROUPS))
            with act.Fori(1, HEADS) as h:
                copy_projections(h, range(3 * GROUPS))

            def relu_gate(t):
                act.wait_ge(g_w_ps, t + 1)
                act.wait_ge(g_z, room(g_z, t))
                act.activation(w_relu[:], bank[0][:], ACT.Relu, scale=1.0 / WS).then_inc(g_w, 1)

            def split_z(t):
                act.wait_ge(g_zT_ps, done(g_zT_ps, t))
                act.wait_ge(g_wo, room(g_wo, t))
                act.activation(zT_hi[:].rearrange("p k c -> p (k c)"), bank[1][:], ACT.Copy).then_inc(g_hi, 1)

            def row_high(t):
                act.wait_ge(nd["xn"], t + 1)
                act.wait_ge(row_stored, t * 16 + 16)
                act.wait_ge(nd["xT_psum"], room(nd["xT_psum"], t))
                act.activation(row_parts[:, 0, :], xn[:, 0, :], ACT.Copy).then_inc(row_hi, 1)

            def rows_hi(t):
                act.wait_ge(nd["xT_psum"], done(nd["xT_psum"], t))
                act.activation(xT_hi[:, :, bass.ds(t * P, P)], bank[3][:].rearrange("p (k c) -> p k c", c=P),
                               ACT.Copy).then_inc(nd["hi"], 1)

            def tile_steps(t):
                if inside(t):
                    split_z(t)
                if inside(t - 3):
                    rows_hi(t - 3)
                if inside(t - 2):
                    row_high(t - 2)
                if inside(t + 1):
                    relu_gate(t + 1)

            relu_gate(0)
            for t in range(3):
                tile_steps(t)
            with act.Fori(3, TILES - 1) as t:
                tile_steps(t)
            units = list(sw_units())

            def unit_high(n):
                act.wait_ge(d_sw_ps, n + 1)
                act.activation(units[n][1], units[n][0], ACT.Copy, scale=WS).then_inc(d_sw_hi, 1)

            for t in range(TILES - 1, TILES + 3):
                tile_steps(t)
                for n in units_of_step(t):
                    unit_high(n)
            unit_high(2 * KC + len(HC))
            act.wait_ge(d_route, 2)
            act.activation(prob[:], prob[:], ACT.Exp).then_inc(d_exp, 1)

            for m in range(GROUPS):
                for c in range(4):
                    if c < 3:
                        rows, q = HC[c], m * 3 + c
                        act.wait_ge(d_gate_ps, q + 1)
                        act.wait_ge(d_prod, room(d_prod, q))
                        act.activation(hg[0:rows, q % 2, :], bank[q % 2][0:rows, :], ACT.Silu, scale=1.0 / WS).then_inc(d_silu, 1)
                    if c:
                        rows, q = HC[c - 1], m * 3 + c - 1
                        act.wait_ge(d_prod, done(d_prod, q))
                        if c == 1:
                            act.wait_ge(d_y_ps, room(d_y_ps, m * GT + GT - 1))
                        act.activation(hT_hi[0:rows, m % 2, c - 1, :], hp[0:rows, q % 2, :], ACT.Copy).then_inc(d_hhi, 1)
            def load_expert(e):
                act.wait_ge(experts_loaded, 16 * e)
                act.dma_start(experts[:, EXPERTS - 1 - e, :].rearrange("p (k u) -> p k u", k=KC),
                              split_w[e].rearrange("k p u -> p k u")).then_inc(experts_loaded, 16)

            def tile_x_hi(i):
                act.wait_ge(t_xT, i + 1)
                act.activation(xgT_hi[:].rearrange("p k c -> p (k c)"), bank[0][:], ACT.Copy).then_inc(t_xhi, 1)

            def tile_silu(i):
                act.wait_ge(t_gu, i + 1)
                act.wait_ge(t_h, room(t_h, i))
                act.activation(tg[:], bank[1][:, 0:HID], ACT.Silu, scale=1.0 / WS).then_inc(t_silu, 1)

            def tile_part_hi(i):
                act.wait_ge(t_h, done(t_h, i))
                act.wait_ge(t_hT, room(t_hT, i))
                act.activation(th_parts[:, 0, :], th[:], ACT.Copy).then_inc(t_thi, 1)

            def tile_h_hi(i):
                act.wait_ge(t_hT, done(t_hT, i))
                act.activation(thT_hi[:].rearrange("p k c -> p (k c)"), bank[3][:, 0:3 * P], ACT.Copy).then_inc(t_hhi, 1)

            def tile_y(i, slot, lap):
                act.wait_ge(t_y, i + 1)
                act.wait_ge(t_y_stored[slot], 16 * lap + 16)
                act.activation(ty[:, slot, :], bank[4][:], ACT.Copy, scale=1.0 / WS).then_inc(t_ycopy, 1)

            tile_x_hi(0)
            tile_silu(0)
            act.wait_ge(d_acc, done(d_acc, TILES - 1))
            act.wait_ge(d_scattered, 16 * TOP_K * TILES)
            load_expert(2)
            tile_x_hi(1)
            tile_part_hi(0)
            tile_h_hi(0)

            def lap_tiles(lap):
                for s in range(XR):
                    i = lap * XR + (s + 1)
                    tile_silu(i)
                    tile_x_hi(i + 1)
                    tile_part_hi(i)
                    tile_y(i - 1, s, lap)
                    tile_h_hi(i)

            for e in range(3, EXPERTS):
                load_expert(e)
                lap_tiles(e - 3)
            with act.Fori(EXPERTS - 3, SLOTS // XR - 1) as lap:
                lap_tiles(lap)
            for i in range(SLOTS - XR + 1, SLOTS):
                tile_silu(i)
                if i + 1 < SLOTS:
                    tile_x_hi(i + 1)
                tile_part_hi(i)
                tile_y(i - 1, (i - 1) % XR, (i - 1) // XR)
                tile_h_hi(i)
            tile_y(SLOTS - 1, (SLOTS - 1) % XR, (SLOTS - 1) // XR)

        @block.vector
        def _(dve):
            dve.wait_ge(mask_loaded, 16)
            dve.tensor_scalar(maskbias[:], mask_u8[:], -MASKED, MASKED, ALU.mult, ALU.add).then_inc(a_bias, 1)
            dve.tensor_reduce(valid[:], mask_u8[:], AX.X, ALU.max).then_inc(a_valid, 1)

            def normalise0(b, quantised=None):
                dve.wait_ge(batches_loaded, b + 1)
                for j in range(ROWT):
                    dve.bn_stats(stats[:, j, :], x_res[:, ROWT * b + j, :]).then_inc(a_stats, 1)
                hold(dve, a_stats, ROWT * b + ROWT)
                for j in range(ROWT):
                    last = dve.bn_aggr(meanvar[:, j, :], stats[:, j, :])
                last.then_inc(a_meanvar, 1)
                if quantised:
                    quantise_start(*quantised)
                dve.wait_ge(a_rstd, b + 1)
                dve.wait_ge(a_xnT_psum, room(a_xnT_psum, b))
                for j in range(ROWT):
                    last = dve.tensor_scalar(xn0[:, j, :], x_res[:, ROWT * b + j, :], meanvar[:, j, 0:1],
                                             rstd[:, j:j + 1], ALU.subtract, ALU.mult)
                last.then_inc(a_xn, 1)

            def mask_and_max(b):
                dve.wait_ge(a_scores, done(a_scores, b))
                dve.wait_ge(a_probs, room(a_probs, b))
                mb = maskbias[:, b, :]
                for j in range(ROWT):
                    last = dve.tensor_tensor(scores_sb[:, j, :], bank[4][:, j * CTX:(j + 1) * CTX], mb, ALU.add)
                last.then_inc(a_masked, 1)
                dve.wait_ge(a_masked, done(a_masked, b))
                dve.tensor_reduce(rowmax[:], scores_sb[:], AX.X, ALU.max).then_inc(a_rowmax, 1)
                dve.wait_ge(a_rowmax, b + 1)
                dve.tensor_scalar(negmax[:], rowmax[:], -SCALE, None, ALU.mult).then_inc(a_negmax, 1)

            def inverse_sums(b):
                dve.wait_ge(a_probs, done(a_probs, b))
                dve.reciprocal(rinv[:], rowsum[:]).then_inc(a_rinv, 1)
                dve.wait_ge(a_rinv, done(a_rinv, b))
                dve.tensor_scalar(rscale[:], rinv[:], valid[:, bass.ds(b, 1)], None, ALU.mult).then_inc(a_rscale, 1)

            def add_readout(b):
                dve.wait_ge(a_rscale, b + 1)
                dve.wait_ge(a_readout, done(a_readout, b))
                for j in range(ROWT):
                    t = ROWT * b + j
                    last = dve.scalar_tensor_tensor(x_res[:, t, :], bank[6 + j][:], rscale[:, j:j + 1], x_res[:, t, :],
                                                    ALU.mult, ALU.add)
                last.then_inc(a_resid, 1)

            def quantise_start(i, chunk, part):
                dve.wait_ge(w_quant, room(w_quant, i))
                dve.tensor_scalar(expo[:].bitcast(U32), part.bitcast(U32), 0x7F800000, None,
                                  ALU.bitwise_and).then_inc(w_step, 1)
                dve.wait_ge(w_step, i * 3 + 1)
                dve.tensor_scalar(expo[:], expo[:], 2.0 ** -6, 1.5 * 2.0 ** 20, ALU.max, ALU.mult).then_inc(w_step, 1)

            def quantise_end(i, chunk, part):
                dve.wait_ge(w_step, i * 3 + 2)
                dve.tensor_tensor(part, part, expo[:], ALU.add).then_inc(w_step, 1)
                dve.wait_ge(w_step, i * 3 + 3)
                dve.tensor_tensor(chunk, part, expo[:], ALU.subtract).then_inc(w_quant, 1)

            def quantise_to_pool(i):
                odd_or_even = (expo, expo_odd)[i % 2]
                part = raw[:, i % RAW, :]
                dve.wait_ge(ring_loaded[i % RAW], 48 * (i // RAW) + 48)
                dve.wait_ge(w_quant, room(w_quant, i - 1))
                dve.tensor_scalar(odd_or_even[:].bitcast(U32), part.bitcast(U32), 0x7F800000, None,
                                  ALU.bitwise_and).then_inc(w_step, 1)
                dve.wait_ge(w_step, i * 3 + 1)
                dve.tensor_scalar(odd_or_even[:], odd_or_even[:], 2.0 ** -6, 1.5 * 2.0 ** 20, ALU.max, ALU.mult).then_inc(w_step, 1)
                dve.wait_ge(w_step, i * 3 + 2)
                dve.tensor_tensor(part, part, odd_or_even[:], ALU.add).then_inc(w_step, 1)

            def chunk_of(i):
                dve.wait_ge(ring_loaded[i % RAW], 48 * (i // RAW) + 48)
                return i, wq[:, i, :], raw[:, i % RAW, :]

            def rows_stats(g, s):
                for i in range(GT):
                    dve.bn_stats(stats[:, i, :], x_res[:, GT * g + i, :]).then_inc(s["stats"], 1)
                hold(dve, s["stats"], GT * g + GT)
                for i in range(GT):
                    last = dve.bn_aggr(meanvar[:, i, :], stats[:, i, :])
                last.then_inc(s["meanvar"], 1)

            def rows_normalise(g, s):
                dve.wait_ge(s["rstd"], g + 1)
                for i in range(GT):
                    last = dve.tensor_scalar(xn[:, i, :], x_res[:, GT * g + i, :], meanvar[:, i, 0:1],
                                             rstd[:, i:i + 1], ALU.subtract, ALU.mult)
                    if i % 2:
                        last.then_inc(s["xn"], 1)

            def split_lo(g, s, n=0):
                for i in range(GT):
                    at = bass.ds((GT * g + i) * P, P)
                    if i % 2 == 0:
                        dve.wait_ge(s["hi"], 2 * n + i // 2 + 1)
                    last = dve.tensor_tensor(xT_lo[:, :, at], pair[i // 2][:, i % 2, :].rearrange("p (k c) -> p k c", c=P),
                                             xT_hi[:, :, at], ALU.subtract)
                last.then_inc(s["lo"], 1)

            dve.wait_ge(a_bias, 1)
            dve.wait_ge(a_valid, 1)
            normalise0(0)
            normalise0(1)
            mask_and_max(0)
            normalise0(2)

            def batch_steps(b, quantised=None):
                inverse_sums(b - 1)
                mask_and_max(b)
                normalise0(b + 2, quantised)
                add_readout(b - 1)
                if quantised:
                    quantise_end(*quantised)

            batch_steps(1)
            with dve.Fori(0, RAW) as i:
                hold(dve, batches_loaded, i + (BATCH + 1))
                batch_steps(i + 2, (i, wq[:, i, :], raw[:, i, :]))
            batch_steps(BATCH - 3, chunk_of(RAW))
            rows_stats(0, nb)
            inverse_sums(BATCH - 3)
            mask_and_max(BATCH - 2)
            rows_normalise(0, nb)
            add_readout(BATCH - 3)
            inverse_sums(BATCH - 2)
            mask_and_max(BATCH - 1)
            quantise_to_pool(RAW + 1)
            add_readout(BATCH - 2)
            inverse_sums(BATCH - 1)
            dve.wait_ge(a_readout, done(a_readout, BATCH - 1))
            split_lo(0, nb)
            add_readout(BATCH - 1)

            dve.wait_ge(scales_loaded, 48)

            def unit_lo(n, slot):
                dve.wait_ge(u_hi, n + 1)
                dve.scalar_tensor_tensor(unit_split[:, slot, 1, :], unit_f32[:, slot, :], WS, unit_split[:, slot, 0, :],
                                         ALU.mult, ALU.subtract).then_inc(u_lo, 1)

            def half_lo(g, half, n, slot):
                dve.wait_ge(b_silu, n + 1)
                for at, i in ((slot, 2 * half), (2 + slot, 2 * half + 1)):
                    cols = bass.ds((GT * g + i) * P, P)
                    last = dve.tensor_tensor(xT_lo[:, :, cols], bank[at][:].rearrange("p (k c) -> p k c", c=P),
                                             xT_hi[:, :, cols], ALU.subtract)
                last.then_inc(b_fused, 1)

            def product(g, c, n, slot):
                dve.wait_ge(b_silu, n + 1)
                dve.wait_ge(b_up_ps, n + 1)
                dve.wait_ge(b_fhi, room(b_fhi, g * FC + c))
                dve.scalar_tensor_tensor(fused[:, c % 2, :], bank[2 + slot][:], uscale[:, c:c + 1], silu[:, slot, :],
                                         ALU.mult, ALU.mult).then_inc(b_fused, 1)

            def fused_lo(g, c):
                dve.wait_ge(b_fhi, done(b_fhi, g * FC + c))
                dve.tensor_tensor(fT_lo[:, c % FR, :], fused[:, c % 2, :], fT_hi[:, c % FR, :],
                                  ALU.subtract).then_inc(b_flo, 1)

            def add_down(g):
                dve.wait_ge(b_down, done(b_down, FC * g + FC - 1))
                for i in range(GT):
                    t = GT * g + i
                    dve.tensor_tensor(down[:, i % 2, :], bank[4 + i][:], dscale[:], ALU.mult).then_inc(b_scaled, 1)
                    dve.wait_ge(b_scaled, done(b_scaled, GT * g + i))
                    dve.tensor_tensor(x_res[:, t, :], x_res[:, t, :], down[:, i % 2, :], ALU.add).then_inc(b_resid, 1)

            def ffn_group(g, b_rows=True, c_rows=True, units=12, quantised=0):
                for kind, c, n, slot in ffn_items(g, b_rows, c_rows):
                    if kind == "b":
                        half_lo(g + 1, c, n, slot)
                        continue
                    if kind == "c":
                        half_lo(g - 1, c, n, slot)
                        continue
                    product(g, c, n, slot)
                    if c < units:
                        unit_lo((g - 1) * FC + c, c % 2)
                    fused_lo(g, c)
                    if c < quantised:
                        quantise_to_pool(FC - quantised + c)
                    if c_rows and c == 0:
                        add_down(g - 1)
                    if b_rows and c == AFTER_B[0] - 3:
                        rows_stats(g + 1, nb)
                    if b_rows and c == AFTER_B[0] - 2:
                        rows_normalise(g + 1, nb)
                    if c_rows and c == AFTER_C[0] - 3:
                        hold(dve, b_resid, GT * g)
                        rows_stats(g - 1, nr)
                    if c_rows and c == AFTER_C[0] - 2:
                        rows_normalise(g - 1, nr)

            ffn_group(0, c_rows=False, units=0, quantised=FC - RAW - 2)
            dve.wait_ge(filled, 2)
            with dve.Fori(1, GROUPS - 1) as g:
                ffn_group(g)
            ffn_group(GROUPS - 1, b_rows=False, units=EXPERTS * KC - (GROUPS - 2) * FC)
            add_down(GROUPS - 1)

            dve.wait_ge(b_resid, TILES)
            rows_stats(GROUPS - 1, nr)
            dve.wait_ge(c_hi, 1)
            dve.scalar_tensor_tensor(wh_lo[:], wh_f32[:], WS, wh_hi[:], ALU.mult, ALU.subtract).then_inc(c_lo, 1)
            rows_normalise(GROUPS - 1, nr)
            split_lo(GROUPS - 1, nr, 1)
            dve.wait_ge(c_hi, 3)
            for i in range(2):
                dve.scalar_tensor_tensor(wgo_lo[:, i], wgo_f32[:, i], WS, wgo_hi[:, i], ALU.mult, ALU.subtract).then_inc(c_lo, 1)

            dve.wait_ge(weights_loaded, 96)
            oT = ctxT[:].rearrange("p h (b j e) -> p h b j e", j=ROWT, e=P)
            dve.wait_ge(filled, 3)
            with dve.Fori(0, HEADS) as h:
                dve.wait_ge(c_scores, done(c_scores, h))
                dve.tensor_tensor(scaled[:, 0:SEQ], bank[4][:, 0:SEQ], decay[:, 0, h, :], ALU.mult)
                dve.tensor_tensor(scaled[:, SEQ:], bank[5][:, 0:P], decay[:, 1, h, P:SEQ], ALU.mult).then_inc(c_masked, 1)
                dve.wait_ge(c_masked, done(c_masked, h))
                dve.wait_ge(c_o_ps, room(c_o_ps, 4 * h + 3))
                dve.tensor_scalar(floored[:], scaled[:], -1.0, 1.0, ALU.mult, ALU.max).then_inc(c_scaled, 1)
                dve.wait_ge(c_scaled, h + 1)
                dve.tensor_tensor(weightT[:, 0, :], floored[:, 0:SEQ], scaled[:, 0:SEQ], ALU.max)
                dve.tensor_tensor(weightT[:, 1, P:SEQ], floored[:, SEQ:], scaled[:, SEQ:], ALU.max).then_inc(c_weights, 1)
                for j in range(ROWT):
                    for half in range(2):
                        o = 2 * j + half
                        dve.wait_ge(c_o_ps, done(c_o_ps, 4 * h + o))
                        dve.tensor_copy(oT[:, h, 4 * half:4 * half + 4, j, :],
                                        bank[6 + half][:].rearrange("p (b e) -> p b e", e=P)).then_inc(c_o_copied, 1)

            o_tile = ctxT[:].rearrange("p h (t e) -> p t h e", e=P)

            def group_stats(t):
                dve.bn_stats(gn_stats[:], o_tile[:, t]).then_inc(g_stats, 1)

            def group_meanvar(t):
                hold(dve, g_stats, t + 1)
                dve.bn_aggr(gn_meanvar[:], gn_stats[:]).then_inc(g_meanvar, 1)

            def group_vareps(t):
                dve.wait_ge(g_meanvar, t + 1)
                dve.tensor_copy(gn_mean[:, bass.ds(t, 1)], gn_meanvar[:, 0:1])
                dve.tensor_scalar(gn_vareps[:, bass.ds(t, 1)], gn_meanvar[:, 1:2], GN_EPS, None, ALU.add).then_inc(g_vareps, 1)

            def group_normalise(t):
                dve.wait_ge(g_rstd, t + 1)
                dve.wait_ge(g_ygamma, room(g_ygamma, t))
                dve.tensor_scalar(y_norm[:].rearrange("p (h e) -> p h e", e=P), o_tile[:, t], gn_mean[:, bass.ds(t, 1)],
                                  gn_rstd[:, bass.ds(t, 1)], ALU.subtract, ALU.mult).then_inc(g_ynorm, 1)

            def gate_product(t):
                dve.wait_ge(g_w, done(g_w, t))
                dve.wait_ge(g_y, t + 1)
                dve.wait_ge(g_zT_ps, room(g_zT_ps, t))
                dve.tensor_tensor(z[:], w_relu[:], y[:], ALU.mult).then_inc(g_z, 1)

            def split_z_lo(t):
                dve.wait_ge(g_hi, t + 1)
                dve.tensor_tensor(zT_lo[:].rearrange("p k c -> p (k c)"), bank[1][:], zT_hi[:].rearrange("p k c -> p (k c)"),
                                  ALU.subtract).then_inc(g_lo, 1)

            def add_output(t):
                dve.wait_ge(g_wo, done(g_wo, t))
                dve.scalar_tensor_tensor(x_res[:, t, :], bank[2][:], 1.0 / WS, x_res[:, t, :], ALU.mult, ALU.add).then_inc(g_resid, 1)

            def row_stats(t):
                hold(dve, g_resid, done(g_resid, t))
                dve.bn_stats(stats[:, 0, :], x_res[:, t, :]).then_inc(nd["stats"], 1)

            def row_meanvar(t):
                hold(dve, nd["stats"], t + 1)
                dve.bn_aggr(meanvar[:, 0, :], stats[:, 0, :]).then_inc(nd["meanvar"], 1)

            def row_vareps_mean(t):
                dve.wait_ge(nd["meanvar"], t + 1)
                dve.tensor_copy(row_mean[:, bass.ds(t, 1)], meanvar[:, 0, 0:1])
                dve.tensor_scalar(row_vareps[:, bass.ds(t, 1)], meanvar[:, 0, 1:2], LN_EPS, None, ALU.add).then_inc(nd["vareps"], 1)

            def row_normalise(t):
                dve.wait_ge(nd["rstd"], t + 1)
                dve.wait_ge(row_lo, room(row_lo, t))
                dve.tensor_scalar(xn[:, 0, :], x_res[:, t, :], row_mean[:, bass.ds(t, 1)], row_rstd[:, bass.ds(t, 1)],
                                  ALU.subtract, ALU.mult).then_inc(nd["xn"], 1)

            def row_low(t):
                dve.wait_ge(row_hi, t + 1)
                dve.tensor_tensor(row_parts[:, 1, :], xn[:, 0, :], row_parts[:, 0, :], ALU.subtract).then_inc(row_lo, 1)

            def rows_lo(t):
                dve.wait_ge(nd["hi"], t + 1)
                cols = bass.ds(t * P, P)
                dve.tensor_tensor(xT_lo[:, :, cols], bank[3][:].rearrange("p (k c) -> p k c", c=P), xT_hi[:, :, cols],
                                  ALU.subtract).then_inc(nd["lo"], 1)

            def tile_steps(t):
                if inside(t):
                    gate_product(t)
                if inside(t + 1):
                    group_normalise(t + 1)
                if inside(t + 2):
                    group_stats(t + 2)
                if inside(t - 1):
                    add_output(t - 1)
                if inside(t + 2):
                    group_meanvar(t + 2)
                if inside(t):
                    split_z_lo(t)
                if inside(t - 1):
                    row_stats(t - 1)
                if inside(t + 2):
                    group_vareps(t + 2)
                if inside(t - 3):
                    rows_lo(t - 3)
                if inside(t - 1):
                    row_meanvar(t - 1)
                if inside(t - 2):
                    row_normalise(t - 2)
                if inside(t - 1):
                    row_vareps_mean(t - 1)
                if inside(t - 2):
                    row_low(t - 2)

            dve.wait_ge(c_o_copied, done(c_o_copied, 4 * HEADS - 1))
            for t in range(2):
                group_stats(t)
                group_meanvar(t)
                group_vareps(t)
            group_normalise(0)
            for t in range(3):
                tile_steps(t)
            with dve.Fori(3, TILES - 2) as t:
                tile_steps(t)
            units = list(sw_units())

            def unit_low(n):
                dve.wait_ge(d_sw_hi, n + 1)
                dve.scalar_tensor_tensor(units[n][2], units[n][0], WS, units[n][1], ALU.mult, ALU.subtract).then_inc(d_sw_lo, 1)

            tile_steps(TILES - 2)
            for t in range(TILES - 1, TILES + 3):
                tile_steps(t)
                for n in units_of_step(t):
                    unit_low(n)

            unit_low(2 * KC + len(HC))

            steps = [0]

            def route(instruction):
                instruction.then_inc(d_route, 1)
                steps[0] += 1
                dve.wait_ge(d_route, steps[0])

            per_tile = [P, TILES, EXPERTS]
            square = [P, TILES, EXPERTS, EXPERTS]
            dve.wait_ge(d_logits, 1)
            NR = TILES * EXPERTS
            logits = bank[7][:, 0:NR].rearrange("p (t e) -> p t e", e=EXPERTS)
            dve.wait_ge(d_const, 4)
            route(dve.tensor_scalar(rank[:], logits, 1.0 / WS, None, ALU.mult))
            dve.tensor_reduce(prob_max[:], rank[:], AX.X, ALU.max).then_inc(d_weights, 1)
            dve.wait_ge(d_weights, 1)
            route(dve.tensor_tensor(prob[:], rank[:], prob_max[:].unsqueeze(2).broadcast_to(per_tile), ALU.subtract))
            dve.wait_ge(d_exp, 1)
            route(dve.tensor_reduce(prob_sum[:], prob[:], AX.X, ALU.add))
            route(dve.reciprocal(prob_max[:], prob_sum[:]))
            route(dve.tensor_tensor(prob[:], prob[:], prob_max[:].unsqueeze(2).broadcast_to(per_tile), ALU.mult))
            own, other = prob[:].unsqueeze(3).broadcast_to(square), prob[:].unsqueeze(2).broadcast_to(square)
            route(dve.tensor_tensor(above[:], other, own, ALU.is_gt))
            route(dve.tensor_tensor(tied[:], other, own, ALU.is_equal))
            route(dve.tensor_tensor(tied[:], tied[:], lower[:].unsqueeze(1).broadcast_to(square), ALU.mult))
            route(dve.tensor_tensor(above[:], above[:], tied[:], ALU.add))
            route(dve.tensor_reduce(rank[:], above[:], AX.X, ALU.add))
            dve.tensor_scalar(chosen[:], rank[:].rearrange("p t e -> p (t e)"), 1.5, None, ALU.is_lt).then_inc(d_chosen, 1)
            route(dve.scalar_tensor_tensor(prob[:], rank[:], 1.5, prob[:], ALU.is_lt, ALU.mult))
            route(dve.tensor_reduce(prob_sum[:], prob[:], AX.X, ALU.add))
            route(dve.tensor_scalar(prob_sum[:], prob_sum[:], 1e-20, None, ALU.add))
            route(dve.reciprocal(prob_max[:], prob_sum[:]))
            dve.tensor_tensor(expert_w[:], prob[:], prob_max[:].unsqueeze(2).broadcast_to(per_tile), ALU.mult).then_inc(d_weights, 1)
            dve.wait_ge(d_weights, 2)

            def shared_hidden(m):
                for c in range(4):
                    if c < 3:
                        rows, q = HC[c], m * 3 + c
                        dve.wait_ge(d_silu, q + 1)
                        dve.wait_ge(d_up_ps, q + 1)
                        dve.wait_ge(d_hlo, room(d_hlo, q))
                        dve.scalar_tensor_tensor(hp[0:rows, q % 2, :], bank[2 + q % 2][0:rows, :], 1.0 / WS, hg[0:rows, q % 2, :],
                                                 ALU.mult, ALU.mult).then_inc(d_prod, 1)
                    if c:
                        rows, q = HC[c - 1], m * 3 + c - 1
                        dve.wait_ge(d_hhi, q + 1)
                        dve.tensor_tensor(hT_lo[0:rows, m % 2, c - 1, :], hp[0:rows, q % 2, :],
                                          hT_hi[0:rows, m % 2, c - 1, :], ALU.subtract).then_inc(d_hlo, 1)

            def shared_add(m):
                for i in range(GT):
                    t = m * GT + i
                    dve.wait_ge(d_y_ps, done(d_y_ps, m * GT + i))
                    dve.scalar_tensor_tensor(x_res[:, t, :], bank[4 + i][:], 1.0 / WS, x_res[:, t, :],
                                             ALU.mult, ALU.add).then_inc(d_acc, 1)

            shared_hidden(0)

            order = [0]

            def place(instruction):
                instruction.then_inc(d_place, 1)
                order[0] += 1
                dve.wait_ge(d_place, order[0])

            dve.wait_ge(d_counts, 1)
            place(dve.tensor_scalar(tiles_of[:], bank[7][:, NR:NR + EXPERTS], 1.0 / P, (P - 1.0) / P - 0.5 + 0.5 / P,
                                    ALU.mult, ALU.add))
            place(dve.tensor_scalar(tiles_of[:], tiles_of[:], 2.0 ** 23, -2.0 ** 23, ALU.add, ALU.add))
            place(dve.tensor_tensor(tiles_low[:], lower[:], tiles_of[:].unsqueeze(1).broadcast_to([P, EXPERTS, EXPERTS]), ALU.mult))
            place(dve.tensor_reduce(first_tile[:], tiles_low[:], AX.X, ALU.add))
            place(dve.tensor_tensor(end_tile[:], first_tile[:], tiles_of[:], ALU.add))
            place(dve.scalar_tensor_tensor(position[:], first_tile[:].unsqueeze(1).broadcast_to(per_tile), float(P),
                                           bank[7][:, 0:NR].rearrange("p (t e) -> p t e", e=EXPERTS), ALU.mult, ALU.add))
            for c in range(TOP_K):
                place(dve.scalar_tensor_tensor(picked[:, c], rank[:], float(c), position[:], ALU.is_equal, ALU.mult))
                place(dve.scalar_tensor_tensor(picked[:, TOP_K + c], rank[:], float(c), expert_w[:], ALU.is_equal, ALU.mult))
            place(dve.tensor_reduce(slot_f32[:], picked[:], AX.X, ALU.add))
            dve.tensor_copy(slot_u32[:], slot_f32[:, 0:TOP_K].rearrange("p c t -> p (c t)")).then_inc(d_slots, 1)
            sq = [1, SLOTS, EXPERTS]
            place(dve.tensor_tensor(tile_past[:], end_tile[0:1].unsqueeze(1).broadcast_to(sq),
                                    tile_no[:].unsqueeze(2).broadcast_to(sq), ALU.is_le))
            place(dve.tensor_reduce(tile_expert[:], tile_past[:], AX.X, ALU.add))
            place(dve.tensor_scalar(tile_expert[:], tile_expert[:], EXPERTS - 1.0, None, ALU.min))
            dve.tensor_copy(tile_expert_i[:], tile_expert[:]).then_inc(d_tile_expert, 1)

            for m in range(1, GROUPS):
                shared_hidden(m)
                shared_add(m - 1)
            shared_add(GROUPS - 1)

            def tile_x_lo(i):
                dve.wait_ge(t_xhi, i + 1)
                dve.tensor_tensor(xgT_lo[:].rearrange("p k c -> p (k c)"), bank[0][:], xgT_hi[:].rearrange("p k c -> p (k c)"),
                                  ALU.subtract).then_inc(t_xlo, 1)

            def tile_product(i):
                dve.wait_ge(t_silu, i + 1)
                dve.wait_ge(t_tlo, room(t_tlo, i))
                dve.scalar_tensor_tensor(th[:, 0:HID], bank[2][:, 0:HID], 1.0 / WS, tg[:], ALU.mult, ALU.mult).then_inc(t_h, 1)

            def tile_part_lo(i):
                dve.wait_ge(t_thi, i + 1)
                dve.tensor_tensor(th_parts[:, 1, :], th[:], th_parts[:, 0, :], ALU.subtract).then_inc(t_tlo, 1)

            def tile_h_lo(i):
                dve.wait_ge(t_hhi, i + 1)
                dve.tensor_tensor(thT_lo[:].rearrange("p k c -> p (k c)"), bank[3][:, 0:3 * P],
                                  thT_hi[:].rearrange("p k c -> p (k c)"), ALU.subtract).then_inc(t_hlo, 1)

            dve.wait_ge(filled, 4)
            tile_x_lo(0)
            tile_product(0)
            tile_x_lo(1)
            tile_part_lo(0)
            tile_h_lo(0)
            with dve.Fori(1, SLOTS - 1) as i:
                tile_product(i)
                tile_x_lo(i + 1)
                tile_part_lo(i)
                tile_h_lo(i)
            tile_product(SLOTS - 1)
            tile_part_lo(SLOTS - 1)
            tile_h_lo(SLOTS - 1)

            for n in range(TOP_K * TILES):
                t, c = n // TOP_K, n % TOP_K
                dve.wait_ge(y_gathered[n % YR], 16 * (n // YR) + 16)
                if c:
                    dve.wait_ge(y_added, n)
                dve.scalar_tensor_tensor(x_res[:, t, :], yg[:, n % YR, :], slot_f32[:, TOP_K + c, t:t + 1], x_res[:, t, :],
                                         ALU.mult, ALU.add).then_inc(y_added, 1)


INPUTS = ["x", "ctx_2048", "mask_BxS2_bk0", "L0_ffn_gate_w", "L0_ffn_up_w", "L0_ffn_down_w", "L0_ffn_gate_scale",
          "L0_ffn_up_scale", "L0_ffn_down_scale", "L1_xattn_Wh", "L1_xattn_wg_w", "L1_xattn_wo_w",
          "L1_xattn_gn_gamma", "L1_xattn_gn_beta", "L1_ffn_gate_w", "L1_ffn_w1", "L1_ffn_w2", "L1_ffn_sw1",
          "L1_ffn_sw2", "L1_ffn_sw3"]


def decay_table(heads, seq, head_dim):
    import numpy as np
    gam = (1.0 - 2.0 ** (-5.0 - np.arange(heads, dtype=np.float32))).astype(np.float32)
    idx = np.arange(seq, dtype=np.float32)
    expo = idx[None, :] - idx[:, None]
    d = np.where(expo[None] <= 0, gam[:, None, None].astype(np.float64) ** np.minimum(expo, 0)[None], 0.0)
    d = d / np.sqrt(d.sum(axis=-1))[:, None, :] / np.sqrt(float(head_dim))
    return np.ascontiguousarray(d.transpose(2, 0, 1).astype(np.float32))


def kernel(**inputs):
    import numpy as np
    import concourse.bacc as bacc
    from concourse import mybir as mb
    from concourse.bass_utils import run_bass_kernel_spmd

    nc = bacc.Bacc("TRN2", target_bir_lowering=False, num_devices=1)
    arrays, args = {}, []
    for name in INPUTS:
        a = np.ascontiguousarray(inputs[name])
        arrays["in_" + name] = a
        args.append(nc.dram_tensor("in_" + name, a.shape, mb.dt.from_np(a.dtype), kind="ExternalInput").ap())
    heads, head_dim = inputs["L1_xattn_Wh"].shape[:2]
    decay = decay_table(heads, inputs["x"].shape[1], head_dim)
    arrays["in_decay"] = decay
    args.append(nc.dram_tensor("in_decay", decay.shape, mb.dt.float32, kind="ExternalInput").ap())
    out = nc.dram_tensor("out_0", inputs["x"].shape, mb.dt.float32, kind="ExternalOutput").ap()
    build_decoder_pair(nc, *args, out)
    r = run_bass_kernel_spmd(nc, [arrays], core_ids=[0])
    return r.results[0]["out_0"]
```
